# Optimizing a Trainium2 kernel written in Bass

```python
import numpy as np
import jax
import jax.numpy as jnp

def _softmax(x, axis=-1):
    return jax.nn.softmax(x, axis=axis)

def _gelu(x):
    return jax.nn.gelu(x, approximate=True)

def _silu(x):
    return jax.nn.silu(x)

def _sigmoid(x):
    return jax.nn.sigmoid(x)

def _layernorm(x, axis=-1, eps=1e-05):
    m = jnp.mean(x, axis=axis, keepdims=True)
    v = jnp.var(x, axis=axis, keepdims=True)
    return (x - m) / jnp.sqrt(v + eps)

def _scatter_add(tgt, idx, src, axis=0):
    return tgt.at[idx].add(src)

def _segment_sum(src, seg, n):
    return jax.ops.segment_sum(src, seg, n)
kernel_name = 'mk_perceiver_d2_seqx_r4_aca7be'

def setup_inputs(seed: int=0):
    np.random.seed(seed)
    _w = jnp.asarray

    def _rec_inputs():
        import jax
        import jax.numpy as jnp
        _rk = jax.random.key(seed)
        x = -0.0003929 + 0.9999 * jax.random.normal(jax.random.fold_in(_rk, 1), (4, 256, 256), jnp.float32)
        _lenS = 256 - jax.random.randint(jax.random.fold_in(_rk, 7), (4,), 0, max(1, 256 // 4) + 1, jnp.int32)
        _lenS2 = 4096 - jax.random.randint(jax.random.fold_in(_rk, 8), (4,), 0, max(1, 4096 // 4) + 1, jnp.int32)
        _ctx_512P = jax.random.normal(jax.random.fold_in(_rk, 11), (4, 16, 128), jnp.float32)
        _ctx_512c = jax.random.dirichlet(jax.random.fold_in(_rk, 511), 0.3 * jnp.ones((16,), jnp.float32), (4, 4096))
        _ctx_512t = jnp.einsum('bsk,bkd->bsd', _ctx_512c, _ctx_512P)
        _ctx_512t = _ctx_512t * jax.lax.rsqrt(jnp.mean(jnp.square(_ctx_512t)) + 1e-12) * 0.953939
        ctx_512 = -1.39393e-06 + 0.999914 * (_ctx_512t + 0.3 * jax.random.normal(jax.random.fold_in(_rk, 611), (4, 4096, 128), jnp.float32))
        return (x, ctx_512)
    x, ctx_512 = _rec_inputs()

    def _L0_xattn_setup():
        import jax, jax.numpy as jnp
        import numpy as np
        HEADS = 16
        D_MODEL = 256
        IMG_MODEL = 128
        D_K = D_MODEL // HEADS
        key = jax.random.key(seed)
        ks = jax.random.split(key, 12)
        B, LQ, LKV = (8, 512, 256)
        s_dm = 1.0 / np.sqrt(D_MODEL)
        s_im = 1.0 / np.sqrt(IMG_MODEL)
        return {'q': jax.random.normal(ks[0], (B, LQ, D_MODEL), jnp.float32), 'k': jax.random.normal(ks[1], (B, LKV, IMG_MODEL), jnp.float32), 'v': jax.random.normal(ks[2], (B, LKV, IMG_MODEL), jnp.float32), 'Wq': jax.random.normal(ks[3], (D_MODEL, D_MODEL), jnp.float32) * s_dm, 'bq': jnp.zeros((D_MODEL,), jnp.float32), 'Wk': jax.random.normal(ks[4], (IMG_MODEL, D_MODEL), jnp.float32) * s_im, 'bk': jnp.zeros((D_MODEL,), jnp.float32), 'Wv': jax.random.normal(ks[5], (IMG_MODEL, D_MODEL), jnp.float32) * s_im, 'bv': jnp.zeros((D_MODEL,), jnp.float32), 'Wo': jax.random.normal(ks[6], (D_MODEL, D_MODEL), jnp.float32) * s_dm, 'bo': jnp.zeros((D_MODEL,), jnp.float32)}
    _L0_xattn_all = _L0_xattn_setup()
    _L0_xattn_in = {k: v for k, v in _L0_xattn_all.items() if k in ('Wq', 'bq', 'Wk', 'bk', 'Wv', 'bv', 'Wo', 'bo')}
    del _L0_xattn_all

    def _L0_attn_setup():
        import jax, jax.numpy as jnp
        import numpy as np
        DIM = 256
        HEADS = 16
        DHEAD = DIM // HEADS
        key = jax.random.key(seed)
        k1, k2, k3, k4 = jax.random.split(key, 4)
        B, N = (4, 1024)
        x = jax.random.normal(k1, (B, N, DIM), dtype=jnp.float32)
        s = 1.0 / np.sqrt(DIM)
        W_qkv = jax.random.uniform(k2, (DIM, 3 * DIM), jnp.float32, -s, s)
        W_out = jax.random.uniform(k3, (DIM, DIM), jnp.float32, -s, s)
        b_out = jax.random.uniform(k4, (DIM,), jnp.float32, -s, s)
        return {'x': x, 'W_qkv': W_qkv, 'W_out': W_out, 'b_out': b_out}
    _L0_attn_all = _L0_attn_setup()
    _L0_attn_in = {k: v for k, v in _L0_attn_all.items() if k in ('W_qkv', 'W_out', 'b_out')}
    del _L0_attn_all

    def _L0_ffn_setup():
        import jax, jax.numpy as jnp
        import numpy as np
        from functools import partial
        HEADS = 16
        EPS = 1e-12

        def _l2_normalize(z):
            n = jnp.linalg.norm(z, axis=-1, keepdims=True)
            return z / jnp.maximum(n, EPS)
        key = jax.random.key(seed)
        kx, kq, kk, kv, ko, kf = jax.random.split(key, 6)
        B, S, D, L = (2, 512, 256, 256)
        scale = 0.02
        return {'x': jax.random.normal(kx, (B, S, D), dtype=jnp.float32), 'Wq': jax.random.normal(kq, (D, L), dtype=jnp.float32) * scale, 'Wk': jax.random.normal(kk, (D, L), dtype=jnp.float32) * scale, 'Wv': jax.random.normal(kv, (D, L), dtype=jnp.float32) * scale, 'Wo': jax.random.normal(ko, (L, D), dtype=jnp.float32) * scale, 'Wff': jax.random.normal(kf, (D, D), dtype=jnp.float32) * scale}
    _L0_ffn_all = _L0_ffn_setup()
    _L0_ffn_in = {k: v for k, v in _L0_ffn_all.items() if k in ('Wq', 'Wk', 'Wv', 'Wo', 'Wff')}
    del _L0_ffn_all

    def _L1_xattn_setup():
        import jax, jax.numpy as jnp
        import numpy as np
        B, LQ, LK = (8, 512, 512)
        QD, KD, VD = (256, 128, 128)
        key = jax.random.key(seed)
        ks = jax.random.split(key, 9)
        s = 0.02
        return {'query': jax.random.normal(ks[0], (B, LQ, QD), jnp.float32), 'key': jax.random.normal(ks[1], (B, LK, KD), jnp.float32), 'value': jax.random.normal(ks[2], (B, LK, VD), jnp.float32), 'Wq': jax.random.normal(ks[3], (QD, QD), jnp.float32) * s, 'bq': jnp.zeros((QD,), jnp.float32), 'Wk': jax.random.normal(ks[4], (KD, QD), jnp.float32) * s, 'bk': jnp.zeros((QD,), jnp.float32), 'Wv': jax.random.normal(ks[5], (VD, QD), jnp.float32) * s, 'bv': jnp.zeros((QD,), jnp.float32)}
    _L1_xattn_all = _L1_xattn_setup()
    _L1_xattn_in = {k: v for k, v in _L1_xattn_all.items() if k in ('Wq', 'bq', 'Wk', 'bk', 'Wv', 'bv')}
    del _L1_xattn_all

    def _L1_attn_setup():
        import jax, jax.numpy as jnp
        import numpy as np
        DIM = 256
        SEQ = 1024
        BATCH = 4
        ROPE_BASE = 10000.0

        def rotate_half(x):
            x_even = x[..., 0::2]
            x_odd = x[..., 1::2]
            return jnp.stack((-x_odd, x_even), axis=-1).reshape(x.shape)

        def rope_tables(seq_len, dim, base=ROPE_BASE, dtype=jnp.float32):
            pos = jnp.arange(seq_len, dtype=jnp.float32)[:, None]
            inv_freq = 1.0 / base ** (jnp.arange(0, dim, 2, dtype=jnp.float32) / dim)
            freqs = pos * inv_freq
            cos = jnp.repeat(jnp.cos(freqs), 2, axis=-1).astype(dtype)
            sin = jnp.repeat(jnp.sin(freqs), 2, axis=-1).astype(dtype)
            return (cos, sin)
        key = jax.random.key(seed)
        kx, kq, kk, kv = jax.random.split(key, 4)
        s = 1.0 / np.sqrt(DIM)
        return {'x': jax.random.normal(kx, (BATCH, SEQ, DIM), dtype=jnp.float32), 'wq': jax.random.normal(kq, (DIM, DIM), dtype=jnp.float32) * s, 'wk': jax.random.normal(kk, (DIM, DIM), dtype=jnp.float32) * s, 'wv': jax.random.normal(kv, (DIM, DIM), dtype=jnp.float32) * s}
    _L1_attn_all = _L1_attn_setup()
    _L1_attn_in = {k: v for k, v in _L1_attn_all.items() if k in ('wq', 'wk', 'wv')}
    del _L1_attn_all

    def _L1_ffn_setup():
        import jax, jax.numpy as jnp
        import numpy as np
        D_MODEL = 256
        N_HEADS = 16
        N_EXPERTS = 8
        TOP_K = 2
        EXPERT_HIDDEN = D_MODEL * 4 // N_EXPERTS

        def layer_norm(x, g, b, eps=1e-05):
            mu = jnp.mean(x, axis=-1, keepdims=True)
            var = jnp.var(x, axis=-1, keepdims=True)
            return (x - mu) * jax.lax.rsqrt(var + eps) * g + b
        key = jax.random.key(seed)
        ks = jax.random.split(key, 12)
        s = 1.0 / np.sqrt(D_MODEL)
        return {'x': jax.random.normal(ks[0], (2, 512, D_MODEL), dtype=jnp.float32), 'Wq': jax.random.normal(ks[1], (D_MODEL, D_MODEL), dtype=jnp.float32) * s, 'Wk': jax.random.normal(ks[2], (D_MODEL, D_MODEL), dtype=jnp.float32) * s, 'Wv': jax.random.normal(ks[3], (D_MODEL, D_MODEL), dtype=jnp.float32) * s, 'Wo': jax.random.normal(ks[4], (D_MODEL, D_MODEL), dtype=jnp.float32) * s, 'g1': jnp.ones((D_MODEL,), jnp.float32), 'b1': jnp.zeros((D_MODEL,), jnp.float32), 'g2': jnp.ones((D_MODEL,), jnp.float32), 'b2': jnp.zeros((D_MODEL,), jnp.float32), 'Wg': jax.random.normal(ks[5], (D_MODEL, N_EXPERTS), dtype=jnp.float32) * s, 'W1': jax.random.normal(ks[6], (N_EXPERTS, D_MODEL, EXPERT_HIDDEN), dtype=jnp.float32) * s, 'W2': jax.random.normal(ks[7], (N_EXPERTS, EXPERT_HIDDEN, D_MODEL), dtype=jnp.float32) * (1.0 / np.sqrt(EXPERT_HIDDEN))}
    _L1_ffn_all = _L1_ffn_setup()
    _L1_ffn_in = {k: v for k, v in _L1_ffn_all.items() if k in ('Wq', 'Wk', 'Wv', 'Wo', 'g1', 'b1', 'g2', 'b2', 'Wg', 'W1', 'W2')}
    del _L1_ffn_all
    return {'x': x, 'ctx_512': ctx_512, 'L0_xattn_Wq': _L0_xattn_in['Wq'], 'L0_xattn_bq': _L0_xattn_in['bq'], 'L0_xattn_Wk': _L0_xattn_in['Wk'], 'L0_xattn_bk': _L0_xattn_in['bk'], 'L0_xattn_Wv': _L0_xattn_in['Wv'], 'L0_xattn_bv': _L0_xattn_in['bv'], 'L0_xattn_Wo': _L0_xattn_in['Wo'], 'L0_xattn_bo': _L0_xattn_in['bo'], 'L0_attn_W_qkv': _L0_attn_in['W_qkv'], 'L0_attn_W_out': _L0_attn_in['W_out'], 'L0_attn_b_out': _L0_attn_in['b_out'], 'L0_ffn_Wq': _L0_ffn_in['Wq'], 'L0_ffn_Wk': _L0_ffn_in['Wk'], 'L0_ffn_Wv': _L0_ffn_in['Wv'], 'L0_ffn_Wo': _L0_ffn_in['Wo'], 'L0_ffn_Wff': _L0_ffn_in['Wff'], 'L1_xattn_Wq': _L1_xattn_in['Wq'], 'L1_xattn_bq': _L1_xattn_in['bq'], 'L1_xattn_Wk': _L1_xattn_in['Wk'], 'L1_xattn_bk': _L1_xattn_in['bk'], 'L1_xattn_Wv': _L1_xattn_in['Wv'], 'L1_xattn_bv': _L1_xattn_in['bv'], 'L1_attn_wq': _L1_attn_in['wq'], 'L1_attn_wk': _L1_attn_in['wk'], 'L1_attn_wv': _L1_attn_in['wv'], 'L1_ffn_Wq': _L1_ffn_in['Wq'], 'L1_ffn_Wk': _L1_ffn_in['Wk'], 'L1_ffn_Wv': _L1_ffn_in['Wv'], 'L1_ffn_Wo': _L1_ffn_in['Wo'], 'L1_ffn_g1': _L1_ffn_in['g1'], 'L1_ffn_b1': _L1_ffn_in['b1'], 'L1_ffn_g2': _L1_ffn_in['g2'], 'L1_ffn_b2': _L1_ffn_in['b2'], 'L1_ffn_Wg': _L1_ffn_in['Wg'], 'L1_ffn_W1': _L1_ffn_in['W1'], 'L1_ffn_W2': _L1_ffn_in['W2']}

def reference(x, ctx_512, L0_xattn_Wq, L0_xattn_bq, L0_xattn_Wk, L0_xattn_bk, L0_xattn_Wv, L0_xattn_bv, L0_xattn_Wo, L0_xattn_bo, L0_attn_W_qkv, L0_attn_W_out, L0_attn_b_out, L0_ffn_Wq, L0_ffn_Wk, L0_ffn_Wv, L0_ffn_Wo, L0_ffn_Wff, L1_xattn_Wq, L1_xattn_bq, L1_xattn_Wk, L1_xattn_bk, L1_xattn_Wv, L1_xattn_bv, L1_attn_wq, L1_attn_wk, L1_attn_wv, L1_ffn_Wq, L1_ffn_Wk, L1_ffn_Wv, L1_ffn_Wo, L1_ffn_g1, L1_ffn_b1, L1_ffn_g2, L1_ffn_b2, L1_ffn_Wg, L1_ffn_W1, L1_ffn_W2):
    import jax
    import jax.numpy as jnp

    def _L0_xattn_ref(q, k, v, Wq, bq, Wk, bk, Wv, bv, Wo, bo):
        import jax, jax.numpy as jnp
        import numpy as np
        HEADS = 16
        D_MODEL = 256
        IMG_MODEL = 128
        D_K = D_MODEL // HEADS
        B, LQ, _ = q.shape
        LKV = k.shape[1]
        qh = (q @ Wq + bq).reshape(B, LQ, HEADS, D_K).transpose(0, 2, 1, 3)
        kh = (k @ Wk + bk).reshape(B, LKV, HEADS, D_K).transpose(0, 2, 1, 3)
        vh = (v @ Wv + bv).reshape(B, LKV, HEADS, D_K).transpose(0, 2, 1, 3)
        scale = 1.0 / np.sqrt(D_K)
        scores = jnp.einsum('bhqd,bhkd->bhqk', qh, kh) * scale
        attn = jax.nn.softmax(scores, axis=-1)
        out = jnp.einsum('bhqk,bhkd->bhqd', attn, vh)
        concat = out.transpose(0, 2, 1, 3).reshape(B, LQ, D_MODEL)
        return concat @ Wo + bo

    def _L0_attn_ref(x, W_qkv, W_out, b_out):
        import jax, jax.numpy as jnp
        import numpy as np
        DIM = 256
        HEADS = 16
        DHEAD = DIM // HEADS
        B, N, C = x.shape
        qkv = x @ W_qkv
        q, k, v = jnp.split(qkv, 3, axis=-1)
        resh = lambda t: t.reshape(B, N, HEADS, DHEAD).transpose(0, 2, 1, 3)
        q, k, v = (resh(q), resh(k), resh(v))
        q = jax.nn.elu(q) + 1.0
        k = jax.nn.elu(k) + 1.0
        kv = jnp.einsum('bhnd,bhne->bhde', k, v)
        z = k.sum(axis=2)
        numerator = jnp.einsum('bhnd,bhde->bhne', q, kv)
        denominator = jnp.einsum('bhnd,bhd->bhn', q, z)[..., None] + 1e-06
        out = numerator / denominator
        out = out.transpose(0, 2, 1, 3).reshape(B, N, C)
        return out @ W_out + b_out

    def _L0_ffn_ref(x, Wq, Wk, Wv, Wo, Wff):
        import jax, jax.numpy as jnp
        import numpy as np
        from functools import partial
        HEADS = 16
        EPS = 1e-12

        def _l2_normalize(z):
            n = jnp.linalg.norm(z, axis=-1, keepdims=True)
            return z / jnp.maximum(n, EPS)
        B, S, D = x.shape
        H = HEADS
        L = Wq.shape[1]
        dh = L // H

        def split_heads(t):
            return t.reshape(B, S, H, dh).transpose(0, 2, 1, 3).reshape(B * H, S, dh)
        q = split_heads(x @ Wq)
        k = split_heads(x @ Wk)
        v = split_heads(x @ Wv)
        scores = jnp.einsum('bqd,bkd->bkq', q, k) / jnp.sqrt(jnp.asarray(D, x.dtype))
        attn = jax.nn.softmax(scores, axis=-1)
        out = jnp.einsum('bkq,bkv->bqv', attn, v)
        z = out.reshape(B, H, S, dh).transpose(0, 2, 1, 3).reshape(B, S, L)
        z = z @ Wo
        z = _l2_normalize(z)
        z = z @ Wff
        z = _l2_normalize(z)
        z = jax.nn.gelu(z, approximate=False)
        return z

    def _L1_xattn_ref(query, key, value, Wq, bq, Wk, bk, Wv, bv):
        import jax, jax.numpy as jnp
        import numpy as np
        B, LQ, LK = (8, 512, 512)
        QD, KD, VD = (256, 128, 128)
        q = jnp.einsum('bld,de->ble', query, Wq) + bq
        k = jnp.einsum('bld,de->ble', key, Wk) + bk
        v = jnp.einsum('bld,de->ble', value, Wv) + bv
        scores = jnp.einsum('bqe,bke->bqk', q, k)
        attn = jax.nn.softmax(scores, axis=-1)
        out = jnp.einsum('bqk,bke->bqe', attn, v)
        return out

    def _L1_attn_ref(x, wq, wk, wv):
        import jax, jax.numpy as jnp
        import numpy as np
        DIM = 256
        SEQ = 1024
        BATCH = 4
        ROPE_BASE = 10000.0

        def rotate_half(x):
            x_even = x[..., 0::2]
            x_odd = x[..., 1::2]
            return jnp.stack((-x_odd, x_even), axis=-1).reshape(x.shape)

        def rope_tables(seq_len, dim, base=ROPE_BASE, dtype=jnp.float32):
            pos = jnp.arange(seq_len, dtype=jnp.float32)[:, None]
            inv_freq = 1.0 / base ** (jnp.arange(0, dim, 2, dtype=jnp.float32) / dim)
            freqs = pos * inv_freq
            cos = jnp.repeat(jnp.cos(freqs), 2, axis=-1).astype(dtype)
            sin = jnp.repeat(jnp.sin(freqs), 2, axis=-1).astype(dtype)
            return (cos, sin)
        q = jnp.einsum('bsd,ed->bse', x, wq)
        k = jnp.einsum('bsd,ed->bse', x, wk)
        v = jnp.einsum('bsd,ed->bse', x, wv)
        seq_len, dim = (q.shape[-2], q.shape[-1])
        cos, sin = rope_tables(seq_len, dim, dtype=q.dtype)
        q = q * cos + rotate_half(q) * sin
        k = k * cos + rotate_half(k) * sin
        scale = 1.0 / jnp.sqrt(jnp.asarray(dim, dtype=q.dtype))
        scores = jnp.einsum('bqd,bkd->bqk', q, k) * scale
        mask = jnp.triu(jnp.ones((seq_len, seq_len), dtype=bool), k=1)
        scores = jnp.where(mask, jnp.asarray(-jnp.inf, dtype=scores.dtype), scores)
        weights = jax.nn.softmax(scores, axis=-1)
        return jnp.einsum('bqk,bkd->bqd', weights, v)

    def _L1_ffn_ref(x, Wq, Wk, Wv, Wo, g1, b1, g2, b2, Wg, W1, W2):
        import jax, jax.numpy as jnp
        import numpy as np
        D_MODEL = 256
        N_HEADS = 16
        N_EXPERTS = 8
        TOP_K = 2
        EXPERT_HIDDEN = D_MODEL * 4 // N_EXPERTS

        def layer_norm(x, g, b, eps=1e-05):
            mu = jnp.mean(x, axis=-1, keepdims=True)
            var = jnp.var(x, axis=-1, keepdims=True)
            return (x - mu) * jax.lax.rsqrt(var + eps) * g + b
        B, S, D = x.shape
        H, dk = (N_HEADS, D // N_HEADS)
        xn = layer_norm(x, g1, b1)
        q = (xn @ Wq).reshape(B, S, H, dk).transpose(0, 2, 1, 3)
        k = (xn @ Wk).reshape(B, S, H, dk).transpose(0, 2, 1, 3)
        v = (xn @ Wv).reshape(B, S, H, dk).transpose(0, 2, 1, 3)
        scores = jnp.einsum('bhqd,bhkd->bhqk', q, k) / np.sqrt(dk)
        attn = jax.nn.softmax(scores, axis=-1)
        o = jnp.einsum('bhqk,bhkd->bhqd', attn, v)
        o = o.transpose(0, 2, 1, 3).reshape(B, S, D) @ Wo
        x = x + o
        xn2 = layer_norm(x, g2, b2)
        xf = xn2.reshape(B * S, D)
        gate = xf @ Wg
        topv, topi = jax.lax.top_k(gate, TOP_K)
        probs = jax.nn.softmax(topv, axis=-1)
        cw = jnp.sum(jax.nn.one_hot(topi, N_EXPERTS, dtype=xf.dtype) * probs[..., None], axis=1)
        h = jax.nn.relu(jnp.einsum('td,edh->teh', xf, W1))
        y = jnp.einsum('teh,ehd->ted', h, W2)
        moe = jnp.einsum('ted,te->td', y, cw).reshape(B, S, D)
        return x + moe
    x = x + _L0_xattn_ref(_layernorm(x, axis=-1), ctx_512, ctx_512, L0_xattn_Wq, L0_xattn_bq, L0_xattn_Wk, L0_xattn_bk, L0_xattn_Wv, L0_xattn_bv, L0_xattn_Wo, L0_xattn_bo)
    x = x + _L0_attn_ref(_layernorm(x, axis=-1), L0_attn_W_qkv, L0_attn_W_out, L0_attn_b_out)
    x = x + _L0_ffn_ref(_layernorm(x, axis=-1), L0_ffn_Wq, L0_ffn_Wk, L0_ffn_Wv, L0_ffn_Wo, L0_ffn_Wff)
    x = x + _L1_xattn_ref(_layernorm(x, axis=-1), ctx_512, ctx_512, L1_xattn_Wq, L1_xattn_bq, L1_xattn_Wk, L1_xattn_bk, L1_xattn_Wv, L1_xattn_bv)
    x = x + _L1_attn_ref(_layernorm(x, axis=-1), L1_attn_wq, L1_attn_wk, L1_attn_wv)
    x = x + _L1_ffn_ref(_layernorm(x, axis=-1), L1_ffn_Wq, L1_ffn_Wk, L1_ffn_Wv, L1_ffn_Wo, L1_ffn_g1, L1_ffn_b1, L1_ffn_g2, L1_ffn_b2, L1_ffn_Wg, L1_ffn_W1, L1_ffn_W2)
    return x

_drawn_inputs = setup_inputs


def setup_inputs(seed=0):
    import zlib

    import numpy as np

    out = dict(_drawn_inputs(seed))
    spreads = {'L0_xattn_bq': (0.0, 0.1),
     'L0_xattn_bk': (0.0, 2.0),
     'L0_xattn_bv': (0.0, 0.1),
     'L0_xattn_bo': (0.0, 0.1),
     'L1_xattn_bq': (0.0, 0.279),
     'L1_xattn_bk': (0.0, 2.0),
     'L1_xattn_bv': (0.0, 0.1),
     'L1_ffn_g1': (1.0, 0.2),
     'L1_ffn_b1': (0.0, 0.1),
     'L1_ffn_g2': (1.0, 0.2),
     'L1_ffn_b2': (0.0, 0.1)}
    factors = {'L0_ffn_Wq': 25.647, 'L0_ffn_Wk': 24.67}
    for name, (base, spread) in spreads.items():
        noise = np.random.default_rng([zlib.crc32(name.encode()), seed]).standard_normal(out[name].shape)
        drawn = base * np.exp(spread * noise) if base else spread * noise
        out[name] = jnp.asarray(drawn.astype(out[name].dtype))
    for name, factor in factors.items():
        out[name] = (out[name] * factor).astype(out[name].dtype)
    return out
```

```python
from contextlib import ExitStack

import numpy as np

import concourse.bass as bass
from concourse import mybir

F32 = mybir.dt.float32
BF16 = mybir.dt.bfloat16
U32 = mybir.dt.uint32
ACT = mybir.ActivationFunctionType
ALU = mybir.AluOpType
AX = mybir.AxisListType

P = 128
B, S, D = 4, 256, 256
LC, C = 4096, 128
H, DH = 16, 16
NT = B * S // P
KD = D // P
QT = S // P
EPS_LN = 1e-5
BANK = 512
NE, HID = 8, 128

CONST_COLS = {}


def constants():
    p = np.arange(P)
    ident = np.eye(P, dtype=np.float32)
    head_block = (p[:, None] // DH == p[None, :] // DH).astype(np.float32)
    head_col = (p[:, None] // DH == np.arange(P // DH)[None, :]).astype(np.float32)
    gather = np.zeros((P, 2 * (DH + 1)), np.float32)
    for quad in range(4):
        for r in range(DH + 1):
            gather[32 * quad + r, (quad % 2) * (DH + 1) + r] = 1.0
    pos = np.arange(S, dtype=np.float32)[:, None]
    inv = (np.float32(1.0) / np.float32(10000.0) ** (np.arange(0, D, 2, dtype=np.float32) / np.float32(D))).astype(np.float32)
    freqs = (pos * inv).astype(np.float32)
    cos = np.repeat(np.cos(freqs), 2, axis=-1)
    sin = np.repeat(np.sin(freqs), 2, axis=-1)
    sin[:, 0::2] *= -1.0
    by_tile = lambda a: a.reshape(QT, P, D).transpose(1, 0, 2).reshape(P, QT * D)
    causal = np.where(p[None, :] > p[:, None], np.float32(-3e38), np.float32(0.0)).astype(np.float32)
    iota = np.broadcast_to(np.arange(NE, dtype=np.float32), (P, NE))
    minus_half, half = np.full((P, NT), -0.5, np.float32), np.full((P, NT), 0.5, np.float32)
    groups = ([("ident", ident), ("gather", gather), ("minus_half", minus_half), ("half", half)],
              [("head_block", head_block), ("head_col", head_col), ("cos", by_tile(cos)), ("sin", by_tile(sin)),
               ("causal", causal), ("iota", iota)])
    for n, parts in enumerate(groups):
        at = 0
        for name, a in parts:
            CONST_COLS[name] = (n, at, at + a.shape[1])
            at += a.shape[1]
    return [np.ascontiguousarray(np.concatenate([a for _, a in parts], axis=1), dtype=np.float32) for parts in groups]


class Step:

    def __init__(self, queue, make, after, dma_sem, stage):
        self.queue, self.make, self.after, self.dma_sem, self.stage = queue, make, after, dma_sem, stage
        self.wanted = dma_sem is not None
        self.value = None


class Program:

    ENGINES = ("tensor", "vector", "scalar", "gpsimd", "sync")

    def __init__(self, nc, ctx):
        self.nc, self.ctx = nc, ctx
        self.queues = {e: [] for e in self.ENGINES}
        self.stage = "start"
        self.fences = {e: [] for e in self.ENGINES}

    def put(self, engine, make, after=(), dma_sem=None):
        steps = [s for s in list(after) + self.fences[engine] if s is not None]
        self.fences[engine] = []
        for s in steps:
            s.wanted = True
        step = Step(engine, make, steps, dma_sem, self.stage)
        self.queues[engine].append(step)
        return step

    def pe(self, make, after=()):
        return self.put("tensor", make, after)

    def dve(self, make, after=()):
        return self.put("vector", make, after)

    def act(self, make, after=()):
        return self.put("scalar", make, after)

    def pool(self, make, after=()):
        queue = self.queues["gpsimd"]
        if queue:
            after = list(after) + [queue[-1]]
        return self.put("gpsimd", make, after)

    def dma(self, out, in_, sem, after=(), engine="sync", **how):
        return self.put(engine, lambda e: e.dma_start(out, in_, **how), after, dma_sem=sem)

    def barrier(self):
        last = [q[-1] for q in self.queues.values() if q]
        for e in self.ENGINES:
            self.fences[e] = [s for s in last if s.queue != e or e != "tensor"]

    def emit(self):
        nc, sems, counts = self.nc, {}, {}
        for engine, queue in self.queues.items():
            for s in queue:
                if s.wanted:
                    name = s.dma_sem or f"{engine}_{s.stage}"
                    if name not in sems:
                        sems[name] = self.ctx.enter_context(nc.semaphore(name))
                        counts[name] = 0
                    counts[name] += 16 if s.dma_sem else 1
                    s.value = (name, counts[name])
        self.counts = counts
        block = self.ctx.enter_context(nc.Block())

        def run(queue):
            def body(engine):
                reached = {}
                for s in queue:
                    need = {}
                    for a in s.after:
                        name, value = a.value
                        need[name] = max(need.get(name, 0), value)
                    for name, value in need.items():
                        if reached.get(name, 0) < value:
                            engine.wait_ge(sems[name], value)
                            reached[name] = value
                    instruction = s.make(engine)
                    if s.wanted:
                        instruction.then_inc(sems[s.value[0]], 16 if s.dma_sem else 1)
                if queue is self.queues["sync"]:
                    engine.wait_ge(sems["store"], counts["store"])
            return body

        block.tensor(run(self.queues["tensor"]))
        block.vector(run(self.queues["vector"]))
        block.scalar(run(self.queues["scalar"]))
        block.gpsimd(run(self.queues["gpsimd"]))
        block.sync(run(self.queues["sync"]))


def build(nc, io, out, stages=6):
    ctx = ExitStack()
    with ctx:
        pr = Program(nc, ctx)
        pe, dve, act, pool, dma = pr.pe, pr.dve, pr.act, pr.pool, pr.dma
        psum = ctx.enter_context(nc.psum_tensor("psum", [P, 8 * BANK], F32))
        bank_users = [[] for _ in range(8)]
        bank_turn = [0]
        held = set()

        def bank(k):
            return psum[:, k * BANK:(k + 1) * BANK]

        def next_bank():
            k = bank_turn[0] % 8
            bank_turn[0] += 1
            while k in held:
                k = bank_turn[0] % 8
                bank_turn[0] += 1
            return k, bank(k), bank_users[k]

        def sb(scope, name, shape, dt=F32):
            return scope.enter_context(nc.sbuf_tensor(name, shape, dt))

        const_tiles = [sb(ctx, "const", [P, io["const"].shape[1]]), None]
        const_in = dma(const_tiles[0][:, :], io["const"], "in_const")

        def constant(name):
            n, a, b = CONST_COLS[name]
            return const_tiles[n][:, a:b]

        ident = constant("ident")
        small = sb(ctx, "small", [P, 512])
        stat6 = small[:, 0:NT * 6].rearrange("p (t s) -> p t s", t=NT)
        meanvar = small[:, 48:48 + NT * 2].rearrange("p (t s) -> p t s", t=NT)
        rstd = small[:, 64:64 + NT]

        evacs = [0]

        def evacuate(dst, src, after):
            evacs[0] += 1
            if evacs[0] % 2:
                return act(lambda e: e.activation(dst, src, ACT.Copy), after)
            return dve(lambda e: e.tensor_copy(dst, src), after)

        def layer_norm(x, xn, after):
            aggregated = None
            for t in range(NT):
                stats = dve(lambda e, t=t: e.bn_stats(stat6[:, t, :], x[:, t, :]), after)
                aggregated = dve(lambda e, t=t: e.bn_aggr(meanvar[:, t, :], stat6[:, t, :]), [stats])
            guarded = dve(lambda e: e.tensor_scalar(rstd, meanvar[:, :, 1], EPS_LN, None, ALU.add), [aggregated])
            inverse = pool(lambda e: e.tensor_tensor(rstd, rstd, constant("minus_half"), ALU.pow), [guarded, const_in])
            steps = [dve(lambda e, t=t: e.tensor_scalar(xn[:, t, :], x[:, t, :], meanvar[:, t, 0:1],
                                                        rstd[:, t:t + 1], ALU.subtract, ALU.mult), [inverse])
                     for t in range(NT)]
            pr.last_norm = steps[-1]
            return steps

        def transpose_tokens(xn, xnT, ready):
            done = [[] for _ in range(NT)]
            for t0 in range(0, NT, 4):
                for k in range(KD):
                    n, ps, free = next_bank()
                    for i in range(4):
                        last = pe(lambda e, t=t0 + i, i=i, k=k, ps=ps: e.transpose(
                            ps[:, i * P:(i + 1) * P], xn[:, t, k * P:(k + 1) * P], ident),
                            free + [ready[t0 + i], const_in])
                    copied = evacuate(xnT[:, k, t0 * P:(t0 + 4) * P], ps, [last])
                    bank_users[n] = [copied]
                    for i in range(4):
                        done[t0 + i].append(copied)
            return done

        def project_tokens(actT, ready, w, w_ready, use, cols=slice(0, D), blocks=KD):
            width = cols.stop - cols.start
            for t in range(NT):
                n, ps, free = next_bank()
                for k in range(blocks):
                    last = pe(lambda e, t=t, k=k, ps=ps: e.matmul(
                        ps[:, 0:width], actT[:, k, t * P:(t + 1) * P], w[:, k, cols],
                        start=(k == 0), stop=(k == blocks - 1)), free + list(ready[t]) + [w_ready])
                bank_users[n] = use(t, ps[:, 0:width], last)

        def project_T(actT, ready, w, w_ready, use, col0=0):
            for half in range(2):
                for m in range(KD):
                    n, ps, free = next_bank()
                    for k in range(KD):
                        last = pe(lambda e, m=m, k=k, half=half, ps=ps: e.matmul(
                            ps, w[:, k, col0 + m * P:col0 + (m + 1) * P], actT[:, k, half * BANK:(half + 1) * BANK],
                            start=(k == 0), stop=(k == KD - 1)),
                            free + [s for t in range(4 * half, 4 * half + 4) for s in ready[t]] + [w_ready])
                    bank_users[n] = use(m, half, ps, last)

        def weight(scope, name, source, blocks, sem=None):
            n = source.shape[1]
            w = sb(scope, name, [P, blocks, n])
            return w, dma(w[:, :, :], source.rearrange("(k p) n -> p k n", p=P), sem or f"in_{name}")

        def bias_rows(scope, name, source):
            row = sb(scope, name, [P, D])
            return row, dma(row[:, :], source.partition_broadcast(P), f"in_{name}")

        def bias_columns(scope, name, source):
            col = sb(scope, name, [P, KD])
            return col, dma(col[:, :], source.rearrange("(m p) -> p m", p=P), f"in_{name}",
                            allow_slow_non_contiguous=True)

        pr.stage = "xattn0"
        wo, wo_in = weight(ctx, "wo", io["L0_xattn_Wo"], KD)
        bv, bv_in = bias_rows(ctx, "bv", io["L0_xattn_bv"])
        bo, bo_in = bias_rows(ctx, "bo", io["L0_xattn_bo"])
        x = sb(ctx, "x", [P, NT, D])
        heads_out = x
        one = ExitStack()
        wk, wk_in = weight(one, "wk", io["L0_xattn_Wk"], 1)
        wv, wv_in = weight(one, "wv", io["L0_xattn_Wv"], 1)
        bk, bk_in = bias_columns(one, "bk", io["L0_xattn_bk"])
        PARTS = 3
        PAIRS = 6
        ROWS = PAIRS * DH
        AUG = ROWS + 2
        GH = 2
        NG = H // GH
        GROUPS = B * NG
        SLOTS = LC // P // 2
        UNIT_GROUPS = P // (GH * DH)
        RING = 3
        keysT = sb(one, "keysT", [P, RING, GH, LC], BF16)
        values = sb(one, "values", [P, LC // P, H, DH + 1])
        q_parts = sb(one, "q_parts", [P, NT, PARTS, D], BF16)
        q_rows = sb(one, "q_rows", [P, QT, H // 2, ROWS], BF16)
        queriesT = sb(one, "queriesT", [P, 4, GH, S], BF16)
        key_parts = sb(one, "key_parts", [P, 2, PARTS, LC], BF16)
        ctxT = sb(one, "ctxT", [P, LC])
        probs = sb(one, "probs", [P, 2, 4 * S])
        ctx_in = sb(one, "ctx_in", [P, 2, 4, C])
        key_f = sb(one, "key_f", [P, 2, BANK])
        key_r = sb(one, "key_r", [P, BANK])
        outT = sb(one, "outT", [P, S])
        ident_b = sb(one, "ident_b", [P, P], BF16)
        peaks = sb(one, "peaks", [P, 2, GH * QT, 8])
        shift = sb(one, "shift", [P, 2, 3, GH * QT])
        shift_b = sb(one, "shift_b", [P, 2, GH * QT, 2], BF16)
        recip = sb(one, "recip", [P, QT, GH])
        early = keysT[:, 2, :, :].rearrange("p h n -> p (h n)").bitcast(F32)
        x_norm = early[:, 0:NT * D].rearrange("p (t d) -> p t d", t=NT)
        x_normT = early[:, NT * D:2 * NT * D].rearrange("p (k n) -> p k n", k=KD)
        x0 = ctxT[:, 0:NT * D].rearrange("p (t d) -> p t d", t=NT)
        wq = probs[:, 0, 0:KD * D].rearrange("p (k n) -> p k n", k=KD)
        bq = probs[:, 0, KD * D:KD * D + D]
        q_work = probs[:, 1, :].rearrange("p (w d) -> p w d", w=4)

        x_tiles = io["x"].rearrange("b (t p) d -> p (b t) d", p=P)
        x_in = dma(x0, x_tiles, "in_x")
        wq_in = dma(wq, io["L0_xattn_Wq"].rearrange("(k p) n -> p k n", p=P), "in_wq")
        bq_in = dma(bq, io["L0_xattn_bq"].partition_broadcast(P), "in_bq")
        ident_b_made = dve(lambda e: e.tensor_copy(ident_b[:, :], ident), [const_in])
        ones_v = pool(lambda e: e.memset(values[:, :, :, DH:DH + 1], 1.0))
        clear_o = dve(lambda e: e.memset(bank(6), 0.0))
        normed = layer_norm(x0, x_norm, [x_in])
        x_free = normed[-1]
        normedT = transpose_tokens(x_norm, x_normT, normed)
        bq4 = dve(lambda e: e.tensor_scalar(bq, bq, DH ** -0.5, None, ALU.mult), [bq_in])
        split_done = [None] * NT
        work_free = [None, None]

        def split_query(t, ps, made):
            q, r = q_work[:, 2 * (t % 2), :], q_work[:, 2 * (t % 2) + 1, :]
            part = lambda n: q_parts[:, t, n, :]
            s0 = dve(lambda e: e.scalar_tensor_tensor(out=q, in0=ps, scalar=DH ** -0.5, in1=bq,
                                                      op0=ALU.mult, op1=ALU.add), [made, bq4, work_free[t % 2]])
            s1 = act(lambda e: e.activation(part(0), q, ACT.Copy), [s0])
            s2 = dve(lambda e: e.tensor_tensor(r, q, part(0), ALU.subtract), [s1])
            s3 = act(lambda e: e.activation(part(1), r, ACT.Copy), [s2])
            s4 = dve(lambda e: e.tensor_tensor(part(2), r, part(1), ALU.subtract), [s3])
            work_free[t % 2] = s4
            split_done[t] = s4
            return [s0]

        project_tokens(x_normT, normedT, wq, wq_in, split_query)
        early_free = [pr.queues["tensor"][-1], split_done[-1]]
        misc_free = [list(bank_users[7])]

        jobs = {}

        def at(slot, job):
            jobs.setdefault(slot, []).append(job)

        ctx_loaded, ctx_turned, ctx_read = {}, {}, {}
        parts_ready, parts_free = {}, {}
        chunk_done = {}
        rows_ready, rows_free, qT_ready, qT_done = {}, {}, {}, {}
        keys_ready, keys_free = {}, {}
        shifts_ready = {}
        values_ready, values_free = {}, {}
        last_key_f = [None, None]
        last_key_r = [None]
        ctx_users = [[x_free]]
        CH = LC // BANK

        def load_ctx(b, c):
            n = b * CH + c
            ctx_loaded[b, c] = dma(ctx_in[:, n % 2, :, :],
                                   io["ctx_512"][b, c * BANK:(c + 1) * BANK, :].rearrange("(t p) c -> p t c", p=P),
                                   f"in_ctx{n % 2}", [ctx_read.get(n - 2)])

        def turn_ctx(b, c):
            n = b * CH + c
            for i in range(4):
                last = pe(lambda e, i=i: e.transpose(bank(7)[:, i * P:(i + 1) * P], ctx_in[:, n % 2, i, :], ident),
                          misc_free[0] + [ctx_loaded[b, c]])
            ctx_read[n] = last
            ctx_turned[b, c] = act(lambda e: e.activation(ctxT[:, c * BANK:(c + 1) * BANK], bank(7), ACT.Copy),
                                   [last] + ctx_users[0])
            misc_free[0] = [ctx_turned[b, c]]

        def fill_keys(u, c):
            b, m = divmod(u, KD)
            made = pe(lambda e: e.matmul(bank(7), wk[:, 0, m * P:(m + 1) * P], ctxT[:, c * BANK:(c + 1) * BANK],
                                         start=True, stop=True), misc_free[0] + [ctx_turned[b, c], wk_in])
            n = (u * CH + c) % 2
            k, r = key_f[:, n, :], key_r[:, :]
            part = lambda i: key_parts[:, u % 2, i, c * BANK:(c + 1) * BANK]
            s0 = act(lambda e: e.activation(k, bank(7), ACT.Identity, bias=bk[:, m:m + 1]), [made, bk_in, last_key_f[n]])
            misc_free[0] = [s0]
            free = parts_free.get(u - 2, [])
            s1 = pool(lambda e: e.tensor_copy(part(0), k), [s0] + free)
            s2 = pool(lambda e: e.tensor_tensor(r, k, part(0), ALU.subtract), [s1, last_key_r[0]])
            s3 = pool(lambda e: e.tensor_copy(part(1), r), [s2])
            s4 = pool(lambda e: e.tensor_tensor(part(2), r, part(1), ALU.subtract), [s3])
            last_key_f[n], last_key_r[0] = s2, s4
            chunk_done[u] = s4
            if m == KD - 1 and c == CH - 1:
                last_k_read[b] = made

        last_k_read = {}

        def lay_query_rows(u):
            b, m = divmod(u, KD)
            at_block = 0
            for part, times in ((0, 3), (1, 2), (2, 1)):
                for t in range(QT):
                    src = q_parts[:, QT * b + t, part, m * P:(m + 1) * P].rearrange("p (h d) -> p h d", d=DH)
                    for i in range(times):
                        dst = q_rows[:, t, :, (at_block + i) * DH:(at_block + i + 1) * DH]
                        last = pool(lambda e, dst=dst, src=src: e.tensor_copy(dst, src),
                                    [split_done[QT * b + t]] + rows_free.get(u - 1, []))
                at_block += times
            rows_ready[u] = last

        def turn_queries(i):
            u, g = divmod(i, UNIT_GROUPS)
            out_b = bank(7).bitcast(BF16)
            for j in range(GH):
                for t in range(QT):
                    k = j * QT + t
                    last = pe(lambda e, k=k, j=j, t=t: e.transpose(
                        out_b[0:ROWS, k * P:(k + 1) * P], q_rows[:, t, g * GH + j, :], ident_b[:, :]),
                        misc_free[0] + [rows_ready[u], ident_b_made])
            rows_free[u] = [last]
            qT_ready[i] = dve(lambda e: e.tensor_copy(
                queriesT[0:ROWS, i % 4, :, :].rearrange("p h n -> p (h n)"), out_b[0:ROWS, 0:GH * S]),
                [last] + qT_done.get(i - 4, []))
            misc_free[0] = [qT_ready[i]]

        def load_keys(i):
            u, g = divmod(i, UNIT_GROUPS)
            ring = i % RING
            for j in range(GH):
                src0 = (g * GH + j) * DH
                for block, part in enumerate((0, 1, 2, 0, 1, 0)):
                    last = dma(keysT[block * DH:(block + 1) * DH, ring, j, :],
                               key_parts[src0:src0 + DH, u % 2, part, :], f"keys{ring}",
                               [chunk_done[u]] + keys_free.get(i - RING, []) + (early_free if ring == 2 else []))
            keys_ready[i] = last
            parts_free[u] = parts_free.get(u, []) + [last]

        def make_values(b, p):
            for e2 in range(2):
                kt = 2 * p + e2
                made = pe(lambda e, kt=kt, e2=e2: e.matmul(bank(7)[:, e2 * D:(e2 + 1) * D],
                                                           ctxT[:, kt * P:(kt + 1) * P], wv[:, 0, :],
                                                           start=True, stop=True),
                          misc_free[0] + [ctx_turned[b, kt * P // BANK], wv_in])
            values_ready[b, p] = act(lambda e: e.activation(
                values[:, 2 * p:2 * p + 2, :, 0:DH],
                bank(7).rearrange("p (k h d) -> p k h d", k=2, h=H), ACT.Copy),
                [made] + values_free.get((b - 1, p), []))
            misc_free[0] = [values_ready[b, p]]
            last_v_read[b] = made

        last_v_read = {}

        max_free = [None, None]
        peak_read = {}

        def max_step(n):
            i, r = divmod(n, GH * QT * CH)
            if i >= GROUPS:
                return
            pair, c = divmod(r, CH)
            j, t = divmod(pair, QT)
            k = 4 + n % 2
            made = pe(lambda e: e.matmul(bank(k), queriesT[0:ROWS, i % 4, j, t * P:(t + 1) * P],
                                         keysT[0:ROWS, i % RING, j, c * BANK:(c + 1) * BANK], start=True, stop=True),
                      [max_free[n % 2], qT_ready[i], keys_ready[i]] + (bank_users[k] if n < 2 else []))
            max_free[n % 2] = dve(lambda e: e.tensor_reduce(peaks[:, i % 2, pair, c:c + 1], bank(k), AX.X, ALU.max),
                                  [made] + peak_read.get(i - 2, []))
            if r == GH * QT * CH - 1:
                negative, high, rest = (shift[:, i % 2, w, :] for w in range(3))
                s0 = dve(lambda e: e.tensor_reduce(negative, peaks[:, i % 2, :, :], AX.X, ALU.max, negate=True),
                         [max_free[n % 2]])
                peak_read[i] = [s0]
                s1 = dve(lambda e: e.tensor_copy(shift_b[:, i % 2, :, 0], negative), [s0, shift_turned.get(i - 2)])
                s2 = dve(lambda e: e.tensor_tensor(shift_b[:, i % 2, :, 1], negative, shift_b[:, i % 2, :, 0],
                                                   ALU.subtract), [s1])
                shifts_ready[i] = s2

        shift_turned = {}

        def turn_shift(i):
            out_b = bank(7).bitcast(BF16)
            for pair in range(GH * QT):
                last = pe(lambda e, pair=pair: e.transpose(out_b[ROWS:AUG, pair * P:(pair + 1) * P],
                                                           shift_b[:, i % 2, pair, :], ident_b[:, :]),
                          misc_free[0] + [shifts_ready[i]])
            shift_turned[i] = last
            qT_ready[i, "shift"] = dve(lambda e: e.tensor_copy(
                queriesT[ROWS:AUG, i % 4, :, :].rearrange("p h n -> p (h n)"), out_b[ROWS:AUG, 0:GH * S]), [last])
            misc_free[0] = [qT_ready[i, "shift"]]

        score_free, probs_free, probs_ready = {}, {}, {}
        outT_ready, outT_read = {}, {}
        rows_of_ones = pool(lambda e: e.memset(keysT[ROWS:AUG, 0:2, :, :], 1.0))
        rows_of_ones2 = pool(lambda e: e.memset(keysT[ROWS:AUG, 2, :, :], 1.0), early_free)
        ones_steps = [rows_of_ones, rows_of_ones, rows_of_ones2]

        def score_step(t):
            i, p = divmod(t, SLOTS)
            base = (t % 2) * 2 * BANK
            for e2 in range(2):
                for j in range(GH):
                    kt = 2 * p + e2
                    last = pe(lambda e, j=j, kt=kt, o=base + (e2 * GH + j) * S: e.matmul(
                        psum[:, o:o + S], keysT[0:AUG, i % RING, j, kt * P:(kt + 1) * P],
                        queriesT[0:AUG, i % 4, j, :], start=True, stop=True),
                        [score_free.get(t - 2), qT_ready[i, "shift"], keys_ready[i], ones_steps[i % RING]]
                        + (bank_users[2 * t] + bank_users[2 * t + 1] if t < 2 else []))
            probs_ready[t] = act(lambda e: e.activation(probs[:, t % 2, :], psum[:, base:base + 2 * BANK], ACT.Exp),
                                 [last, probs_free.get(t - 2)] + ([split_done[-1], split_done[-2]] if t < 2 else []))
            score_free[t] = probs_ready[t]
            if p == SLOTS - 1:
                keys_free[i] = [last]
                qT_done[i] = [last]

        def value_step(t):
            i, p = divmod(t, SLOTS)
            b, g = divmod(i, NG)
            for e2 in range(2):
                for j in range(GH):
                    quad, kt = e2 * GH + j, 2 * p + e2
                    last = pe(lambda e, quad=quad, kt=kt, j=j: e.matmul(
                        bank(6)[32 * quad:32 * quad + DH + 1, 0:S], values[:, kt, g * GH + j, :],
                        probs[:, t % 2, quad * S:(quad + 1) * S], start=(p == 0), stop=(p == SLOTS - 1)),
                        [probs_ready[t], values_ready[b, p], ones_v, outT_ready.get(i - 1), clear_o])
            probs_free[t] = last
            if g == NG - 1:
                values_free[b, p] = [last]
            return last

        def finish_group(i, last):
            outT_ready[i] = act(lambda e: e.activation(outT[:, :], bank(6)[:, 0:S], ACT.Copy),
                                [last, outT_read.get(i - 1)])

        def normalize_group(i):
            b, g = divmod(i, NG)
            W = GH * (DH + 1)
            for t in range(QT):
                last = pe(lambda e, t=t: e.matmul(bank(7)[:, t * 64:t * 64 + W], outT[:, t * P:(t + 1) * P],
                                                  constant("gather"), start=True, stop=True),
                          misc_free[0] + [outT_ready[i], const_in])
            outT_read[i] = last
            both = bank(7)[:, 0:QT * 64].rearrange("p (t w) -> p t w", t=QT)[:, :, 0:W].rearrange(
                "p t (h d) -> p t h d", h=GH)
            s0 = dve(lambda e: e.reciprocal(recip[:, :, :], both[:, :, :, DH]), [last, recip_read[0]])
            for t in range(QT):
                recip_read[0] = dve(lambda e, t=t: e.tensor_tensor(
                    heads_out[:, QT * b + t, g * GH * DH:(g + 1) * GH * DH].rearrange("p (h d) -> p h d", h=GH),
                    both[:, t, :, 0:DH], recip[:, t, :].unsqueeze(2).to_broadcast([P, GH, DH]), ALU.mult), [s0])
            misc_free[0] = [recip_read[0]]
            group_out[i] = recip_read[0]

        recip_read, group_out = [None], {}

        UNIT = UNIT_GROUPS * SLOTS
        for u in range(B * KD):
            b, m = divmod(u, KD)
            for c in range(CH):
                slot = UNIT * u - 100 + 8 * c
                if m == 0:
                    at(slot - 8, lambda b=b, c=c: load_ctx(b, c))

                    def turn(b=b, c=c):
                        if b and c == 0:
                            ctx_users[0] = [last_k_read[b - 1], last_v_read[b - 1]]
                        turn_ctx(b, c)
                    at(slot, turn)
                    at(slot + 2, lambda u=u, c=c: fill_keys(u, c))
                else:
                    at(slot, lambda u=u, c=c: fill_keys(u, c))
            at(UNIT * u - 24, lambda u=u: lay_query_rows(u))
        for i in range(GROUPS):
            at(SLOTS * i - 32, lambda i=i: load_keys(i))
            at(SLOTS * i - 20, lambda i=i: turn_queries(i))
            at(SLOTS * i - 2, lambda i=i: turn_shift(i))
            at(SLOTS * i + SLOTS + 1, lambda i=i: normalize_group(i))
        for b in range(B):
            for p in range(SLOTS):
                at(SLOTS * NG * b - SLOTS + p + 1, lambda b=b, p=p: make_values(b, p))
        LEAD = 18
        total = GROUPS * SLOTS
        for t in range(min(jobs), total + 2 + 1):
            if 0 <= t and t % (SLOTS * NG) == 0:
                pr.stage = f"xattn0_b{t // (SLOTS * NG)}"
            if 0 <= t < total:
                score_step(t)
            if t + LEAD >= 0:
                max_step(2 * (t + LEAD))
            if 1 <= t <= total:
                last = value_step(t - 1)
                if t % SLOTS == 0:
                    finish_group(t // SLOTS - 1, last)
            if t + LEAD >= 0:
                max_step(2 * (t + LEAD) + 1)
            for job in jobs.get(t, []):
                job()

        pr.stage = "xattn0_out"
        for k in range(8):
            bank_users[k] = []
        bank_users[7] = misc_free[0]
        bank_users[6] = [outT_ready[GROUPS - 1]]
        bank_users[4] = bank_users[5] = [max_free[0], max_free[1]]
        for k in range(4):
            bank_users[k] = [probs_ready[total - 1], probs_ready[total - 2]]
        pr.barrier()
        one.close()

        xn = sb(ctx, "xn", [P, NT, D])
        xnT = sb(ctx, "xnT", [P, KD, B * S])
        const_tiles[1] = sb(ctx, "const2", [P, io["const2"].shape[1]])
        x_old = sb(ctx, "x_old", [P, NT, D])
        x_old_in = dma(x_old[:, :, :], x_tiles, "in_x")
        const2_in = dma(const_tiles[1][:, :], io["const2"], "in_const2")
        wl, wl_in = weight(ctx, "w_qkv", io["L0_attn_W_qkv"], KD)
        wlo, wlo_in = weight(ctx, "w_out", io["L0_attn_W_out"], KD)
        blo, blo_in = bias_rows(ctx, "b_out", io["L0_attn_b_out"])

        biased = [dve(lambda e, t=t: e.tensor_tensor(xn[:, t, :], heads_out[:, t, :], bv[:, :], ALU.add),
                      [bv_in, group_out[GROUPS - 1]]) for t in range(NT)]
        outT_done = transpose_tokens(xn, xnT, biased)
        x_bias = [pool(lambda e, t=t: e.tensor_tensor(x_old[:, t, :], x_old[:, t, :], bo[:, :], ALU.add),
                       [x_old_in, bo_in]) for t in range(NT)]
        x_ready = [None] * NT

        def add_to_stream(t, ps, made):
            x_ready[t] = dve(lambda e: e.tensor_tensor(x[:, t, :], ps, x_old[:, t, :], ALU.add), [made, x_bias[t], biased[t]])
            return [x_ready[t]]

        project_tokens(xnT, outT_done, wo, wo_in, add_to_stream)
        def norm_and_turn(ready):
            normed = layer_norm(x, xn, ready)
            return normed, transpose_tokens(xn, xnT, normed)

        def keep_T(dst, done):
            def use(m, half, ps, made):
                done[m, half] = evacuate(dst[:, m, half * BANK:(half + 1) * BANK], ps, [made])
                return [done[m, half]]
            return use

        def keep_tokens(dst, done):
            def use(t, ps, made):
                done[t] = evacuate(dst[:, t, :], ps, [made])
                return [done[t]]
            return use

        def isolate_heads(srcT, heads, b, m, ready, users, heads_ready):
            n = (b * KD + m) % 2
            for h in range(P // DH):
                engine = dve if h % 2 else pool
                step = engine(lambda e, h=h: e.tensor_scalar(heads[:, n, h, :], srcT[:, m, b * S:(b + 1) * S],
                                                             constant("head_col")[:, h:h + 1], None, ALU.mult),
                              [ready[m, b * S // BANK], const2_in] + users.get((n, h), []))
                heads_ready[n, h] = step

        def add_bias_to_stream(bias, bias_in):
            before = list(x_ready)
            return [pool(lambda e, t=t: e.tensor_tensor(x[:, t, :], x[:, t, :], bias[:, :], ALU.add),
                         [before[t], bias_in, pr.last_norm]) for t in range(NT)]

        def accumulate(plus=None):
            def use(t, ps, made):
                x_ready[t] = dve(lambda e: e.tensor_tensor(x[:, t, :], ps, x[:, t, :], ALU.add),
                                 [made, plus[t] if plus else None])
                return [x_ready[t]]
            return use

        def linear_attention():
            pr.stage = "attn0"
            two = ExitStack()
            k_feat = sb(two, "k_feat", [P, NT, D])
            v_aug = sb(two, "v_aug", [P, NT, KD, P + 1])
            q_featT = sb(two, "q_featT", [P, KD, B * S])
            NKV = P + P // DH
            kv = sb(two, "kv", [P, B, KD, NKV])
            lin_out = sb(two, "lin_out", [P, NT, D])
            lin_outT = sb(two, "lin_outT", [P, KD, B * S])
            low_part = sb(two, "low_part", [P, 4, BANK])
            den = sb(two, "den", [P, 2, KD, P // DH])
            _, xT_done = norm_and_turn(x_ready)
            ones_set = pool(lambda e: e.memset(v_aug[:, :, :, P:P + 1], 1.0))
            low_free = [None] * 4
            low_turn = [0]

            def elu_plus_one(dst, ps, made):
                n = low_turn[0] % 4
                low_turn[0] += 1
                low = low_part[:, n, 0:ps.shape[1]]
                s0 = dve(lambda e: e.tensor_scalar(low, ps, 0.0, None, ALU.min), [made, low_free[n]])
                s1 = act(lambda e: e.activation(low, low, ACT.Exp), [s0])
                low_free[n] = dve(lambda e: e.scalar_tensor_tensor(out=dst, in0=ps, scalar=0.0, in1=low,
                                                                   op0=ALU.max, op1=ALU.add), [s1])
                return low_free[n]

            k_done, v_done = {}, {}

            def keep_kv(t, ps, made):
                v_done[t] = act(lambda e: e.activation(v_aug[:, t, :, 0:P],
                                                       ps[:, D:2 * D].rearrange("p (m n) -> p m n", m=KD), ACT.Copy), [made])
                k_done[t] = elu_plus_one(k_feat[:, t, :], ps[:, 0:D], v_done[t])
                return [k_done[t], v_done[t]]

            project_tokens(xnT, xT_done, wl, wl_in, keep_kv, cols=slice(D, 3 * D))
            q_done = {}

            def keep_q(m, half, ps, made):
                q_done[m, half] = elu_plus_one(q_featT[:, m, half * BANK:(half + 1) * BANK], ps, made)
                return [q_done[m, half]]

            project_T(xnT, xT_done, wl, wl_in, keep_q)
            kv_done = {}
            for b in range(B):
                for m in range(KD):
                    n, ps, free = next_bank()
                    for i in range(QT):
                        t = QT * b + i
                        last = pe(lambda e, t=t, m=m, i=i, ps=ps: e.matmul(
                            ps[:, 0:P + 1], k_feat[:, t, m * P:(m + 1) * P], v_aug[:, t, m, :],
                            start=(i == 0), stop=(i == QT - 1)), free + [k_done[t], v_done[t], ones_set])
                    s0 = dve(lambda e, b=b, m=m, ps=ps: e.tensor_tensor(kv[:, b, m, 0:P], ps[:, 0:P],
                                                                        constant("head_block"), ALU.mult), [last, const2_in])
                    s1 = dve(lambda e, b=b, m=m, ps=ps: e.tensor_tensor(
                        kv[:, b, m, P:NKV], ps[:, P:P + 1].to_broadcast([P, P // DH]), constant("head_col"), ALU.mult), [last])
                    bank_users[n] = [s1]
                    kv_done[b, m] = s1
            lin_done = []
            for t in range(NT):
                n, ps, free = next_bank()
                b = t // QT
                for m in range(KD):
                    last = pe(lambda e, t=t, m=m, b=b, ps=ps: e.matmul(
                        ps[:, m * NKV:(m + 1) * NKV], q_featT[:, m, t * P:(t + 1) * P], kv[:, b, m, :],
                        start=True, stop=True), free + [q_done[m, t * P // BANK], kv_done[b, m]])
                both = ps[:, 0:KD * NKV].rearrange("p (m n) -> p m n", m=KD)
                dn = den[:, t % 2, :, :]
                s0 = dve(lambda e, both=both, dn=dn: e.tensor_scalar(dn, both[:, :, P:NKV], 1e-6, None, ALU.add),
                         [last] + lin_done[-2:-1])
                s1 = dve(lambda e, dn=dn: e.reciprocal(dn, dn), [s0])
                for m in range(KD):
                    s2 = dve(lambda e, t=t, m=m, both=both, dn=dn: e.tensor_tensor(
                        lin_out[:, t, m * P:(m + 1) * P].rearrange("p (h d) -> p h d", d=DH),
                        both[:, m, 0:P].rearrange("p (h d) -> p h d", d=DH),
                        dn[:, m, :].unsqueeze(2).to_broadcast([P, P // DH, DH]), ALU.mult), [s1])
                lin_done.append(s2)
                bank_users[n] = [s2]
            linT_done = transpose_tokens(lin_out, lin_outT, lin_done)

            biased = add_bias_to_stream(blo, blo_in)
            project_tokens(lin_outT, linT_done, wlo, wlo_in, accumulate(biased))
            pr.barrier()
            two.close()

        linear_attention()

        def query_softmax_attention():
            pr.stage = "ffn0"
            three = ExitStack()
            w_q, w_q_in = weight(three, "w3_q", io["L0_ffn_Wq"], KD)
            w_k, w_k_in = weight(three, "w3_k", io["L0_ffn_Wk"], KD)
            w_v, w_v_in = weight(three, "w3_v", io["L0_ffn_Wv"], KD)
            w_ff, w_ff_in = weight(three, "w3_ff", io["L0_ffn_Wff"], KD)
            QUADS, HG = 4, H // 4
            w_o = sb(three, "w3_o", [P, HG, D])
            w_o_zero = pool(lambda e: e.memset(w_o[:, :, :], 0.0))
            for j in range(QUADS):
                w_o_in = dma(w_o[32 * j:32 * j + DH, :, :],
                             io["L0_ffn_Wo"].rearrange("(g j d) n -> j d g n", j=QUADS, d=DH)[j], "in_w3_o", [w_o_zero])
            qT = sb(three, "qT", [P, KD, B * S])
            kT = sb(three, "kT", [P, KD, B * S])
            kT_heads = sb(three, "kT_heads", [P, 2, P // DH, S])
            v_tok = sb(three, "v_tok", [P, NT, D])
            NR = 8
            weights3 = sb(three, "weights3", [P, NR, QT, S])
            v_scaled = sb(three, "v_scaled", [P, NR, QT, 32])
            sums3 = sb(three, "sums3", [P, NR, 2, QT])
            outT3 = sb(three, "outT3", [P, HG, B * S])
            norm3 = sb(three, "norm3", [P, 2, NT, 4])
            square3 = sb(three, "square3", [P, 2, D])
            _, xT_done = norm_and_turn(x_ready)
            v_zero = pool(lambda e: e.memset(v_scaled[:, :, :, :], 0.0))

            qd, kd, vd = {}, {}, {}
            project_T(xnT, xT_done, w_k, w_k_in, keep_T(kT, kd))
            project_T(xnT, xT_done, w_q, w_q_in, keep_T(qT, qd))
            project_tokens(xnT, xT_done, w_v, w_v_in, keep_tokens(v_tok, vd))
            heads_ready, heads_users, ring_free = {}, {}, {}
            SC3 = 1.0 / D ** 0.5
            pending = []
            outT3_done = {}
            quad_bank = {}

            def scores3(b, m, h):
                hn = (b * KD + m) * (P // DH) + h
                r = hn % NR
                n, ps, free = next_bank()
                hb = (b * KD + m) % 2
                for kt in range(QT):
                    last = pe(lambda e, kt=kt, ps=ps: e.matmul(
                        ps[:, kt * S:(kt + 1) * S], kT_heads[:, hb, h, kt * P:(kt + 1) * P],
                        qT[:, m, b * S:(b + 1) * S], start=True, stop=True),
                        free + [heads_ready[hb, h], qd[m, b * S // BANK]])
                heads_users[hb, h] = [last]
                peak, total = sums3[:, r, 0, :], sums3[:, r, 1, :]
                s0 = dve(lambda e: e.tensor_reduce(peak, ps.rearrange("p (k q) -> p k q", k=QT), AX.X, ALU.max, negate=True),
                         [last] + ring_free.get(r, []))
                s1 = dve(lambda e: e.tensor_scalar(peak, peak, SC3, None, ALU.mult), [s0])
                for kt in range(QT):
                    s2 = act(lambda e, kt=kt: e.activation(weights3[:, r, kt, :], ps[:, kt * S:(kt + 1) * S], ACT.Exp,
                                                           bias=peak[:, kt:kt + 1], scale=SC3,
                                                           accum_out=total[:, kt:kt + 1]), [s1])
                bank_users[n] = [s2]
                s3 = dve(lambda e: e.reciprocal(total, total), [s2])
                c0 = (m * (P // DH) + h) * DH
                s4 = dve(lambda e: e.tensor_tensor(v_scaled[:, r, :, 0:DH], v_tok[:, QT * b:QT * b + QT, c0:c0 + DH],
                                                   total.unsqueeze(2).to_broadcast([P, QT, DH]), ALU.mult),
                         [s3, v_zero, vd[QT * b], vd[QT * b + 1]])
                return s2, s4

            def values3(b, g, ready):
                n, ps, free = next_bank()
                for kt in range(QT):
                    for j in range(QUADS):
                        r = (b * H + 4 * g + j) % NR
                        last = pe(lambda e, kt=kt, j=j, r=r, ps=ps: e.matmul(
                            ps[32 * j:32 * j + 32, 0:S], v_scaled[:, r, kt, :], weights3[:, r, kt, :],
                            start=(kt == 0), stop=(kt == QT - 1)), free + list(ready[j]))
                for j in range(QUADS):
                    ring_free[(b * H + 4 * g + j) % NR] = [last]
                outT3_done[b, g] = evacuate(outT3[:, g, b * S:(b + 1) * S], ps[:, 0:S], [last])
                bank_users[n] = [outT3_done[b, g]]

            for b in range(B):
                for m in range(KD):
                    isolate_heads(kT, kT_heads, b, m, kd, heads_users, heads_ready)
                    for g in range(2):
                        ready = [scores3(b, m, 4 * g + j) for j in range(QUADS)]
                        pending.append((b, 2 * m + g, ready))
                        if len(pending) > 1:
                            values3(*pending.pop(0))
            values3(*pending.pop(0))

            square_free = [None, None]

            def l2_normalize(which, dst, done):
                def use(t, ps, made):
                    w = norm3[:, which, t, :]
                    s0 = act(lambda e: e.activation(square3[:, t % 2, :], ps, ACT.Square, accum_out=w[:, 0:1]),
                             [made, square_free[t % 2]])
                    square_free[t % 2] = s0
                    s1 = pool(lambda e: e.tensor_tensor(w[:, 1:2], w[:, 0:1], constant("half")[:, 0:1], ALU.pow), [s0])
                    s2 = dve(lambda e: e.tensor_scalar(w[:, 2:3], w[:, 1:2], 1e-12, None, ALU.max), [s1])
                    s3 = dve(lambda e: e.reciprocal(w[:, 3:4], w[:, 2:3]), [s2])
                    done[t] = dve(lambda e: e.tensor_scalar(dst[:, t, :], ps, w[:, 3:4], None, ALU.mult), [s3])
                    return [done[t]]
                return use

            z_done, z2_done = {}, {}
            oT_ready = [[outT3_done[t // QT, g] for g in range(HG)] for t in range(NT)]
            project_tokens(outT3, oT_ready, w_o, w_o_in, l2_normalize(0, xn, z_done), blocks=HG)
            zT_done = transpose_tokens(xn, xnT, z_done)
            project_tokens(xnT, zT_done, w_ff, w_ff_in, l2_normalize(1, v_tok, z2_done))
            for t in range(NT):
                s0 = act(lambda e, t=t: e.activation(v_tok[:, t, :], v_tok[:, t, :], ACT.Gelu), [z2_done[t], x_ready[t]])
                x_ready[t] = dve(lambda e, t=t: e.tensor_tensor(x[:, t, :], x[:, t, :], v_tok[:, t, :], ALU.add), [s0])
            pr.barrier()
            three.close()

        query_softmax_attention()

        def context_attention():
            pr.stage = "xattn1"
            four = ExitStack()
            w_q, w_q_in = weight(four, "w4_q", io["L1_xattn_Wq"], KD)
            w_k, w_k_in = weight(four, "w4_k", io["L1_xattn_Wk"], 1)
            w_v, w_v_in = weight(four, "w4_v", io["L1_xattn_Wv"], 1)
            b_q, b_q_in = bias_columns(four, "b4_q", io["L1_xattn_bq"])
            b_k, b_k_in = bias_columns(four, "b4_k", io["L1_xattn_bk"])
            b_v, b_v_in = bias_rows(four, "b4_v", io["L1_xattn_bv"])
            w_kT = sb(four, "w4_kT", [P, KD, C])
            q4T = sb(four, "q4T", [P, KD, B * S])
            qcT = sb(four, "qcT", [P, B * S])
            offset = sb(four, "offset", [P, NT])
            KT = LC // P
            ctx_nat = sb(four, "ctx_nat", [P, KT, C])
            ctx_T = sb(four, "ctx_T", [P, 2, LC])
            row_w = sb(four, "row_w", [P, 2, LC])
            col_w = sb(four, "col_w", [P, 4, BANK])
            peaks4 = sb(four, "peaks4", [P, 2, 8])
            stat4 = sb(four, "stat4", [P, NT, 6])
            sums4 = sb(four, "sums4", [P, 2, 2])
            ucT = sb(four, "ucT", [P, B * S])
            ctx_here, ctxT_here = {}, {}
            nat_users, T_users = {}, {}

            def fetch_ctx(b):
                for c in range(8):
                    ctx_here[b, c] = dma(ctx_nat[:, 4 * c:4 * c + 4, :],
                                         io["ctx_512"][b, c * BANK:(c + 1) * BANK, :].rearrange("(t p) c -> p t c", p=P),
                                         f"in_nat{c}", nat_users.get((b - 1, c), []))

            def turn_nat(b, c):
                n, ps, free = next_bank()
                for i in range(4):
                    last = pe(lambda e, i=i, ps=ps: e.transpose(ps[:, i * P:(i + 1) * P], ctx_nat[:, 4 * c + i, :], ident),
                              free + [ctx_here[b, c]])
                ctxT_here[b, c] = evacuate(ctx_T[:, b % 2, c * BANK:(c + 1) * BANK], ps, [last] + T_users.get(b - 2, []))
                bank_users[n] = [ctxT_here[b, c]]

            fetch_ctx(0)
            _, xT_done = norm_and_turn(x_ready)
            n, ps, free = next_bank()
            for k in range(KD):
                last = pe(lambda e, k=k, ps=ps: e.transpose(ps[:, k * C:(k + 1) * C], w_k[:, 0, k * P:(k + 1) * P], ident),
                          free + [w_k_in])
            w_kT_done = evacuate(w_kT[:, :, :].rearrange("p k c -> p (k c)"), ps[:, 0:KD * C], [last])
            bank_users[n] = [w_kT_done]
            q4_done = {}

            def keep_q4(m, half, ps, made):
                q4_done[m, half] = act(lambda e: e.activation(q4T[:, m, half * BANK:(half + 1) * BANK], ps, ACT.Identity,
                                                              bias=b_q[:, m:m + 1]), [made, b_q_in])
                return [q4_done[m, half]]

            project_T(xnT, xT_done, w_q, w_q_in, keep_q4)
            qc_done = {}
            for half in range(2):
                n, ps, free = next_bank()
                for k in range(KD):
                    last = pe(lambda e, k=k, half=half, ps=ps: e.matmul(ps, w_kT[:, k, :],
                                                                        q4T[:, k, half * BANK:(half + 1) * BANK],
                                                                        start=(k == 0), stop=(k == KD - 1)),
                              free + [w_kT_done, q4_done[k, half]])
                qc_done[half] = evacuate(qcT[:, half * BANK:(half + 1) * BANK], ps, [last])
                bank_users[n] = [qc_done[half]]
            n, ps, free = next_bank()
            for t in range(NT):
                for k in range(KD):
                    last = pe(lambda e, t=t, k=k, ps=ps: e.matmul(ps[:, t:t + 1], q4T[:, k, t * P:(t + 1) * P], b_k[:, k:k + 1],
                                                                  start=(k == 0), stop=(k == KD - 1)),
                              free + [b_k_in, q4_done[k, t * P // BANK]])
            offset_done = dve(lambda e, ps=ps: e.tensor_copy(offset[:, :], ps[:, 0:NT]), [last])
            bank_users[n] = [offset_done]

            row_free, col_free, uc_done = {}, {}, {}
            exp4 = {}

            def scores4(t):
                b, r = t // QT, t % 2
                copies, maxima = [], []
                for c in range(8):
                    n, ps, free = next_bank()
                    made = pe(lambda e, c=c, ps=ps: e.matmul(ps, qcT[:, t * P:(t + 1) * P],
                                                             ctx_T[:, b % 2, c * BANK:(c + 1) * BANK], start=True, stop=True),
                              free + [qc_done[t * P // BANK], ctxT_here[b, c]])
                    T_users[b] = [made]
                    copies.append(act(lambda e, c=c, ps=ps: e.activation(row_w[:, r, c * BANK:(c + 1) * BANK], ps, ACT.Copy),
                                      [made] + row_free.get(r, [])))
                    maxima.append(dve(lambda e, c=c: e.tensor_reduce(peaks4[:, r, c:c + 1],
                                                                     row_w[:, r, c * BANK:(c + 1) * BANK], AX.X, ALU.max),
                                      [copies[-1]] + ([exp4[t - 2]] if t >= 2 else [])))
                    bank_users[n] = [copies[-1]]
                w = stat4[:, t, :]
                s0 = dve(lambda e: e.tensor_reduce(w[:, 0:1], peaks4[:, r, :], AX.X, ALU.max), [maxima[-1]])
                s1 = dve(lambda e: e.tensor_tensor(w[:, 1:2], w[:, 0:1], offset[:, t:t + 1], ALU.add), [s0, offset_done])
                s2 = dve(lambda e: e.tensor_tensor(w[:, 2:3], offset[:, t:t + 1], w[:, 1:2], ALU.subtract), [s1])
                for half in range(2):
                    exp4[t, half] = act(lambda e, half=half: e.activation(
                        row_w[:, r, half * LC // 2:(half + 1) * LC // 2], row_w[:, r, half * LC // 2:(half + 1) * LC // 2],
                        ACT.Exp, bias=w[:, 2:3], accum_out=w[:, 3 + half:4 + half]), [s2])
                exp4[t] = exp4[t, 1]
                s3 = dve(lambda e: e.tensor_tensor(w[:, 5:6], w[:, 3:4], w[:, 4:5], ALU.add), [exp4[t, 1]])
                exp4[t, "inverse"] = dve(lambda e: e.reciprocal(w[:, 5:6], w[:, 5:6]), [s3])

            def weigh4(t):
                b, r = t // QT, t % 2
                no, acc, free_acc = next_bank()
                held.add(no)
                columns = {}

                def turn_weights(c):
                    n, ps, free = next_bank()
                    for i in range(4):
                        kt = 4 * c + i
                        last = pe(lambda e, i=i, kt=kt, ps=ps: e.transpose(ps[:, i * P:(i + 1) * P],
                                                                           row_w[:, r, kt * P:(kt + 1) * P], ident),
                                  free + [exp4[t, 4 * c // (KT // 2)]])
                    w = col_free["turn"] = (col_free.get("turn", -1) + 1) % 4
                    columns[c] = (w, evacuate(col_w[:, w, :], ps, [last] + col_free.get(w, [])))
                    bank_users[n] = [columns[c][1]]
                    return last

                def weigh(c):
                    w, ready = columns[c]
                    for i in range(4):
                        kt = 4 * c + i
                        last = pe(lambda e, i=i, kt=kt, w=w: e.matmul(acc[:, 0:P], ctx_nat[:, kt, :],
                                                                      col_w[:, w, i * P:(i + 1) * P],
                                                                      start=(kt == 0), stop=(kt == KT - 1)),
                                  free_acc + [ready, ctx_here[b, c]])
                    col_free[w] = [last]
                    nat_users[b, c] = nat_users.get((b, c), []) + [last]
                    return last

                for c in range(8):
                    turned = turn_weights(c)
                    if c >= 2:
                        weigh(c - 2)
                row_free[r] = [turned]
                weigh(6)
                last = weigh(7)
                uc_done[t] = evacuate(ucT[:, t * P:(t + 1) * P], acc[:, 0:P], [last])
                bank_users[no] = [uc_done[t]]
                held.discard(no)

            for c in range(8):
                turn_nat(0, c)
            scores4(0)
            for t in range(NT):
                if t % QT == 0 and t + 1 < NT:
                    scores4(t + 1)
                weigh4(t)
                if t % QT == 1 and t + 1 < NT:
                    fetch_ctx(t // QT + 1)
                    for c in range(8):
                        turn_nat(t // QT + 1, c)
                    scores4(t + 1)
            biased = [pool(lambda e, t=t: e.tensor_tensor(x[:, t, :], x[:, t, :], b_v[:, :], ALU.add),
                           [x_ready[t], b_v_in, pr.last_norm]) for t in range(NT)]
            for t in range(NT):
                n, ps, free = next_bank()
                last = pe(lambda e, t=t, ps=ps: e.matmul(ps[:, 0:D], ucT[:, t * P:(t + 1) * P], w_v[:, 0, :],
                                                         start=True, stop=True), free + [uc_done[t], w_v_in])
                x_ready[t] = dve(lambda e, t=t, ps=ps: e.scalar_tensor_tensor(
                    out=x[:, t, :], in0=ps[:, 0:D], scalar=stat4[:, t, 5:6], in1=x[:, t, :], op0=ALU.mult, op1=ALU.add),
                    [last, biased[t], exp4[t, "inverse"]])
                bank_users[n] = [x_ready[t]]
            pr.barrier()
            four.close()

        context_attention()

        def causal_attention():
            pr.stage = "attn1"
            five = ExitStack()
            w_in = {}
            w_rows = sb(five, "w5_rows", [P, 3, KD, D])
            w5 = [sb(five, f"w5_{n}", [P, KD, D]) for n in "qkv"]
            for n, name in enumerate("qkv"):
                w_in[n] = dma(w_rows[:, n, :, :], io[f"L1_attn_w{name}"].rearrange("(k p) n -> p k n", p=P), f"in_w5_{name}")
            qk = sb(five, "qk", [P, NT, 2, D])
            rotated = sb(five, "rotated", [P, NT, 2, D])
            v5 = sb(five, "v5", [P, NT, D])
            turned5 = sb(five, "turned5", [P, 2, KD, B * S])
            rows5 = sb(five, "rows5", [P, NT, S])
            cols5 = sb(five, "cols5", [P, NT, QT, P])
            stat5 = sb(five, "stat5", [P, NT, 4])
            _, xT_done = norm_and_turn(x_ready)
            w5_done = []
            for w in range(3):
                n, ps, free = next_bank()
                for k in range(KD):
                    for m in range(KD):
                        last = pe(lambda e, k=k, m=m, w=w, ps=ps: e.transpose(
                            ps[:, (k * KD + m) * P:(k * KD + m + 1) * P], w_rows[:, w, m, k * P:(k + 1) * P], ident),
                            free + [w_in[w]])
                w5_done.append(evacuate(w5[w][:, :, :].rearrange("p k n -> p (k n)"), ps, [last]))
                bank_users[n] = [w5_done[w]]
            qk_done = [{}, {}]
            for w in range(2):
                project_tokens(xnT, xT_done, w5[w], w5_done[w], keep_tokens(qk[:, :, w, :], qk_done[w]))
            v5_done = {}
            project_tokens(xnT, xT_done, w5[2], w5_done[2], keep_tokens(v5, v5_done))
            cos = constant("cos").rearrange("p (t d) -> p t d", t=QT)
            sin = constant("sin").rearrange("p (t d) -> p t d", t=QT)
            turned_done = [{}, {}]
            for t in range(NT):
                i = t % QT
                for w in range(2):
                    src, dst, other = qk[:, t, w, :], rotated[:, t, w, :], xn[:, t, :]
                    pair = lambda a, o: a.rearrange("p (n two) -> p n two", two=2)[:, :, o]
                    s0 = dve(lambda e, src=src, dst=dst, i=i: e.tensor_tensor(dst, src, cos[:, i, :], ALU.mult),
                             [qk_done[w][t], const2_in, pr.last_norm] + [s for s in xT_done[t]])
                    for o in range(2):
                        s1 = pool(lambda e, src=src, other=other, o=o, i=i, pair=pair: e.tensor_tensor(
                            pair(other, o), pair(src, 1 - o), pair(sin[:, i, :], o), ALU.mult),
                            [qk_done[w][t], const2_in] + xT_done[t] + ([last_rot] if w else []))
                    last_rot = dve(lambda e, dst=dst, other=other: e.tensor_tensor(dst, dst, other, ALU.add), [s0, s1])
                    turned_done[w][t] = last_rot
            tT = []
            for w in range(2):
                tT.append(transpose_tokens(rotated[:, :, w, :], turned5[:, w, :, :], turned_done[w]))
            SC5 = 1.0 / D ** 0.5
            out5 = {}
            for t in range(NT):
                b, i = divmod(t, QT)
                width = (i + 1) * P
                n, ps, free = next_bank()
                for k in range(KD):
                    last = pe(lambda e, t=t, b=b, k=k, width=width, ps=ps: e.matmul(
                        ps[:, 0:width], turned5[:, 0, k, t * P:(t + 1) * P], turned5[:, 1, k, b * S:b * S + width],
                        start=(k == 0), stop=(k == KD - 1)),
                        free + tT[0][t] + [s for u in range(QT * b, QT * b + i + 1) for s in tT[1][u]])
                w = stat5[:, t, :]
                row = rows5[:, t, 0:width]
                steps = []
                if i:
                    steps.append(act(lambda e, row=row, ps=ps, i=i: e.activation(row[:, 0:i * P], ps[:, 0:i * P], ACT.Copy,
                                                                                 scale=SC5), [last]))
                steps.append(dve(lambda e, row=row, ps=ps, i=i: e.scalar_tensor_tensor(
                    out=row[:, i * P:(i + 1) * P], in0=ps[:, i * P:(i + 1) * P], scalar=SC5, in1=constant("causal"),
                    op0=ALU.mult, op1=ALU.add), [last] + steps))
                bank_users[n] = steps
                s0 = dve(lambda e, w=w, row=row: e.tensor_reduce(w[:, 0:1], row, AX.X, ALU.max, negate=True), steps)
                s1 = act(lambda e, w=w, row=row: e.activation(row, row, ACT.Exp, bias=w[:, 0:1], accum_out=w[:, 1:2]), [s0])
                s2 = dve(lambda e, w=w: e.reciprocal(w[:, 2:3], w[:, 1:2]), [s1])
                out5[t] = (s1, s2)
            for t in range(NT):
                b, i = divmod(t, QT)
                s1, s2 = out5[t]
                n, ps, free = next_bank()
                for kt in range(i + 1):
                    last = pe(lambda e, t=t, kt=kt, ps=ps: e.transpose(ps[:, kt * P:(kt + 1) * P],
                                                                       rows5[:, t, kt * P:(kt + 1) * P], ident), free + [s1])
                s3 = evacuate(cols5[:, t, 0:i + 1, :].rearrange("p k q -> p (k q)"), ps[:, 0:(i + 1) * P], [last])
                bank_users[n] = [s3]
                out5[t] = (s3, s2)
            for t in range(NT):
                b, i = divmod(t, QT)
                s3, s2 = out5[t]
                n, ps, free = next_bank()
                for kt in range(i + 1):
                    last = pe(lambda e, t=t, b=b, i=i, kt=kt, ps=ps: e.matmul(
                        ps[:, 0:D], cols5[:, t, kt, :], v5[:, QT * b + kt, :], start=(kt == 0), stop=(kt == i)),
                        free + [s3, v5_done[QT * b + kt]])
                x_ready[t] = dve(lambda e, t=t, ps=ps: e.scalar_tensor_tensor(
                    out=x[:, t, :], in0=ps[:, 0:D], scalar=stat5[:, t, 2:3], in1=x[:, t, :], op0=ALU.mult, op1=ALU.add),
                    [last, s2, pr.last_norm])
                bank_users[n] = [x_ready[t]]
            pr.barrier()
            five.close()

        causal_attention()

        def attention_and_experts():
            pr.stage = "ffn1"
            six = ExitStack()
            w6 = {n: weight(six, f"w6_{n}", io[f"L1_ffn_W{n}"], KD) for n in "qkvog"}
            rows6 = {n: bias_rows(six, f"r6_{n}", io[f"L1_ffn_{n}"]) for n in ("g1", "b1", "g2", "b2")}
            w1 = sb(six, "w6_1", [P, KD, NE, HID])
            w1_in = None
            for k in range(KD):
                w1_in = dma(w1[:, k, :, :], io["L1_ffn_W1"][:, k * P:(k + 1) * P, :].rearrange("e p h -> p e h"), "in_w6_1")
            w2 = sb(six, "w6_2", [P, NE, D])
            w2_in = dma(w2[:, :, :], io["L1_ffn_W2"].rearrange("e h n -> h e n"), "in_w6_2")
            y = sb(six, "y", [P, NT, D])
            qT = sb(six, "q6T", [P, KD, B * S])
            kT = sb(six, "k6T", [P, KD, B * S])
            q_heads = sb(six, "q_heads", [P, 2, P // DH, S])
            v6 = sb(six, "v6", [P, NT, D])
            NR6 = 4
            rows_w = sb(six, "rows_w", [P, NR6, QT, S])
            cols_w = sb(six, "cols_w", [P, NR6, QT, S])
            stat6b = sb(six, "stat6b", [P, B * H, 2, QT])
            gates = sb(six, "gates", [P, NT, NE])
            top = sb(six, "top", [P, NT, NE])
            top_at = sb(six, "top_at", [P, NT, NE], U32)
            top_f = sb(six, "top_f", [P, NT, 2])
            pick = sb(six, "pick", [P, NT, 2, NE])
            prob = sb(six, "prob", [P, NT, 4])
            mix = sb(six, "mix", [P, NT, NE])
            hiddenT = sb(six, "hiddenT", [P, NE, BANK])

            def affine(g, b, ready):
                steps = []
                for t in range(NT):
                    s0 = pool(lambda e, t=t: e.tensor_tensor(xn[:, t, :], xn[:, t, :], g[0][:, :], ALU.mult), [ready[t], g[1]])
                    steps.append(dve(lambda e, t=t: e.tensor_tensor(xn[:, t, :], xn[:, t, :], b[0][:, :], ALU.add), [s0, b[1]]))
                return steps

            y_made = layer_norm(x, y, x_ready)
            normed = layer_norm(y, xn, y_made)
            xn_made = affine(rows6["g1"], rows6["b1"], normed)
            xT_done = transpose_tokens(xn, xnT, xn_made)
            qd, kd, vd = {}, {}, {}
            project_T(xnT, xT_done, *w6["q"], keep_T(qT, qd))
            project_T(xnT, xT_done, *w6["k"], keep_T(kT, kd))
            project_tokens(xnT, xT_done, *w6["v"], keep_tokens(v6, vd))
            heads_ready, heads_users = {}, {}
            SC6 = DH ** -0.5
            rows_free, cols_free = {}, {}

            def scores6(b, m, h):
                hn = (b * KD + m) * (P // DH) + h
                r, hb = hn % NR6, (b * KD + m) % 2
                n, ps, free = next_bank()
                for i in range(QT):
                    last = pe(lambda e, i=i, ps=ps: e.matmul(ps[:, i * S:(i + 1) * S], q_heads[:, hb, h, i * P:(i + 1) * P],
                                                             kT[:, m, b * S:(b + 1) * S], start=True, stop=True),
                              free + [heads_ready[hb, h], kd[m, b * S // BANK]])
                heads_users[hb, h] = [last]
                peak, total = stat6b[:, hn, 0, :], stat6b[:, hn, 1, :]
                s0 = dve(lambda e: e.tensor_reduce(peak, ps.rearrange("p (k q) -> p k q", k=QT), AX.X, ALU.max, negate=True),
                         [last])
                s1 = dve(lambda e: e.tensor_scalar(peak, peak, SC6, None, ALU.mult), [s0])
                for i in range(QT):
                    s2 = act(lambda e, i=i: e.activation(rows_w[:, r, i, :], ps[:, i * S:(i + 1) * S], ACT.Exp,
                                                         bias=peak[:, i:i + 1], scale=SC6, accum_out=total[:, i:i + 1]),
                             [s1] + rows_free.get(r, []))
                bank_users[n] = [s2]
                return s2

            def turn6(b, m, h, made):
                hn = (b * KD + m) * (P // DH) + h
                r = hn % NR6
                n, ps, free = next_bank()
                for kt in range(QT):
                    for i in range(QT):
                        last = pe(lambda e, kt=kt, i=i, ps=ps: e.transpose(
                            ps[:, kt * S + i * P:kt * S + (i + 1) * P], rows_w[:, r, i, kt * P:(kt + 1) * P], ident),
                            free + [made])
                rows_free[r] = [last]
                s = evacuate(cols_w[:, r, :, :].rearrange("p k q -> p (k q)"), ps, [last] + cols_free.get(r, []))
                bank_users[n] = [s]
                return s

            out_bank, o_done = {}, []
            sums_ready = {}

            def weigh6(b, m, h, ready):
                hn = (b * KD + m) * (P // DH) + h
                r, c0 = hn % NR6, (m * (P // DH) + h) * DH
                if m == 0 and h == 0:
                    out_bank[b] = next_bank()
                    held.add(out_bank[b][0])
                no, acc, free_acc = out_bank[b]
                for i in range(QT):
                    for kt in range(QT):
                        last = pe(lambda e, i=i, kt=kt: e.matmul(
                            acc[:, i * D + c0:i * D + c0 + DH], cols_w[:, r, kt, i * P:(i + 1) * P],
                            v6[:, QT * b + kt, c0:c0 + DH], start=(kt == 0), stop=(kt == QT - 1)),
                            free_acc + [ready, vd[QT * b + kt]])
                cols_free[r] = [last]
                if m == KD - 1 and h == P // DH - 1:
                    inverse = dve(lambda e: e.reciprocal(stat6b[:, b * H:(b + 1) * H, 1, :], stat6b[:, b * H:(b + 1) * H, 1, :]),
                                  [sums_ready[b]])
                    for i in range(QT):
                        s = dve(lambda e, i=i: e.tensor_tensor(
                            xn[:, QT * b + i, :].rearrange("p (h d) -> p h d", d=DH),
                            acc[:, i * D:(i + 1) * D].rearrange("p (h d) -> p h d", d=DH),
                            stat6b[:, b * H:(b + 1) * H, 1, i].unsqueeze(2).to_broadcast([P, H, DH]), ALU.mult),
                            [last, inverse])
                        o_done.append(s)
                    bank_users[no] = [s]
                    held.discard(no)

            stage1, stage2 = [], []
            for b in range(B):
                for m in range(KD):
                    isolate_heads(qT, q_heads, b, m, qd, heads_users, heads_ready)
                    for h in range(P // DH):
                        made = scores6(b, m, h)
                        sums_ready[b] = made
                        stage1.append((b, m, h, made))
                        if len(stage1) > 2:
                            job = stage1.pop(0)
                            stage2.append(job[:3] + (turn6(*job),))
                        if len(stage2) > 1:
                            weigh6(*stage2.pop(0))
            for job in stage1:
                stage2.append(job[:3] + (turn6(*job),))
                weigh6(*stage2.pop(0))
            while stage2:
                weigh6(*stage2.pop(0))
            oT_done = transpose_tokens(xn, xnT, o_done)
            y_ready = [None] * NT

            def add_to_y(t, ps, made):
                y_ready[t] = dve(lambda e: e.tensor_tensor(y[:, t, :], ps, y[:, t, :], ALU.add), [made])
                return [y_ready[t]]

            project_tokens(xnT, oT_done, *w6["o"], add_to_y)
            normed = layer_norm(y, xn, y_ready)
            xn_made = affine(rows6["g2"], rows6["b2"], normed)
            xT_done = transpose_tokens(xn, xnT, xn_made)
            base = [pool(lambda e, t=t: e.tensor_tensor(x[:, t, :], x[:, t, :], y[:, t, :], ALU.add), [y_ready[t]])
                    for t in range(NT)]
            gate_done = {}
            project_tokens(xnT, xT_done, *w6["g"], keep_tokens(gates, gate_done), cols=slice(0, NE))
            mix_done = {}
            for t in range(NT):
                g, p4 = gates[:, t, :], prob[:, t, :]
                s0 = dve(lambda e, t=t, g=g: e.max(top[:, t, :], g), [gate_done[t]])
                s1 = dve(lambda e, t=t, g=g: e.max_index(top_at[:, t, :], top[:, t, :], g), [s0])
                s2 = dve(lambda e, t=t: e.tensor_copy(top_f[:, t, :], top_at[:, t, 0:2]), [s1])
                s3 = dve(lambda e, t=t, p4=p4: e.tensor_scalar(p4[:, 0:2], top[:, t, 0:2], top[:, t, 0:1], None, ALU.subtract), [s0])
                s4 = act(lambda e, p4=p4: e.activation(p4[:, 0:2], p4[:, 0:2], ACT.Exp, accum_out=p4[:, 2:3]), [s3])
                s5 = dve(lambda e, p4=p4: e.reciprocal(p4[:, 3:4], p4[:, 2:3]), [s4])
                s6 = dve(lambda e, p4=p4: e.tensor_scalar(p4[:, 0:2], p4[:, 0:2], p4[:, 3:4], None, ALU.mult), [s5])
                for j in range(2):
                    s7 = dve(lambda e, t=t, j=j, p4=p4: e.tensor_scalar(pick[:, t, j, :], constant("iota"), top_f[:, t, j:j + 1],
                                                                        p4[:, j:j + 1], ALU.is_equal, ALU.mult), [s2, s6])
                mix_done[t] = dve(lambda e, t=t: e.tensor_tensor(mix[:, t, :], pick[:, t, 0, :], pick[:, t, 1, :], ALU.add), [s7])
            hidden_free = {}
            final = [base[t] for t in range(NT)]
            for half in range(2):
                hidden_done = {}
                for ex in range(NE):
                    n, ps, free = next_bank()
                    for k in range(KD):
                        last = pe(lambda e, k=k, ex=ex, half=half, ps=ps: e.matmul(
                            ps, w1[:, k, ex, :], xnT[:, k, half * BANK:(half + 1) * BANK],
                            start=(k == 0), stop=(k == KD - 1)),
                            free + [s for t in range(4 * half, 4 * half + 4) for s in xT_done[t]] + [w1_in])
                    hidden_done[ex] = act(lambda e, ex=ex, ps=ps: e.activation(hiddenT[:, ex, :], ps, ACT.Relu),
                                          [last, hidden_free.get(ex)])
                    bank_users[n] = [hidden_done[ex]]
                for i in range(4):
                    t = 4 * half + i
                    for ex in range(NE):
                        if ex % 2 == 0:
                            n, ps, free = next_bank()
                        cols = slice((ex % 2) * D, (ex % 2 + 1) * D)
                        last = pe(lambda e, ex=ex, i=i, ps=ps, cols=cols: e.matmul(
                            ps[:, cols], hiddenT[:, ex, i * P:(i + 1) * P], w2[:, ex, :], start=True, stop=True),
                            free + [hidden_done[ex], w2_in])
                        hidden_free[ex] = last
                        if ex % 2:
                            for o in (ex - 1, ex):
                                final[t] = dve(lambda e, t=t, o=o, ps=ps: e.scalar_tensor_tensor(
                                    out=x[:, t, :], in0=ps[:, (o % 2) * D:(o % 2 + 1) * D], scalar=mix[:, t, o:o + 1],
                                    in1=x[:, t, :], op0=ALU.mult, op1=ALU.add), [last, mix_done[t], final[t]])
                            bank_users[n] = [final[t]]
            x_ready[:] = final
            six.close()

        attention_and_experts()

        stored = dma(out.rearrange("b (t p) d -> p (b t) d", p=P), x[:, :, :], "store", x_ready)
        pr.emit()


def kernel(**inputs):
    import numpy as _np
    import concourse.bacc as _bacc
    from concourse import mybir as _mybir
    from concourse.bass_utils import run_bass_kernel_spmd as _run

    nc = _bacc.Bacc("TRN2", target_bir_lowering=False, num_devices=1)
    host = {name: _np.ascontiguousarray(a) for name, a in inputs.items()}
    host["const"], host["const2"] = constants()
    arrays, io = {}, {}
    for name, a in host.items():
        arrays[f"in_{name}_dram"] = a
        io[name] = nc.dram_tensor(f"in_{name}_dram", a.shape, _mybir.dt.from_np(a.dtype), kind="ExternalInput").ap()
    out = nc.dram_tensor("out_0_dram", (B, S, D), _mybir.dt.float32, kind="ExternalOutput").ap()
    build(nc, io, out)
    r = _run(nc, [arrays], core_ids=[0])
    return r.results[0]["out_0_dram"]
```

```python
from contextlib import ExitStack

import numpy as np

import concourse.bass as bass
from concourse import mybir

F32 = mybir.dt.float32
BF16 = mybir.dt.bfloat16
U32 = mybir.dt.uint32
ACT = mybir.ActivationFunctionType
ALU = mybir.AluOpType
AX = mybir.AxisListType

P = 128
B, S, D = 4, 256, 256
LC, C = 4096, 128
H, DH = 16, 16
NT = B * S // P
KD = D // P
QT = S // P
EPS_LN = 1e-5
BANK = 512
NE, HID = 8, 128

CONST_COLS = {}


def constants():
    p = np.arange(P)
    ident = np.eye(P, dtype=np.float32)
    head_block = (p[:, None] // DH == p[None, :] // DH).astype(np.float32)
    head_col = (p[:, None] // DH == np.arange(P // DH)[None, :]).astype(np.float32)
    gather = np.zeros((P, 2 * (DH + 1)), np.float32)
    for quad in range(4):
        for r in range(DH + 1):
            gather[32 * quad + r, (quad % 2) * (DH + 1) + r] = 1.0
    gather4 = np.zeros((P, 4 * (DH + 1)), np.float32)
    for quad in range(4):
        for r in range(DH + 1):
            gather4[32 * quad + r, quad * (DH + 1) + r] = 1.0
    pos = np.arange(S, dtype=np.float32)[:, None]
    inv = (np.float32(1.0) / np.float32(10000.0) ** (np.arange(0, D, 2, dtype=np.float32) / np.float32(D))).astype(np.float32)
    freqs = (pos * inv).astype(np.float32)
    cos = np.repeat(np.cos(freqs), 2, axis=-1)
    sin = np.repeat(np.sin(freqs), 2, axis=-1)
    sin[:, 0::2] *= -1.0
    by_tile = lambda a: a.reshape(QT, P, D).transpose(1, 0, 2).reshape(P, QT * D)
    causal = np.where(p[None, :] > p[:, None], np.float32(-3e38), np.float32(0.0)).astype(np.float32)
    iota = np.broadcast_to(np.arange(NE, dtype=np.float32), (P, NE))
    minus_half, half = np.full((P, NT), -0.5, np.float32), np.full((P, NT), 0.5, np.float32)
    groups = ([("ident", ident), ("gather", gather), ("minus_half", minus_half), ("half", half)],
              [("head_block", head_block), ("head_col", head_col), ("cos", by_tile(cos)), ("sin", by_tile(sin)),
               ("causal", causal), ("iota", iota), ("gather4", gather4)])
    for n, parts in enumerate(groups):
        at = 0
        for name, a in parts:
            CONST_COLS[name] = (n, at, at + a.shape[1])
            at += a.shape[1]
    return [np.ascontiguousarray(np.concatenate([a for _, a in parts], axis=1), dtype=np.float32) for parts in groups]


class Step:

    def __init__(self, queue, make, after, dma_sem, stage):
        self.queue, self.make, self.after, self.dma_sem, self.stage = queue, make, after, dma_sem, stage
        self.wanted = dma_sem is not None
        self.value = None


class Program:

    ENGINES = ("tensor", "vector", "scalar", "gpsimd", "sync")

    def __init__(self, nc, ctx):
        self.nc, self.ctx = nc, ctx
        self.queues = {e: [] for e in self.ENGINES}
        self.stage = "start"
        self.fences = {e: [] for e in self.ENGINES}

    def put(self, engine, make, after=(), dma_sem=None):
        steps = [s for s in list(after) + self.fences[engine] if s is not None]
        self.fences[engine] = []
        for s in steps:
            s.wanted = True
        step = Step(engine, make, steps, dma_sem, self.stage)
        self.queues[engine].append(step)
        return step

    def pe(self, make, after=()):
        return self.put("tensor", make, after)

    def dve(self, make, after=()):
        return self.put("vector", make, after)

    def act(self, make, after=()):
        return self.put("scalar", make, after)

    def pool(self, make, after=()):
        queue = self.queues["gpsimd"]
        if queue:
            after = list(after) + [queue[-1]]
        return self.put("gpsimd", make, after)

    def dma(self, out, in_, sem, after=(), engine="sync", **how):
        return self.put(engine, lambda e: e.dma_start(out, in_, **how), after, dma_sem=sem)

    def barrier(self):
        last = [q[-1] for q in self.queues.values() if q]
        for e in self.ENGINES:
            self.fences[e] = [s for s in last if s.queue != e or e != "tensor"]

    def emit(self):
        nc, sems, counts = self.nc, {}, {}
        for engine, queue in self.queues.items():
            for s in queue:
                if s.wanted:
                    name = s.dma_sem or f"{engine}_{s.stage}"
                    if name not in sems:
                        sems[name] = self.ctx.enter_context(nc.semaphore(name))
                        counts[name] = 0
                    counts[name] += 16 if s.dma_sem else 1
                    s.value = (name, counts[name])
        self.counts = counts
        block = self.ctx.enter_context(nc.Block())

        def run(queue):
            def body(engine):
                reached = {}
                for s in queue:
                    need = {}
                    for a in s.after:
                        name, value = a.value
                        need[name] = max(need.get(name, 0), value)
                    for name, value in need.items():
                        if reached.get(name, 0) < value:
                            engine.wait_ge(sems[name], value)
                            reached[name] = value
                    instruction = s.make(engine)
                    if s.wanted:
                        instruction.then_inc(sems[s.value[0]], 16 if s.dma_sem else 1)
                if queue is self.queues["sync"]:
                    engine.wait_ge(sems["store"], counts["store"])
            return body

        block.tensor(run(self.queues["tensor"]))
        block.vector(run(self.queues["vector"]))
        block.scalar(run(self.queues["scalar"]))
        block.gpsimd(run(self.queues["gpsimd"]))
        block.sync(run(self.queues["sync"]))


def build(nc, io, out, stages=6):
    ctx = ExitStack()
    with ctx:
        pr = Program(nc, ctx)
        pe, dve, act, pool, dma = pr.pe, pr.dve, pr.act, pr.pool, pr.dma
        psum = ctx.enter_context(nc.psum_tensor("psum", [P, 8 * BANK], F32))
        bank_users = [[] for _ in range(8)]
        bank_turn = [0]
        held = set()

        def bank(k):
            return psum[:, k * BANK:(k + 1) * BANK]

        def next_bank():
            k = bank_turn[0] % 8
            bank_turn[0] += 1
            while k in held:
                k = bank_turn[0] % 8
                bank_turn[0] += 1
            return k, bank(k), bank_users[k]

        def sb(scope, name, shape, dt=F32):
            return scope.enter_context(nc.sbuf_tensor(name, shape, dt))

        const_tiles = [sb(ctx, "const", [P, io["const"].shape[1]]), None]
        const_in = dma(const_tiles[0][:, :], io["const"], "in_const")

        def constant(name):
            n, a, b = CONST_COLS[name]
            return const_tiles[n][:, a:b]

        ident = constant("ident")
        small = sb(ctx, "small", [P, 512])
        stat6 = small[:, 0:NT * 6].rearrange("p (t s) -> p t s", t=NT)
        meanvar = small[:, 48:48 + NT * 2].rearrange("p (t s) -> p t s", t=NT)
        rstd = small[:, 64:64 + NT]

        evacs = [0]

        def evacuate(dst, src, after):
            evacs[0] += 1
            if evacs[0] % 2:
                return act(lambda e: e.activation(dst, src, ACT.Copy), after)
            return dve(lambda e: e.tensor_copy(dst, src), after)

        def layer_norm(x, xn, after):
            steps = []
            for half in range(2):
                tiles = range(half * NT // 2, (half + 1) * NT // 2)
                own = slice(tiles[0], tiles[-1] + 1)
                stats = [dve(lambda e, t=t: e.bn_stats(stat6[:, t, :], x[:, t, :]), [after[t]]) for t in tiles]
                means = [dve(lambda e, t=t: e.bn_aggr(meanvar[:, t, :], stat6[:, t, :]), [stats[t - tiles[0]]])
                         for t in tiles]
                guarded = dve(lambda e, own=own: e.tensor_scalar(rstd[:, own], meanvar[:, own, 1], EPS_LN, None,
                                                                 ALU.add), means)
                inverse = pool(lambda e, own=own: e.tensor_tensor(rstd[:, own], rstd[:, own],
                                                                  constant("minus_half")[:, own], ALU.pow),
                               [guarded, const_in])
                steps += [dve(lambda e, t=t: e.tensor_scalar(xn[:, t, :], x[:, t, :], meanvar[:, t, 0:1],
                                                             rstd[:, t:t + 1], ALU.subtract, ALU.mult), [inverse])
                          for t in tiles]
            pr.last_norm = steps[-1]
            return steps

        def transpose_tokens(xn, xnT, ready, affine=None):
            done = [[] for _ in range(NT)]
            for t0 in range(0, NT, 4):
                for k in range(KD):
                    n, ps, free = next_bank()
                    for i in range(4):
                        last = pe(lambda e, t=t0 + i, i=i, k=k, ps=ps: e.transpose(
                            ps[:, i * P:(i + 1) * P], xn[:, t, k * P:(k + 1) * P], ident),
                            free + [ready[t0 + i], const_in])
                    dst = xnT[:, k, t0 * P:(t0 + 4) * P]
                    if affine:
                        (g, g_in), (bias, bias_in) = affine
                        copied = dve(lambda e, dst=dst, ps=ps, k=k: e.tensor_scalar(
                            dst, ps, g[:, k:k + 1], bias[:, k:k + 1], ALU.mult, ALU.add), [last, g_in, bias_in])
                    else:
                        copied = evacuate(dst, ps, [last])
                    bank_users[n] = [copied]
                    for i in range(4):
                        done[t0 + i].append(copied)
            return done

        def project_tokens(actT, ready, w, w_ready, use, cols=slice(0, D), blocks=KD, tiles=range(NT)):
            width = cols.stop - cols.start
            taken = {}
            for t in tiles:
                n, ps, free = next_bank()
                for k in range(blocks):
                    last = pe(lambda e, t=t, k=k, ps=ps: e.matmul(
                        ps[:, 0:width], actT[:, k, t * P:(t + 1) * P], w[:, k, cols],
                        start=(k == 0), stop=(k == blocks - 1)), free + list(ready[t]) + [w_ready])
                bank_users[n] = use(t, ps[:, 0:width], last)
                taken[t] = n
            return taken

        def project_T(actT, ready, w, w_ready, use, col0=0):
            for half in range(2):
                for m in range(KD):
                    n, ps, free = next_bank()
                    for k in range(KD):
                        last = pe(lambda e, m=m, k=k, half=half, ps=ps: e.matmul(
                            ps, w[:, k, col0 + m * P:col0 + (m + 1) * P], actT[:, k, half * BANK:(half + 1) * BANK],
                            start=(k == 0), stop=(k == KD - 1)),
                            free + [s for t in range(4 * half, 4 * half + 4) for s in ready[t]] + [w_ready])
                    bank_users[n] = use(m, half, ps, last)

        def weight(scope, name, source, blocks, sem=None):
            n = source.shape[1]
            w = sb(scope, name, [P, blocks, n])
            return w, dma(w[:, :, :], source.rearrange("(k p) n -> p k n", p=P), sem or f"in_{name}")

        def bias_rows(scope, name, source):
            row = sb(scope, name, [P, D])
            return row, dma(row[:, :], source.partition_broadcast(P), f"in_{name}")

        def bias_columns(scope, name, source):
            col = sb(scope, name, [P, KD])
            return col, dma(col[:, :], source.rearrange("(m p) -> p m", p=P), f"in_{name}",
                            allow_slow_non_contiguous=True)

        pr.stage = "xattn0"
        x = sb(ctx, "x", [P, NT, D])
        heads_out = x
        wo_sb, bv_sb, bo_sb = sb(ctx, "wo", [P, KD, D]), sb(ctx, "bv", [P, D]), sb(ctx, "bo", [P, D])
        one = ExitStack()
        PARTS = 3
        PAIRS = 6
        ROWS = PAIRS * DH
        AUG = ROWS + 2
        GH = 2
        NG = H // GH
        GROUPS = B * NG
        SLOTS = LC // P // 2
        UNIT_GROUPS = P // (GH * DH)
        RING = 3
        keysT = sb(one, "keysT", [P, RING, GH, LC], BF16)
        values = sb(one, "values", [P, LC // P, H, DH + 1])
        q_parts = sb(one, "q_parts", [P, NT, PARTS, D], BF16)
        q_rows = sb(one, "q_rows", [P, QT, H // 2, ROWS], BF16)
        queriesT = sb(one, "queriesT", [P, 4, GH, S], BF16)
        key_parts = sb(one, "key_parts", [P, 2, PARTS, LC], BF16)
        ctxT = sb(one, "ctxT", [P, LC])
        probs = sb(one, "probs", [P, 2, 4 * S])
        ctx_in = sb(one, "ctx_in", [P, 2, 4, C])
        key_f = sb(one, "key_f", [P, 2, BANK])
        key_r = sb(one, "key_r", [P, BANK])
        outT = sb(one, "outT", [P, S])
        ident_b = sb(one, "ident_b", [P, P], BF16)
        peaks = sb(one, "peaks", [P, 2, GH * QT, 8])
        shift = sb(one, "shift", [P, 2, 3, GH * QT])
        shift_b = sb(one, "shift_b", [P, 2, GH * QT, 2], BF16)
        recip = sb(one, "recip", [P, QT, GH])
        early = keysT[:, 2, :, :].rearrange("p h n -> p (h n)").bitcast(F32)
        x_norm = early[:, 0:NT * D].rearrange("p (t d) -> p t d", t=NT)
        x_normT = early[:, NT * D:2 * NT * D].rearrange("p (k n) -> p k n", k=KD)
        x0 = ctxT[:, LC - NT * D:LC].rearrange("p (t d) -> p t d", t=NT)
        wq = probs[:, 0, 0:KD * D].rearrange("p (k n) -> p k n", k=KD)
        bq = probs[:, 0, KD * D:KD * D + D]
        q_work = probs[:, 1, :].rearrange("p (w d) -> p w d", w=4)

        x_tiles = io["x"].rearrange("b (t p) d -> p (b t) d", p=P)
        ctx_first = key_parts[:, 1, :, :].rearrange("p i n -> p (i n)").bitcast(F32)[:, 0:LC].rearrange(
            "p (n t c) -> p n t c", t=4, c=C)
        CH = LC // BANK
        ctx_loaded = {}

        def load_first_ctx(c, chunks):
            step = dma(ctx_first[:, c:c + chunks, :, :],
                       io["ctx_512"][0, c * BANK:(c + chunks) * BANK, :].rearrange(
                           "(n t p) c -> p n t c", p=P, t=4), f"in_first{c}")
            for k in range(c, c + chunks):
                ctx_loaded[0, k] = step

        load_first_ctx(0, 1)
        x_in = [dma(x0[:, 0:NT // 2, :], x_tiles[:, 0:NT // 2, :], "in_x0")] * (NT // 2)
        wk, wk_in = weight(one, "wk", io["L0_xattn_Wk"], 1)
        bk, bk_in = bias_columns(one, "bk", io["L0_xattn_bk"])
        load_first_ctx(1, 1)
        x_in += [dma(x0[:, NT // 2:NT, :], x_tiles[:, NT // 2:NT, :], "in_x1")] * (NT // 2)
        wq_in = dma(wq, io["L0_xattn_Wq"].rearrange("(k p) n -> p k n", p=P), "in_wq")
        bq_in = dma(bq, io["L0_xattn_bq"].partition_broadcast(P), "in_bq")
        load_first_ctx(2, 2)
        load_first_ctx(4, 4)
        wv, wv_in = weight(one, "wv", io["L0_xattn_Wv"], 1)
        ident_b_made = dve(lambda e: e.tensor_copy(ident_b[:, :], ident), [const_in])
        clear_o = dve(lambda e: e.memset(bank(6), 0.0))
        bank_users[6] = [clear_o]
        normed = layer_norm(x0, x_norm, x_in)
        x_free = normed[-1]
        ones_v = pool(lambda e: e.memset(values[:, :, :, DH:DH + 1], 1.0))
        bq4 = dve(lambda e: e.tensor_scalar(bq, bq, DH ** -0.5, None, ALU.mult), [bq_in])
        split_done = [None] * NT
        work_free = [None, None]

        normedT, early_free = {}, []

        def turn_norm(t0):
            for k in range(KD):
                kb, ps, free = misc()
                for i in range(4):
                    last = pe(lambda e, i=i, k=k, ps=ps: e.transpose(
                        ps[:, i * P:(i + 1) * P], x_norm[:, t0 + i, k * P:(k + 1) * P], ident),
                        free + [normed[t0 + i], const_in])
                normedT[t0, k] = evacuate(x_normT[:, k, t0 * P:(t0 + 4) * P], ps, [last])
                bank_users[kb] = [normedT[t0, k]]

        def make_queries(t0):
            made, banks = [], []
            for t in (t0, t0 + 1):
                kb, ps, free = misc()
                banks.append((kb, ps))
                for k in range(KD):
                    last = pe(lambda e, t=t, k=k, ps=ps: e.matmul(
                        ps[:, 0:D], x_normT[:, k, t * P:(t + 1) * P], wq[:, k, :],
                        start=(k == 0), stop=(k == KD - 1)), free + [normedT[t // 4 * 4, k], wq_in])
                made.append(last)
            q, r = (lambda w: q_work[:, 2 * w, :]), (lambda w: q_work[:, 2 * w + 1, :])
            part = lambda w, n: q_parts[:, t0 + w, n, :]
            s0 = [dve(lambda e, w=w: e.scalar_tensor_tensor(out=q(w), in0=banks[w][1][:, 0:D], scalar=DH ** -0.5,
                                                            in1=bq, op0=ALU.mult, op1=ALU.add),
                      [made[w], bq4, work_free[w]]) for w in range(2)]
            s1 = [act(lambda e, w=w: e.activation(part(w, 0), q(w), ACT.Copy), [s0[w]]) for w in range(2)]
            s2 = [dve(lambda e, w=w: e.tensor_tensor(r(w), q(w), part(w, 0), ALU.subtract), [s1[w]])
                  for w in range(2)]
            s3 = [act(lambda e, w=w: e.activation(part(w, 1), r(w), ACT.Copy), [s2[w]]) for w in range(2)]
            for w in range(2):
                bank_users[banks[w][0]] = [s0[w]]
                s4 = dve(lambda e, w=w: e.tensor_tensor(part(w, 2), r(w), part(w, 1), ALU.subtract), [s3[w]])
                work_free[w] = split_done[t0 + w] = s4
            if t0 == NT - 2:
                early_free.extend([made[1], s4])

        def misc():
            choice = [7, 0, 1, 2, 3] if now[0] < -1 else [7]
            misc_turn[0] += 1
            k = choice[misc_turn[0] % len(choice)]
            return k, bank(k), bank_users[k]

        now, misc_turn = [-1000], [0]

        jobs = {}

        def at(slot, job):
            jobs.setdefault(slot, []).append(job)

        ctx_turned, ctx_read = {}, {}
        parts_ready, parts_free = {}, {}
        chunk_done = {}
        rows_ready, rows_free, qT_ready, qT_done = {}, {}, {}, {}
        keys_ready, keys_free = {}, {}
        shifts_ready = {}
        values_ready, values_free = {}, {}
        later = []
        key_work = [[(x[:, 2 * w:2 * w + 2, :].rearrange("p t d -> p (t d)"),
                      key_f[:, w, :] if w < 2 else ctx_in[:, w - 2, :, :].rearrange("p t c -> p (t c)"))
                     for w in range(4)],
                    [(key_f[:, w, :], key_r[:, :]) for w in range(2)]]
        key_work_free = [[] for _ in range(4)]
        recip_read = [[]]
        ctx_users = [[x_free]]

        def load_ctx(b, c):
            n = b * CH + c
            ctx_loaded[b, c] = dma(ctx_in[:, n % 2, :, :],
                                   io["ctx_512"][b, c * BANK:(c + 1) * BANK, :].rearrange("(t p) c -> p t c", p=P),
                                   f"in_ctx{n % 2}", ctx_read.get(n - 2, []))

        def turn_ctx(b, c):
            n = b * CH + c
            source = ctx_in[:, n % 2, :, :] if b else ctx_first[:, c, :, :]
            kb, ps, free = misc()
            for i in range(4):
                last = pe(lambda e, i=i: e.transpose(ps[:, i * P:(i + 1) * P], source[:, i, :], ident),
                          free + [ctx_loaded[b, c], const_in])
            if b:
                ctx_read[n] = [last]
            else:
                parts_free[-1] = [last]
            ctx_turned[b, c] = act(lambda e: e.activation(ctxT[:, c * BANK:(c + 1) * BANK], ps, ACT.Copy),
                                   [last] + (ctx_users[0] if b or c >= CH - NT * D // BANK else []))
            bank_users[kb] = [ctx_turned[b, c]]

        def fill_keys(u, c):
            b, m = divmod(u, KD)
            kb, ps, free_bank = misc()
            made = pe(lambda e: e.matmul(ps, wk[:, 0, m * P:(m + 1) * P], ctxT[:, c * BANK:(c + 1) * BANK],
                                         start=True, stop=True), free_bank + [ctx_turned[b, c], wk_in])
            n = c % len(key_work[u > 0])
            k, r = key_work[u > 0][n]
            part = lambda i: key_parts[:, u % 2, i, c * BANK:(c + 1) * BANK]
            free = parts_free.get(u - 2, []) + key_work_free[n]
            s0 = act(lambda e: e.activation(k, ps, ACT.Identity, bias=bk[:, m:m + 1]), [made, bk_in] + free)
            bank_users[kb] = [s0]
            if u == 0:
                s1 = act(lambda e: e.activation(part(0), ps, ACT.Identity, bias=bk[:, m:m + 1]), [made])
                bank_users[kb] = [s1]
                split = pool if c in (1, 4) else dve
            else:
                s1 = pool(lambda e: e.tensor_copy(part(0), k), [s0])
                split = pool

            def rest():
                s2 = split(lambda e: e.tensor_tensor(r, k, part(0), ALU.subtract), [s0, s1])
                s3 = split(lambda e: e.tensor_copy(part(1), r), [s2])
                s4 = split(lambda e: e.tensor_tensor(part(2), r, part(1), ALU.subtract), [s3])
                key_work_free[n] = [s4]
                chunk_done[u, c] = s4
                if u == 0 and c == CH - 1:
                    for w in range(2):
                        key_work_free[w] = ctx_read[CH - 2 + w] = [chunk_done[0, other] for other in range(CH)]
                    recip_read[0] = [chunk_done[0, other] for other in range(CH)]
            if u == 0:
                later.append(rest)
                if c:
                    later.pop(0)()
            else:
                rest()
            if m == KD - 1 and c == CH - 1:
                last_k_read[b] = made

        last_k_read = {}

        def lay_query_rows(u):
            b, m = divmod(u, KD)
            at_block = 0
            for part, times in ((0, 3), (1, 2), (2, 1)):
                for t in range(QT):
                    src = q_parts[:, QT * b + t, part, m * P:(m + 1) * P].rearrange("p (h d) -> p h d", d=DH)
                    for i in range(times):
                        dst = q_rows[:, t, :, (at_block + i) * DH:(at_block + i + 1) * DH]
                        last = pool(lambda e, dst=dst, src=src: e.tensor_copy(dst, src),
                                    [split_done[QT * b + t]] + rows_free.get(u - 1, []))
                at_block += times
            rows_ready[u] = last

        def turn_queries(i):
            u, g = divmod(i, UNIT_GROUPS)
            kb, ps, free = misc()
            out_b = ps.bitcast(BF16)
            for j in range(GH):
                for t in range(QT):
                    k = j * QT + t
                    last = pe(lambda e, k=k, j=j, t=t: e.transpose(
                        out_b[0:ROWS, k * P:(k + 1) * P], q_rows[:, t, g * GH + j, :], ident_b[:, :]),
                        free + [rows_ready[u], ident_b_made])
            rows_free[u] = [last]
            qT_ready[i] = dve(lambda e: e.tensor_copy(
                queriesT[0:ROWS, i % 4, :, :].rearrange("p h n -> p (h n)"), out_b[0:ROWS, 0:GH * S]),
                [last] + qT_done.get(i - 4, []))
            bank_users[kb] = [qT_ready[i]]

        def load_keys(i, chunks=range(CH)):
            keys = slice(chunks[0] * BANK, (chunks[-1] + 1) * BANK)
            u, g = divmod(i, UNIT_GROUPS)
            ring = i % RING
            for j in range(GH):
                src0 = (g * GH + j) * DH
                for block, part in enumerate((0, 1, 2, 0, 1, 0)):
                    last = dma(keysT[block * DH:(block + 1) * DH, ring, j, keys],
                               key_parts[src0:src0 + DH, u % 2, part, keys], f"keys{ring}",
                               [chunk_done[u, c] for c in chunks] + keys_free.get(i - RING, []) + (early_free if ring == 2 else []))
            keys_ready[i] = last
            parts_free[u] = parts_free.get(u, []) + [last]

        def make_values(b, p):
            kb, ps, free = misc()
            for e2 in range(2):
                kt = 2 * p + e2
                made = pe(lambda e, kt=kt, e2=e2: e.matmul(ps[:, e2 * D:(e2 + 1) * D],
                                                           ctxT[:, kt * P:(kt + 1) * P], wv[:, 0, :],
                                                           start=True, stop=True),
                          free + [ctx_turned[b, kt * P // BANK], wv_in])
            values_ready[b, p] = act(lambda e: e.activation(
                values[:, 2 * p:2 * p + 2, :, 0:DH],
                ps.rearrange("p (k h d) -> p k h d", k=2, h=H), ACT.Copy),
                [made] + values_free.get((b - 1, p), []))
            bank_users[kb] = [values_ready[b, p]]
            last_v_read[b] = made

        last_v_read = {}

        max_free = [None, None]
        peak_read = {}

        def max_step(n):
            i, r = divmod(n, GH * QT * CH)
            if i >= GROUPS:
                return
            pair, c = divmod(r, CH)
            j, t = divmod(pair, QT)
            k = 4 + n % 2
            made = pe(lambda e: e.matmul(bank(k), queriesT[0:ROWS, i % 4, j, t * P:(t + 1) * P],
                                         keysT[0:ROWS, i % RING, j, c * BANK:(c + 1) * BANK], start=True, stop=True),
                      [max_free[n % 2], qT_ready[i], keys_ready[i]] + (bank_users[k] if n < 2 else []))
            max_free[n % 2] = dve(lambda e: e.tensor_reduce(peaks[:, i % 2, pair, c:c + 1], bank(k), AX.X, ALU.max),
                                  [made] + peak_read.get(i - 2, []))
            if r == GH * QT * CH - 1:
                negative, high, rest = (shift[:, i % 2, w, :] for w in range(3))
                s0 = dve(lambda e: e.tensor_reduce(negative, peaks[:, i % 2, :, :], AX.X, ALU.max, negate=True),
                         [max_free[n % 2]])
                peak_read[i] = [s0]
                s1 = dve(lambda e: e.tensor_copy(shift_b[:, i % 2, :, 0], negative), [s0, shift_turned.get(i - 2)])
                s2 = dve(lambda e: e.tensor_tensor(shift_b[:, i % 2, :, 1], negative, shift_b[:, i % 2, :, 0],
                                                   ALU.subtract), [s1])
                shifts_ready[i] = s2

        shift_turned = {}

        def turn_shift(i):
            kb, ps, free = misc()
            out_b = ps.bitcast(BF16)
            for pair in range(GH * QT):
                last = pe(lambda e, pair=pair: e.transpose(out_b[ROWS:AUG, pair * P:(pair + 1) * P],
                                                           shift_b[:, i % 2, pair, :], ident_b[:, :]),
                          free + [shifts_ready[i]])
            shift_turned[i] = last
            qT_ready[i, "shift"] = dve(lambda e: e.tensor_copy(
                queriesT[ROWS:AUG, i % 4, :, :].rearrange("p h n -> p (h n)"), out_b[ROWS:AUG, 0:GH * S]), [last])
            bank_users[kb] = [qT_ready[i, "shift"]]

        score_free, probs_free, probs_ready = {}, {}, {}
        outT_ready, outT_read = {}, {}
        ones_steps = []

        def add_ones(ring):
            ones_steps.append(pool(lambda e: e.memset(keysT[ROWS:AUG, ring, :, :], 1.0),
                                   early_free if ring == 2 else []))


        def score_step(t):
            i, p = divmod(t, SLOTS)
            base = (t % 2) * 2 * BANK
            for e2 in range(2):
                for j in range(GH):
                    kt = 2 * p + e2
                    last = pe(lambda e, j=j, kt=kt, o=base + (e2 * GH + j) * S: e.matmul(
                        psum[:, o:o + S], keysT[0:AUG, i % RING, j, kt * P:(kt + 1) * P],
                        queriesT[0:AUG, i % 4, j, :], start=True, stop=True),
                        [score_free.get(t - 2), qT_ready[i, "shift"], keys_ready[i], ones_steps[i % RING]]
                        + (bank_users[2 * t] + bank_users[2 * t + 1] if t < 2 else []))
            probs_ready[t] = act(lambda e: e.activation(probs[:, t % 2, :], psum[:, base:base + 2 * BANK], ACT.Exp),
                                 [last, probs_free.get(t - 2)] + (work_free if t < 2 else []))
            score_free[t] = probs_ready[t]
            if p == SLOTS - 1:
                keys_free[i] = [last]
                qT_done[i] = [last]

        def value_step(t):
            i, p = divmod(t, SLOTS)
            b, g = divmod(i, NG)
            for e2 in range(2):
                for j in range(GH):
                    quad, kt = e2 * GH + j, 2 * p + e2
                    last = pe(lambda e, quad=quad, kt=kt, j=j: e.matmul(
                        bank(6)[32 * quad:32 * quad + DH + 1, 0:S], values[:, kt, g * GH + j, :],
                        probs[:, t % 2, quad * S:(quad + 1) * S], start=(p == 0), stop=(p == SLOTS - 1)),
                        [probs_ready[t], values_ready[b, p], ones_v, outT_ready.get(i - 1), clear_o])
            probs_free[t] = last
            if g == NG - 1:
                values_free[b, p] = [last]
            return last

        def finish_group(i, last):
            outT_ready[i] = act(lambda e: e.activation(outT[:, :], bank(6)[:, 0:S], ACT.Copy),
                                [last, outT_read.get(i - 1)])

        def normalize_group(i):
            b, g = divmod(i, NG)
            W = GH * (DH + 1)
            kb, ps, free = misc()
            for t in range(QT):
                last = pe(lambda e, t=t: e.matmul(ps[:, t * 64:t * 64 + W], outT[:, t * P:(t + 1) * P],
                                                  constant("gather"), start=True, stop=True),
                          free + [outT_ready[i], const_in])
            outT_read[i] = last
            both = ps[:, 0:QT * 64].rearrange("p (t w) -> p t w", t=QT)[:, :, 0:W].rearrange(
                "p t (h d) -> p t h d", h=GH)
            s0 = dve(lambda e: e.reciprocal(recip[:, :, :], both[:, :, :, DH]), [last] + recip_read[0])
            for t in range(QT):
                scaled = dve(lambda e, t=t: e.tensor_tensor(
                    heads_out[:, QT * b + t, g * GH * DH:(g + 1) * GH * DH].rearrange("p (h d) -> p h d", h=GH),
                    both[:, t, :, 0:DH], recip[:, t, :].unsqueeze(2).to_broadcast([P, GH, DH]), ALU.mult), [s0])
            recip_read[0] = bank_users[kb] = [scaled]
            group_out[i] = scaled

        group_out = {}

        UNIT = UNIT_GROUPS * SLOTS
        for u in range(B * KD):
            b, m = divmod(u, KD)
            for c in range(CH):
                slot = UNIT * u - 101 + 8 * c
                if m == 0:
                    if b:
                        at(slot - 8, lambda b=b, c=c: load_ctx(b, c))

                    def turn(b=b, c=c):
                        if b and c == 0:
                            ctx_users[0] = [last_k_read[b - 1], last_v_read[b - 1]]
                        turn_ctx(b, c)
                    at(slot, turn)
                    at(slot + (2 if b else 9 if c < CH - 1 else 7), lambda u=u, c=c: fill_keys(u, c))
                else:
                    at(slot, lambda u=u, c=c: fill_keys(u, c))
            at(UNIT * u - SLOTS * 2 - 6, lambda u=u: lay_query_rows(u))
        first = -101
        for slot, job, t in ((first + 12, turn_norm, 0), (first + 13, make_queries, 0), (first + 20, turn_norm, 4),
                             (first + 28, make_queries, 2), (first + 36, make_queries, 4),
                             (first + 44, make_queries, 6)):
            at(slot, lambda job=job, t=t: job(t))
        for ring in range(RING):
            at((-37, -10, 2)[ring], lambda ring=ring: add_ones(ring))
        at(-60, lambda: load_keys(0, range(CH // 2)))
        at(-38, lambda: later.pop(0)())

        def load_output_weights():
            return (dma(wo_sb[:, :, :], io["L0_xattn_Wo"].rearrange("(k p) n -> p k n", p=P), "in_wo"),
                    dma(bv_sb[:, :], io["L0_xattn_bv"].partition_broadcast(P), "in_bv"),
                    dma(bo_sb[:, :], io["L0_xattn_bo"].partition_broadcast(P), "in_bo"))
        late = []
        at(4, lambda: late.extend(load_output_weights()))
        for i in range(GROUPS):
            at(SLOTS * i - (32 if i else 38), lambda i=i: load_keys(i, range(0 if i else CH // 2, CH)))
            at(SLOTS * i - 24, lambda i=i: turn_queries(i))
            at(SLOTS * i - 2, lambda i=i: turn_shift(i))
            at(SLOTS * i + SLOTS + 1, lambda i=i: normalize_group(i))
        for b in range(B):
            for p in range(SLOTS):
                at(SLOTS * NG * b - SLOTS + p + 1, lambda b=b, p=p: make_values(b, p))
        LEAD = 18
        total = GROUPS * SLOTS
        for t in range(min(jobs), total + 2 + 1):
            if 0 <= t and t % (SLOTS * NG) == 0:
                pr.stage = f"xattn0_b{t // (SLOTS * NG)}"
            if 0 <= t < total:
                score_step(t)
            if t + LEAD >= 0:
                max_step(2 * (t + LEAD))
            if 1 <= t <= total:
                last = value_step(t - 1)
                if t % SLOTS == 0:
                    finish_group(t // SLOTS - 1, last)
            if t + LEAD >= 0:
                max_step(2 * (t + LEAD) + 1)
            now[0] = t
            for job in jobs.get(t, []):
                job()

        (wo, bv, bo), (wo_in, bv_in, bo_in) = (wo_sb, bv_sb, bo_sb), late
        pr.stage = "xattn0_out"
        bank_users[6] = [outT_ready[GROUPS - 1]]
        bank_users[4] = bank_users[5] = [max_free[0], max_free[1]]
        for k in range(4):
            bank_users[k] = [probs_ready[total - 1], probs_ready[total - 2]]
        pr.barrier()
        one.close()

        xn = sb(ctx, "xn", [P, NT, D])
        xnT = sb(ctx, "xnT", [P, KD, B * S])
        const_tiles[1] = sb(ctx, "const2", [P, io["const2"].shape[1]])
        x_old = sb(ctx, "x_old", [P, NT, D])
        x_old_in = dma(x_old[:, :, :], x_tiles, "in_x")
        const2_in = dma(const_tiles[1][:, :], io["const2"], "in_const2")
        wl, wl_in = weight(ctx, "w_qkv", io["L0_attn_W_qkv"], KD)
        wlo, wlo_in = weight(ctx, "w_out", io["L0_attn_W_out"], KD)
        blo, blo_in = bias_rows(ctx, "b_out", io["L0_attn_b_out"])
        w3_q, w3_q_in = weight(ctx, "w3_q", io["L0_ffn_Wq"], KD)
        w3_k, w3_k_in = weight(ctx, "w3_k", io["L0_ffn_Wk"], KD)
        w3_v, w3_v_in = weight(ctx, "w3_v", io["L0_ffn_Wv"], KD)
        w3_ff, w3_ff_in = weight(ctx, "w3_ff", io["L0_ffn_Wff"], KD)
        QUADS, HG = 4, H // 4
        w3_o = sb(ctx, "w3_o", [P, HG, D])
        w3_o_zero = pool(lambda e: e.memset(w3_o[:, :, :], 0.0))
        for j in range(QUADS):
            w3_o_in = dma(w3_o[32 * j:32 * j + DH, :, :],
                          io["L0_ffn_Wo"].rearrange("(g j d) n -> j d g n", j=QUADS, d=DH)[j], "in_w3_o", [w3_o_zero])
        w4_q, w4_q_in = weight(ctx, "w4_q", io["L1_xattn_Wq"], KD)
        w4_k, w4_k_in = weight(ctx, "w4_k", io["L1_xattn_Wk"], 1)
        w4_v, w4_v_in = weight(ctx, "w4_v", io["L1_xattn_Wv"], 1)
        b4_q, b4_q_in = bias_columns(ctx, "b4_q", io["L1_xattn_bq"])
        b4_k, b4_k_in = bias_columns(ctx, "b4_k", io["L1_xattn_bk"])
        b4_v, b4_v_in = bias_rows(ctx, "b4_v", io["L1_xattn_bv"])
        KT = LC // P
        ctx_nat = [sb(ctx, "ctx_nat0", [P, KT, C]), None]
        ctx_T = sb(ctx, "ctx_T", [P, 2, LC])
        ctx_here, ctxT_here, nat_users, T_users = {}, {}, {}, {}

        def fetch_ctx(b, chunks=range(CH)):
            for c in chunks:
                ctx_here[b, c] = dma(ctx_nat[b % 2][:, 4 * c:4 * c + 4, :],
                                     io["ctx_512"][b, c * BANK:(c + 1) * BANK, :].rearrange("(t p) c -> p t c", p=P),
                                     f"in_nat{b % 2}_{c}", nat_users.get((b - 2, c), []))

        def turn_nat(b, c):
            n, ps, free = next_bank()
            nat = ctx_nat[b % 2]
            for i in range(4):
                last = pe(lambda e, i=i, ps=ps: e.transpose(ps[:, i * P:(i + 1) * P], nat[:, 4 * c + i, :], ident),
                          free + [ctx_here[b, c]])
            ctxT_here[b, c] = evacuate(ctx_T[:, b % 2, c * BANK:(c + 1) * BANK], ps, [last] + T_users.get(b - 2, []))
            bank_users[n] = [ctxT_here[b, c]]

        fetch_ctx(0)

        biased = [dve(lambda e, t=t: e.tensor_tensor(xn[:, t, :], heads_out[:, t, :], bv[:, :], ALU.add),
                      [bv_in, group_out[GROUPS - 1]]) for t in range(NT)]
        outT_done = transpose_tokens(xn, xnT, biased)
        x_bias = [pool(lambda e, t=t: e.tensor_tensor(x_old[:, t, :], x_old[:, t, :], bo[:, :], ALU.add),
                       [x_old_in, bo_in]) for t in range(NT)]
        x_ready = [None] * NT

        def add_to_stream(t, ps, made):
            x_ready[t] = dve(lambda e: e.tensor_tensor(x[:, t, :], ps, x_old[:, t, :], ALU.add), [made, x_bias[t], biased[t]])
            return [x_ready[t]]

        project_tokens(xnT, outT_done, wo, wo_in, add_to_stream)
        def norm_and_turn(ready):
            normed = layer_norm(x, xn, ready)
            return normed, transpose_tokens(xn, xnT, normed)

        def keep_T(dst, done):
            def use(m, half, ps, made):
                done[m, half] = evacuate(dst[:, m, half * BANK:(half + 1) * BANK], ps, [made])
                return [done[m, half]]
            return use

        def keep_tokens(dst, done):
            def use(t, ps, made):
                done[t] = evacuate(dst[:, t, :], ps, [made])
                return [done[t]]
            return use

        def isolate_heads(srcT, heads, b, m, ready, users, heads_ready, scale):
            n = (b * KD + m) % 2
            for h in range(P // DH):
                engine = dve if h % 2 else pool
                step = engine(lambda e, h=h: e.tensor_scalar(heads[:, n, h, :], srcT[:, m, b * S:(b + 1) * S],
                                                             constant("head_col")[:, h:h + 1], scale,
                                                             ALU.mult, ALU.mult),
                              [ready[m, b * S // BANK], const2_in] + users.get((n, h), []))
                heads_ready[n, h] = step

        def add_bias_to_stream(bias, bias_in):
            before = list(x_ready)
            return [pool(lambda e, t=t: e.tensor_tensor(x[:, t, :], x[:, t, :], bias[:, :], ALU.add),
                         [before[t], bias_in, pr.last_norm]) for t in range(NT)]

        def accumulate(plus=None):
            def use(t, ps, made):
                x_ready[t] = dve(lambda e: e.tensor_tensor(x[:, t, :], ps, x[:, t, :], ALU.add),
                                 [made, plus[t] if plus else None])
                return [x_ready[t]]
            return use

        late = {}
        xT_next = []
        xT_next[:] = norm_and_turn(x_ready)[1]

        def linear_attention():
            pr.stage = "attn0"
            two = ExitStack()
            k_feat = sb(two, "k_feat", [P, NT, D])
            v_aug = sb(two, "v_aug", [P, NT, KD, P + 1])
            q_featT = sb(two, "q_featT", [P, KD, B * S])
            NKV = P + P // DH
            kv = sb(two, "kv", [P, B, KD, NKV])
            lin_out = sb(two, "lin_out", [P, NT, D])
            lin_outT = sb(two, "lin_outT", [P, KD, B * S])
            low_part = sb(two, "low_part", [P, 4, BANK])
            den = sb(two, "den", [P, 2, KD, P // DH])
            xT_done = list(xT_next)
            ones_set = pool(lambda e: e.memset(v_aug[:, :, :, P:P + 1], 1.0))
            low_free = [None] * 4
            low_turn = [0]

            def elu_plus_one(dst, ps, made):
                n = low_turn[0] % 4
                low_turn[0] += 1
                low = low_part[:, n, 0:ps.shape[1]]
                s0 = dve(lambda e: e.tensor_scalar(low, ps, 0.0, None, ALU.min), [made, low_free[n]])
                s1 = act(lambda e: e.activation(low, low, ACT.Exp), [s0])
                low_free[n] = dve(lambda e: e.scalar_tensor_tensor(out=dst, in0=ps, scalar=0.0, in1=low,
                                                                   op0=ALU.max, op1=ALU.add), [s1])
                return low_free[n]

            k_done, v_done = {}, {}

            def keep_kv(t, ps, made):
                v_done[t] = act(lambda e: e.activation(v_aug[:, t, :, 0:P],
                                                       ps[:, D:2 * D].rearrange("p (m n) -> p m n", m=KD), ACT.Copy), [made])
                k_done[t] = elu_plus_one(k_feat[:, t, :], ps[:, 0:D], v_done[t])
                return [k_done[t], v_done[t]]

            project_tokens(xnT, xT_done, wl, wl_in, keep_kv, cols=slice(D, 3 * D))
            q_done = {}

            def keep_q(m, half, ps, made):
                q_done[m, half] = elu_plus_one(q_featT[:, m, half * BANK:(half + 1) * BANK], ps, made)
                return [q_done[m, half]]

            project_T(xnT, xT_done, wl, wl_in, keep_q)
            kv_done = {}
            for b in range(B):
                for m in range(KD):
                    n, ps, free = next_bank()
                    for i in range(QT):
                        t = QT * b + i
                        last = pe(lambda e, t=t, m=m, i=i, ps=ps: e.matmul(
                            ps[:, 0:P + 1], k_feat[:, t, m * P:(m + 1) * P], v_aug[:, t, m, :],
                            start=(i == 0), stop=(i == QT - 1)), free + [k_done[t], v_done[t], ones_set])
                    s0 = dve(lambda e, b=b, m=m, ps=ps: e.tensor_tensor(kv[:, b, m, 0:P], ps[:, 0:P],
                                                                        constant("head_block"), ALU.mult), [last, const2_in])
                    s1 = dve(lambda e, b=b, m=m, ps=ps: e.tensor_tensor(
                        kv[:, b, m, P:NKV], ps[:, P:P + 1].to_broadcast([P, P // DH]), constant("head_col"), ALU.mult), [last])
                    bank_users[n] = [s1]
                    kv_done[b, m] = s1
            lin_done = []
            for t in range(NT):
                n, ps, free = next_bank()
                b = t // QT
                for m in range(KD):
                    last = pe(lambda e, t=t, m=m, b=b, ps=ps: e.matmul(
                        ps[:, m * NKV:(m + 1) * NKV], q_featT[:, m, t * P:(t + 1) * P], kv[:, b, m, :],
                        start=True, stop=True), free + [q_done[m, t * P // BANK], kv_done[b, m]])
                both = ps[:, 0:KD * NKV].rearrange("p (m n) -> p m n", m=KD)
                dn = den[:, t % 2, :, :]
                s0 = dve(lambda e, both=both, dn=dn: e.tensor_scalar(dn, both[:, :, P:NKV], 1e-6, None, ALU.add),
                         [last] + lin_done[-2:-1])
                s1 = dve(lambda e, dn=dn: e.reciprocal(dn, dn), [s0])
                for m in range(KD):
                    s2 = dve(lambda e, t=t, m=m, both=both, dn=dn: e.tensor_tensor(
                        lin_out[:, t, m * P:(m + 1) * P].rearrange("p (h d) -> p h d", d=DH),
                        both[:, m, 0:P].rearrange("p (h d) -> p h d", d=DH),
                        dn[:, m, :].unsqueeze(2).to_broadcast([P, P // DH, DH]), ALU.mult), [s1])
                lin_done.append(s2)
                bank_users[n] = [s2]
            linT_done = transpose_tokens(lin_out, lin_outT, lin_done)

            biased = add_bias_to_stream(blo, blo_in)
            project_tokens(lin_outT, linT_done, wlo, wlo_in, accumulate(biased))
            xT_next[:] = norm_and_turn(x_ready)[1]
            pr.barrier()
            two.close()

        linear_attention()

        def query_softmax_attention():
            pr.stage = "ffn0"
            three = ExitStack()
            qT = sb(three, "qT", [P, KD, B * S])
            kT = sb(three, "kT", [P, KD, B * S])
            kT_heads = sb(three, "kT_heads", [P, 2, P // DH, S])
            v_tok = sb(three, "v_tok", [P, NT, D])
            NR = 8
            weights3 = sb(three, "weights3", [P, NR, QT, S])
            v_scaled = sb(three, "v_scaled", [P, 2, QT, QUADS, 32])
            peaks3 = sb(three, "peaks3", [P, 2, QUADS, QT])
            sums3 = sb(three, "sums3", [P, 2, QT, QUADS])
            outT3 = sb(three, "outT3", [P, HG, B * S])
            norm3 = sb(three, "norm3", [P, 2, 3, NT])
            xT_done = list(xT_next)
            v_zero = pool(lambda e: e.memset(v_scaled[:, :, :, :, :], 0.0))

            qd, kd, vd = {}, {}, {}
            project_T(xnT, xT_done, w3_k, w3_k_in, keep_T(kT, kd))
            project_T(xnT, xT_done, w3_q, w3_q_in, keep_T(qT, qd))
            project_tokens(xnT, xT_done, w3_v, w3_v_in, keep_tokens(v_tok, vd))
            heads_ready, heads_users, ring_free = {}, {}, {}
            SC3 = 1.0 / D ** 0.5
            pending = []
            outT3_done = {}
            quad_bank = {}

            def scores3(b, m, h):
                hn = (b * KD + m) * (P // DH) + h
                r, w, j = hn % NR, hn // QUADS % 2, hn % QUADS
                n, ps, free = next_bank()
                hb = (b * KD + m) % 2
                for kt in range(QT):
                    last = pe(lambda e, kt=kt, ps=ps: e.matmul(
                        ps[:, kt * S:(kt + 1) * S], kT_heads[:, hb, h, kt * P:(kt + 1) * P],
                        qT[:, m, b * S:(b + 1) * S], start=True, stop=True),
                        free + [heads_ready[hb, h], qd[m, b * S // BANK]])
                heads_users[hb, h] = [last]
                peak = peaks3[:, w, j, :]
                s0 = dve(lambda e: e.tensor_reduce(peak, ps.rearrange("p (k q) -> p k q", k=QT), AX.X, ALU.max, negate=True),
                         [last] + ring_free.get(r, []))
                for kt in range(QT):
                    s2 = act(lambda e, kt=kt: e.activation(weights3[:, r, kt, :], ps[:, kt * S:(kt + 1) * S], ACT.Exp,
                                                           bias=peak[:, kt:kt + 1], accum_out=sums3[:, w, kt, j:j + 1]),
                             [s0] + sums_free.get(w, []))
                bank_users[n] = [s2]
                return s2

            def values3(b, g, exps):
                w = (b * HG + g) % 2
                s0 = dve(lambda e: e.reciprocal(sums3[:, w, :, :], sums3[:, w, :, :]), [exps[-1]])
                c0 = g * QUADS * DH
                for kt in range(QT):
                    s1 = dve(lambda e, kt=kt: e.tensor_tensor(
                        v_scaled[:, w, kt, :, 0:DH], v_tok[:, QT * b + kt, c0:c0 + QUADS * DH].rearrange("p (j d) -> p j d", d=DH),
                        sums3[:, w, kt, :].unsqueeze(2).to_broadcast([P, QUADS, DH]), ALU.mult),
                        [s0, v_zero, vd[QT * b + kt]] + v_users.get(w, []))
                sums_free[w] = [s1]
                n, ps, free = next_bank()
                for kt in range(QT):
                    for j in range(QUADS):
                        r = (b * H + QUADS * g + j) % NR
                        last = pe(lambda e, kt=kt, j=j, r=r, ps=ps: e.matmul(
                            ps[32 * j:32 * j + 32, 0:S], v_scaled[:, w, kt, j, :], weights3[:, r, kt, :],
                            start=(kt == 0), stop=(kt == QT - 1)), free + [s1, exps[j]])
                v_users[w] = [last]
                for j in range(QUADS):
                    ring_free[(b * H + QUADS * g + j) % NR] = [last]
                outT3_done[b, g] = dve(lambda e: e.tensor_copy(outT3[:, g, b * S:(b + 1) * S], ps[:, 0:S]), [last])
                bank_users[n] = [outT3_done[b, g]]

            sums_free, v_users = {}, {}
            isolate_heads(kT, kT_heads, 0, 0, kd, heads_users, heads_ready, SC3)
            for b in range(B):
                for m in range(KD):
                    following = b * KD + m + 1
                    if following < B * KD:
                        isolate_heads(kT, kT_heads, *divmod(following, KD), kd, heads_users, heads_ready, SC3)
                    for g in range(2):
                        exps = [scores3(b, m, QUADS * g + j) for j in range(QUADS)]
                        if pending:
                            values3(*pending.pop(0))
                        pending.append((b, 2 * m + g, exps))
                        if len(ctxT_here) < CH:
                            turn_nat(0, len(ctxT_here))
            values3(*pending.pop(0))

            def l2_normalize(which, actT, ready, w, w_in, blocks, dst):
                done = [None] * NT
                for t0 in range(0, NT, 4):
                    in_banks = {}

                    def keep(t, ps, made):
                        in_banks[t] = (ps, act(lambda e: e.activation(dst[:, t, :], ps, ACT.Square,
                                                                      accum_out=norm3[:, which, 0, t:t + 1]), [made]))
                        return [in_banks[t][1]]

                    taken = project_tokens(actT, ready, w, w_in, keep, blocks=blocks, tiles=range(t0, t0 + 4))
                    own = slice(t0, t0 + 4)
                    v = norm3[:, which, :, own]
                    s1 = pool(lambda e, v=v, own=own: e.tensor_tensor(v[:, 1, :], v[:, 0, :], constant("half")[:, own],
                                                                      ALU.pow), [in_banks[t0 + 3][1]])
                    s2 = dve(lambda e, v=v: e.tensor_scalar(v[:, 1, :], v[:, 1, :], 1e-12, None, ALU.max), [s1])
                    s3 = dve(lambda e, v=v: e.reciprocal(v[:, 2, :], v[:, 1, :]), [s2])
                    for t in range(t0, t0 + 4):
                        done[t] = dve(lambda e, t=t, ps=in_banks[t][0]: e.tensor_scalar(
                            dst[:, t, :], ps, norm3[:, which, 2, t:t + 1], None, ALU.mult), [s3])
                        bank_users[taken[t]] = [done[t]]
                return done

            oT_ready = [[outT3_done[t // QT, g] for g in range(HG)] for t in range(NT)]
            z_done = l2_normalize(0, outT3, oT_ready, w3_o, w3_o_in, HG, xn)
            zT_done = transpose_tokens(xn, xnT, z_done)
            z2_done = l2_normalize(1, xnT, zT_done, w3_ff, w3_ff_in, KD, v_tok)
            for t in range(NT):
                s0 = act(lambda e, t=t: e.activation(v_tok[:, t, :], v_tok[:, t, :], ACT.Gelu), [z2_done[t], x_ready[t]])
                x_ready[t] = dve(lambda e, t=t: e.tensor_tensor(x[:, t, :], x[:, t, :], v_tok[:, t, :], ALU.add), [s0])
            xT_next[:] = norm_and_turn(x_ready)[1]
            pr.barrier()
            three.close()
            ctx_nat[1] = sb(ctx, "ctx_nat1", [P, KT, C])
            w5_rows = sb(ctx, "w5_rows", [P, 3, KD, D])
            w5 = [sb(ctx, f"w5_{n}", [P, KD, D]) for n in "qkv"]
            fetch_ctx(1)
            w5_in = [dma(w5_rows[:, n, :, :], io[f"L1_attn_w{name}"].rearrange("(k p) n -> p k n", p=P), f"in_w5_{name}")
                     for n, name in enumerate("qkv")]
            late.update(w5_rows=w5_rows, w5_in=w5_in, w5=w5, w5_done=[])

        query_softmax_attention()

        def context_attention():
            pr.stage = "xattn1"
            four = ExitStack()
            w_kT = sb(four, "w4_kT", [P, KD, C])
            q4T = sb(four, "q4T", [P, KD, B * S])
            qcT = sb(four, "qcT", [P, B * S])
            offset = sb(four, "offset", [P, NT])
            row_w = sb(four, "row_w", [P, 2, LC])
            col_w = sb(four, "col_w", [P, 4, BANK])
            peaks4 = sb(four, "peaks4", [P, 2, 8])
            stat4 = sb(four, "stat4", [P, NT, 6])
            sums4 = sb(four, "sums4", [P, 2, 2])
            ucT = sb(four, "ucT", [P, B * S])
            xT_done = list(xT_next)
            n, ps, free = next_bank()
            for k in range(KD):
                last = pe(lambda e, k=k, ps=ps: e.transpose(ps[:, k * C:(k + 1) * C], w4_k[:, 0, k * P:(k + 1) * P], ident),
                          free + [w4_k_in])
            w_kT_done = evacuate(w_kT[:, :, :].rearrange("p k c -> p (k c)"), ps[:, 0:KD * C], [last])
            bank_users[n] = [w_kT_done]
            q4_done = {}

            def keep_q4(m, half, ps, made):
                q4_done[m, half] = act(lambda e: e.activation(q4T[:, m, half * BANK:(half + 1) * BANK], ps, ACT.Identity,
                                                              bias=b4_q[:, m:m + 1]), [made, b4_q_in])
                return [q4_done[m, half]]

            project_T(xnT, xT_done, w4_q, w4_q_in, keep_q4)
            qc_done = {}
            for half in range(2):
                n, ps, free = next_bank()
                for k in range(KD):
                    last = pe(lambda e, k=k, half=half, ps=ps: e.matmul(ps, w_kT[:, k, :],
                                                                        q4T[:, k, half * BANK:(half + 1) * BANK],
                                                                        start=(k == 0), stop=(k == KD - 1)),
                              free + [w_kT_done, q4_done[k, half]])
                qc_done[half] = evacuate(qcT[:, half * BANK:(half + 1) * BANK], ps, [last])
                bank_users[n] = [qc_done[half]]
            n, ps, free = next_bank()
            for t in range(NT):
                for k in range(KD):
                    last = pe(lambda e, t=t, k=k, ps=ps: e.matmul(ps[:, t:t + 1], q4T[:, k, t * P:(t + 1) * P], b4_k[:, k:k + 1],
                                                                  start=(k == 0), stop=(k == KD - 1)),
                              free + [b4_k_in, q4_done[k, t * P // BANK]])
            offset_done = dve(lambda e, ps=ps: e.tensor_copy(offset[:, :], ps[:, 0:NT]), [last])
            bank_users[n] = [offset_done]

            w_rows, w_in, w5, w5_done = late["w5_rows"], late["w5_in"], late["w5"], late["w5_done"]
            for w in range(3):
                n, ps, free = next_bank()
                for k in range(KD):
                    for m in range(KD):
                        last = pe(lambda e, k=k, m=m, w=w, ps=ps: e.transpose(
                            ps[:, (k * KD + m) * P:(k * KD + m + 1) * P], w_rows[:, w, m, k * P:(k + 1) * P], ident),
                            free + [w_in[w]])
                w5_done.append(evacuate(w5[w][:, :, :].rearrange("p k n -> p (k n)"), ps, [last]))
                bank_users[n] = [w5_done[w]]
            row_free, col_free, uc_done = {}, {}, {}
            exp4 = {}

            def score_chunk(t, c):
                b, r = t // QT, t % 2
                n, ps, free = next_bank()
                here = slice(c * BANK, (c + 1) * BANK)
                made = pe(lambda e: e.matmul(ps, qcT[:, t * P:(t + 1) * P], ctx_T[:, b % 2, here], start=True, stop=True),
                          free + [qc_done[t * P // BANK], ctxT_here[b, c]])
                T_users[b] = [made]
                copied = act(lambda e: e.activation(row_w[:, r, here], ps, ACT.Copy), [made, row_free.get((r, c))])
                bank_users[n] = [copied]
                found = dve(lambda e: e.tensor_reduce(peaks4[:, r, c:c + 1], row_w[:, r, here], AX.X, ALU.max),
                            [copied, exp4.get(t - 2)])
                if c < CH - 1:
                    return
                w = stat4[:, t, :]
                s0 = dve(lambda e: e.tensor_reduce(w[:, 0:1], peaks4[:, r, :], AX.X, ALU.max), [found])
                s1 = dve(lambda e: e.tensor_tensor(w[:, 1:2], w[:, 0:1], offset[:, t:t + 1], ALU.add), [s0, offset_done])
                s2 = dve(lambda e: e.tensor_tensor(w[:, 2:3], offset[:, t:t + 1], w[:, 1:2], ALU.subtract), [s1])
                for half in range(2):
                    own = slice(half * LC // 2, (half + 1) * LC // 2)
                    exp4[t, half] = act(lambda e, half=half, own=own: e.activation(
                        row_w[:, r, own], row_w[:, r, own], ACT.Exp, bias=w[:, 2:3], accum_out=w[:, 3 + half:4 + half]), [s2])
                exp4[t] = exp4[t, 1]

            def turn_chunk(t, c):
                r, w = t % 2, (t * CH + c) % 4
                n, ps, free = next_bank()
                for i in range(4):
                    kt = 4 * c + i
                    last = pe(lambda e, i=i, kt=kt: e.transpose(ps[:, i * P:(i + 1) * P],
                                                                row_w[:, r, kt * P:(kt + 1) * P], ident),
                              free + [exp4[t, 2 * c // CH]])
                row_free[r, c] = last
                columns[t, c] = dve(lambda e: e.tensor_copy(col_w[:, w, :], ps), [last, col_free.get(w)])
                bank_users[n] = [columns[t, c]]

            def weigh_chunk(t, c):
                b, w = t // QT, (t * CH + c) % 4
                if c == 0:
                    acc_bank[t] = next_bank()
                    held.add(acc_bank[t][0])
                no, acc, free = acc_bank[t]
                for i in range(4):
                    kt = 4 * c + i
                    last = pe(lambda e, i=i, kt=kt: e.matmul(acc[:, 0:P], ctx_nat[b % 2][:, kt, :],
                                                             col_w[:, w, i * P:(i + 1) * P],
                                                             start=(kt == 0), stop=(kt == KT - 1)),
                              free + [columns[t, c], ctx_here[b, c]])
                col_free[w] = last
                nat_users[b, c] = [last]
                if c == CH - 1:
                    uc_done[t] = dve(lambda e: e.tensor_copy(ucT[:, t * P:(t + 1) * P], acc[:, 0:P]), [last])
                    bank_users[no] = [uc_done[t]]
                    held.discard(no)
                    w4 = stat4[:, t, :]
                    s3 = dve(lambda e: e.tensor_tensor(w4[:, 5:6], w4[:, 3:4], w4[:, 4:5], ALU.add), [exp4[t, 1]])
                    exp4[t, "inverse"] = dve(lambda e: e.reciprocal(w4[:, 5:6], w4[:, 5:6]), [s3])

            biased = [pool(lambda e, t=t: e.tensor_tensor(x[:, t, :], x[:, t, :], b4_v[:, :], ALU.add),
                           [x_ready[t], b4_v_in, pr.last_norm]) for t in range(NT)]
            columns, acc_bank = {}, {}
            AHEAD = CH + 3
            BATCH = QT * CH
            for s in range(-AHEAD, NT * CH + 2):
                if 0 <= s + AHEAD < NT * CH:
                    score_chunk(*divmod(s + AHEAD, CH))
                if 0 <= s < NT * CH:
                    turn_chunk(*divmod(s, CH))
                if 0 <= s - 2:
                    weigh_chunk(*divmod(s - 2, CH))
                for b in range(1, B):
                    if b >= 2 and 0 <= s - (BATCH * (b - 1) - 5) < CH:
                        fetch_ctx(b, [s - (BATCH * (b - 1) - 5)])
                    if 0 <= s - (BATCH * (b - 1) + 1 - 4 * (b == 1)) < CH:
                        turn_nat(b, s - (BATCH * (b - 1) + 1 - 4 * (b == 1)))
            for t in range(NT):
                n, ps, free = next_bank()
                last = pe(lambda e, t=t, ps=ps: e.matmul(ps[:, 0:D], ucT[:, t * P:(t + 1) * P], w4_v[:, 0, :],
                                                         start=True, stop=True), free + [uc_done[t], w4_v_in])
                x_ready[t] = dve(lambda e, t=t, ps=ps: e.scalar_tensor_tensor(
                    out=x[:, t, :], in0=ps[:, 0:D], scalar=stat4[:, t, 5:6], in1=x[:, t, :], op0=ALU.mult, op1=ALU.add),
                    [last, biased[t], exp4[t, "inverse"]])
                bank_users[n] = [x_ready[t]]
            xT_next[:] = norm_and_turn(x_ready)[1]
            pr.barrier()
            four.close()
            late["w6"] = {n: weight(ctx, f"w6_{n}", io[f"L1_ffn_W{n}"], KD) for n in "qkvog"}
            late["rows6"] = {n: bias_columns(ctx, f"r6_{n}", io[f"L1_ffn_{n}"]) for n in ("g1", "b1", "g2", "b2")}
            w1 = sb(ctx, "w6_1", [P, KD, NE, HID])
            for k in range(KD):
                w1_in = dma(w1[:, k, :, :], io["L1_ffn_W1"][:, k * P:(k + 1) * P, :].rearrange("e p h -> p e h"), "in_w6_1")
            w2 = sb(ctx, "w6_2", [P, NE, D])
            w2_in = dma(w2[:, :, :], io["L1_ffn_W2"].rearrange("e h n -> h e n"), "in_w6_2")
            late.update(w1=w1, w1_in=w1_in, w2=w2, w2_in=w2_in)

        context_attention()

        def causal_attention():
            pr.stage = "attn1"
            five = ExitStack()
            w5, w5_done = late["w5"], late["w5_done"]
            swapped = sb(five, "swapped", [P, 2, 2, D])
            qk = ctx_nat[0][:, :, :].rearrange("p (t w two) c -> p t w (two c)", w=2, two=2)
            rotated = ctx_T[:, 0, :].rearrange("p (t w d) -> p t w d", w=2, d=D)
            turned5 = ctx_T[:, 1, :].rearrange("p (w k n) -> p w k n", w=2, k=KD)
            v5 = sb(five, "v5", [P, NT, D])
            rows5 = sb(five, "rows5", [P, NT, S])
            cols5 = sb(five, "cols5", [P, NT, QT, P])
            stat5 = sb(five, "stat5", [P, NT, 4])
            xT_done = list(xT_next)
            qk_done, turned_done = [None] * NT, [None] * NT
            cos = constant("cos").rearrange("p (t d) -> p t d", t=QT)
            sin = constant("sin").rearrange("p (t d) -> p t d", t=QT)
            pair = lambda a, o: a.rearrange("p w (n two) -> p w n two", two=2)[:, :, :, o]
            wide = lambda a: a.unsqueeze(1).to_broadcast([P, 2, a.shape[1]])
            for t in range(NT):
                i = t % QT
                n, ps, free = next_bank()
                for w in range(2):
                    for k in range(KD):
                        last = pe(lambda e, t=t, w=w, k=k, ps=ps: e.matmul(
                            ps[:, w * D:(w + 1) * D], xnT[:, k, t * P:(t + 1) * P], w5[w][:, k, :],
                            start=(k == 0), stop=(k == KD - 1)), free + list(xT_done[t]) + [w5_done[w]])
                src, dst, other = qk[:, t, :, :], rotated[:, t, :, :], swapped[:, t % 2, :, :]
                qk_done[t] = act(lambda e, src=src, ps=ps: e.activation(
                    src, ps.rearrange("p (w d) -> p w d", w=2), ACT.Copy), [last])
                bank_users[n] = [qk_done[t]]
                s0 = dve(lambda e, src=src, dst=dst, i=i: e.tensor_tensor(dst, src, wide(cos[:, i, :]), ALU.mult),
                         [qk_done[t], const2_in])
                s1 = pool(lambda e, src=src, other=other, i=i: e.tensor_tensor(
                    pair(other, 0), pair(src, 1), wide(sin[:, i, 0::2]), ALU.mult),
                    [qk_done[t], const2_in] + ([turned_done[t - 2]] if t >= 2 else []))
                s2 = dve(lambda e, src=src, other=other, i=i: e.tensor_tensor(
                    pair(other, 1), pair(src, 0), wide(sin[:, i, 1::2]), ALU.mult), [qk_done[t], const2_in]
                    + ([turned_done[t - 2]] if t >= 2 else []))
                turned_done[t] = dve(lambda e, dst=dst, other=other: e.tensor_tensor(dst, dst, other, ALU.add), [s0, s1, s2])
            v5_done = {}
            project_tokens(xnT, xT_done, w5[2], w5_done[2], keep_tokens(v5, v5_done))
            tT = []
            for w in range(2):
                tT.append(transpose_tokens(rotated[:, :, w, :], turned5[:, w, :, :], turned_done))
            SC5 = 1.0 / D ** 0.5
            out5 = {}
            for t in range(NT):
                b, i = divmod(t, QT)
                width = (i + 1) * P
                n, ps, free = next_bank()
                for k in range(KD):
                    last = pe(lambda e, t=t, b=b, k=k, width=width, ps=ps: e.matmul(
                        ps[:, 0:width], turned5[:, 0, k, t * P:(t + 1) * P], turned5[:, 1, k, b * S:b * S + width],
                        start=(k == 0), stop=(k == KD - 1)),
                        free + tT[0][t] + [s for u in range(QT * b, QT * b + i + 1) for s in tT[1][u]])
                w = stat5[:, t, :]
                row = rows5[:, t, 0:width]
                steps = []
                if i:
                    steps.append(act(lambda e, row=row, ps=ps, i=i: e.activation(row[:, 0:i * P], ps[:, 0:i * P], ACT.Copy,
                                                                                 scale=SC5), [last]))
                steps.append(dve(lambda e, row=row, ps=ps, i=i: e.scalar_tensor_tensor(
                    out=row[:, i * P:(i + 1) * P], in0=ps[:, i * P:(i + 1) * P], scalar=SC5, in1=constant("causal"),
                    op0=ALU.mult, op1=ALU.add), [last] + steps))
                bank_users[n] = steps
                s0 = dve(lambda e, w=w, row=row: e.tensor_reduce(w[:, 0:1], row, AX.X, ALU.max, negate=True), steps)
                s1 = act(lambda e, w=w, row=row: e.activation(row, row, ACT.Exp, bias=w[:, 0:1], accum_out=w[:, 1:2]), [s0])
                s2 = dve(lambda e, w=w: e.reciprocal(w[:, 2:3], w[:, 1:2]), [s1])
                out5[t] = (s1, s2)
            for t in range(NT):
                b, i = divmod(t, QT)
                s1, s2 = out5[t]
                n, ps, free = next_bank()
                for kt in range(i + 1):
                    last = pe(lambda e, t=t, kt=kt, ps=ps: e.transpose(ps[:, kt * P:(kt + 1) * P],
                                                                       rows5[:, t, kt * P:(kt + 1) * P], ident), free + [s1])
                s3 = evacuate(cols5[:, t, 0:i + 1, :].rearrange("p k q -> p (k q)"), ps[:, 0:(i + 1) * P], [last])
                bank_users[n] = [s3]
                out5[t] = (s3, s2)
            for t in range(NT):
                b, i = divmod(t, QT)
                s3, s2 = out5[t]
                n, ps, free = next_bank()
                for kt in range(i + 1):
                    last = pe(lambda e, t=t, b=b, i=i, kt=kt, ps=ps: e.matmul(
                        ps[:, 0:D], cols5[:, t, kt, :], v5[:, QT * b + kt, :], start=(kt == 0), stop=(kt == i)),
                        free + [s3, v5_done[QT * b + kt]])
                x_ready[t] = dve(lambda e, t=t, ps=ps: e.scalar_tensor_tensor(
                    out=x[:, t, :], in0=ps[:, 0:D], scalar=stat5[:, t, 2:3], in1=x[:, t, :], op0=ALU.mult, op1=ALU.add),
                    [last, s2, pr.last_norm])
                bank_users[n] = [x_ready[t]]
            rows6 = late["rows6"]
            y_made = layer_norm(x, x_old, x_ready)
            normed = layer_norm(x_old, xn, y_made)
            xT_next[:] = transpose_tokens(xn, xnT, normed, affine=(rows6["g1"], rows6["b1"]))
            pr.barrier()
            five.close()

        causal_attention()

        def attention_and_experts():
            pr.stage = "ffn1"
            six = ExitStack()
            w6, w1, w1_in, w2, w2_in = (late[n] for n in ("w6", "w1", "w1_in", "w2", "w2_in"))
            y = x_old
            qT = ctx_T[:, 0, 0:KD * B * S].rearrange("p (k n) -> p k n", k=KD)
            kT = ctx_T[:, 0, KD * B * S:2 * KD * B * S].rearrange("p (k n) -> p k n", k=KD)
            hiddenT = ctx_T[:, 1, :].rearrange("p (x n) -> p x n", x=NE)
            q_heads = ctx_nat[0][:, :, :].rearrange("p (w h two) c -> p w h (two c)", w=2, two=2)
            NR6, NC6 = 4, 8
            rows_w = sb(six, "rows_w", [P, NR6, QT, S])
            cols_w = sb(six, "cols_w", [P, NC6, QT, S])
            peaks6 = sb(six, "peaks6", [P, B * H, QT])
            v_ones = ctx_nat[1][:, :, :].rearrange("p k c -> p (k c)").rearrange("p (t h f) -> p t h f", t=NT, h=H)
            outT6 = sb(six, "outT6", [P, 2, S])
            recip6 = sb(six, "recip6", [P, 2, QUADS])
            gates = sb(six, "gates", [P, NT, NE])
            top = sb(six, "top", [P, NT, NE])
            top_at = sb(six, "top_at", [P, NT, NE], U32)
            top_f = sb(six, "top_f", [P, NT, 2])
            pick = sb(six, "pick", [P, NT, 2, NE])
            prob = sb(six, "prob", [P, NT, 4])
            mix = sb(six, "mix", [P, NT, NE])
            xT_done = list(xT_next)

            qd, kd, vd = {}, {}, {}
            project_T(xnT, xT_done, *w6["q"], keep_T(qT, qd))
            project_T(xnT, xT_done, *w6["k"], keep_T(kT, kd))
            zeros6 = pool(lambda e: e.memset(v_ones[:, :, :, DH + 1:], 0.0))
            ones6 = pool(lambda e: e.memset(v_ones[:, :, :, DH:DH + 1], 1.0))

            def keep_v6(t, ps, made):
                vd[t] = evacuate(v_ones[:, t, :, 0:DH], ps.rearrange("p (h d) -> p h d", d=DH), [made])
                return [vd[t]]

            project_tokens(xnT, xT_done, *w6["v"], keep_v6)
            heads_ready, heads_users = {}, {}
            SC6 = DH ** -0.5
            rows_free, cols_free = {}, {}

            def scores6(b, m, h):
                hn = (b * KD + m) * (P // DH) + h
                r, hb = hn % NR6, (b * KD + m) % 2
                n, ps, free = next_bank()
                for i in range(QT):
                    last = pe(lambda e, i=i, ps=ps: e.matmul(ps[:, i * S:(i + 1) * S], q_heads[:, hb, h, i * P:(i + 1) * P],
                                                             kT[:, m, b * S:(b + 1) * S], start=True, stop=True),
                              free + [heads_ready[hb, h], kd[m, b * S // BANK]])
                heads_users[hb, h] = [last]
                peak = peaks6[:, hn, :]
                s0 = dve(lambda e: e.tensor_reduce(peak, ps.rearrange("p (k q) -> p k q", k=QT), AX.X, ALU.max, negate=True),
                         [last])
                for i in range(QT):
                    s2 = act(lambda e, i=i: e.activation(rows_w[:, r, i, :], ps[:, i * S:(i + 1) * S], ACT.Exp,
                                                         bias=peak[:, i:i + 1]), [s0] + rows_free.get(r, []))
                bank_users[n] = [s2]
                return s2

            def turn6(b, m, h, made):
                hn = (b * KD + m) * (P // DH) + h
                r = hn % NR6
                n, ps, free = next_bank()
                for kt in range(QT):
                    for i in range(QT):
                        last = pe(lambda e, kt=kt, i=i, ps=ps: e.transpose(
                            ps[:, kt * S + i * P:kt * S + (i + 1) * P], rows_w[:, r, i, kt * P:(kt + 1) * P], ident),
                            free + [made])
                rows_free[r] = [last]
                rc = hn % NC6
                s = evacuate(cols_w[:, rc, :, :].rearrange("p k q -> p (k q)"), ps, [last] + cols_free.get(rc, []))
                bank_users[n] = [s]
                return s

            def weigh6(b, g, ready):
                w = (b * HG + g) % 2
                n, ps, free = next_bank()
                for kt in range(QT):
                    for j in range(QUADS):
                        rc = (b * H + g * QUADS + j) % NC6
                        last = pe(lambda e, kt=kt, j=j, rc=rc: e.matmul(
                            ps[32 * j:32 * j + 32, 0:S], v_ones[:, QT * b + kt, g * QUADS + j, :],
                            cols_w[:, rc, kt, :], start=(kt == 0), stop=(kt == QT - 1)),
                            free + [ready[j], vd[QT * b + kt], ones6])
                for j in range(QUADS):
                    cols_free[(b * H + g * QUADS + j) % NC6] = [last]
                out6[b, g] = dve(lambda e: e.tensor_copy(outT6[:, w, :], ps[:, 0:S]), [last] + outT6_free.get(w, []))
                bank_users[n] = [out6[b, g]]

            def finish6(b, g):
                w, W = (b * HG + g) % 2, QUADS * (DH + 1)
                n, ps, free = next_bank()
                for i in range(QT):
                    last = pe(lambda e, i=i: e.matmul(ps[:, i * W:(i + 1) * W], outT6[:, w, i * P:(i + 1) * P],
                                                      constant("gather4"), start=True, stop=True),
                              free + [out6[b, g], const2_in])
                outT6_free[w] = [last]
                both = ps[:, 0:QT * W].rearrange("p (t h d) -> p t h d", t=QT, h=QUADS)
                s0 = dve(lambda e: e.reciprocal(recip6[:, :, :], both[:, :, :, DH]), [last] + o_done[-1:])
                for i in range(QT):
                    c0 = g * QUADS * DH
                    s1 = dve(lambda e, i=i: e.tensor_tensor(
                        xn[:, QT * b + i, c0:c0 + QUADS * DH].rearrange("p (h d) -> p h d", d=DH), both[:, i, :, 0:DH],
                        recip6[:, i, :].unsqueeze(2).to_broadcast([P, QUADS, DH]), ALU.mult), [s0])
                o_done.append(s1)
                bank_users[n] = [s1]

            out6, outT6_free, o_done = {}, {}, []
            made6, turned6, finish = [], [], []
            isolate_heads(qT, q_heads, 0, 0, qd, heads_users, heads_ready, SC6)
            LAG6 = 2
            for n6 in range(B * H + LAG6):
                if n6 < B * H:
                    unit, h = divmod(n6, P // DH)
                    if h == 1 and unit + 1 < B * KD:
                        isolate_heads(qT, q_heads, *divmod(unit + 1, KD), qd, heads_users, heads_ready, SC6)
                    made6.append(scores6(*divmod(unit, KD), h))
                if n6 >= LAG6:
                    hn = n6 - LAG6
                    unit, h = divmod(hn, P // DH)
                    turned6.append(turn6(*divmod(unit, KD), h, made6[hn]))
                    if hn % QUADS == 1 and hn > QUADS:
                        group = hn // QUADS - 1
                        weigh6(*divmod(group, HG), turned6[group * QUADS:(group + 1) * QUADS])
                    if hn % QUADS == 3 and hn > QUADS:
                        finish6(*divmod(hn // QUADS - 1, HG))
            weigh6(B - 1, HG - 1, turned6[-QUADS:])
            finish6(B - 1, HG - 1)
            o_done = [o_done[HG * (t // QT) + HG - 1] for t in range(NT)]
            oT_done = transpose_tokens(xn, xnT, o_done)
            y_ready = [None] * NT

            def add_to_y(t, ps, made):
                y_ready[t] = dve(lambda e: e.tensor_tensor(y[:, t, :], ps, y[:, t, :], ALU.add), [made])
                return [y_ready[t]]

            project_tokens(xnT, oT_done, *w6["o"], add_to_y)
            normed = layer_norm(y, xn, y_ready)
            xT_done = transpose_tokens(xn, xnT, normed, affine=(late["rows6"]["g2"], late["rows6"]["b2"]))
            base = [pool(lambda e, t=t: e.tensor_tensor(x[:, t, :], x[:, t, :], y[:, t, :], ALU.add), [y_ready[t]])
                    for t in range(NT)]
            gate_done = {}
            project_tokens(xnT, xT_done, *w6["g"], keep_tokens(gates, gate_done), cols=slice(0, NE))
            mix_done = {}
            for t in range(NT):
                g, p4 = gates[:, t, :], prob[:, t, :]
                s0 = dve(lambda e, t=t, g=g: e.max(top[:, t, :], g), [gate_done[t]])
                s1 = dve(lambda e, t=t, g=g: e.max_index(top_at[:, t, :], top[:, t, :], g), [s0])
                s2 = dve(lambda e, t=t: e.tensor_copy(top_f[:, t, :], top_at[:, t, 0:2]), [s1])
                s3 = dve(lambda e, t=t, p4=p4: e.tensor_scalar(p4[:, 0:2], top[:, t, 0:2], top[:, t, 0:1], None, ALU.subtract), [s0])
                s4 = act(lambda e, p4=p4: e.activation(p4[:, 0:2], p4[:, 0:2], ACT.Exp, accum_out=p4[:, 2:3]), [s3])
                s5 = dve(lambda e, p4=p4: e.reciprocal(p4[:, 3:4], p4[:, 2:3]), [s4])
                s6 = dve(lambda e, p4=p4: e.tensor_scalar(p4[:, 0:2], p4[:, 0:2], p4[:, 3:4], None, ALU.mult), [s5])
                for j in range(2):
                    s7 = dve(lambda e, t=t, j=j, p4=p4: e.tensor_scalar(pick[:, t, j, :], constant("iota"), top_f[:, t, j:j + 1],
                                                                        p4[:, j:j + 1], ALU.is_equal, ALU.mult), [s2, s6])
                mix_done[t] = dve(lambda e, t=t: e.tensor_tensor(mix[:, t, :], pick[:, t, 0, :], pick[:, t, 1, :], ALU.add), [s7])
            hidden_free = {}
            final = [base[t] for t in range(NT)]
            for half in range(2):
                hidden_done = {}
                for ex in range(NE):
                    n, ps, free = next_bank()
                    for k in range(KD):
                        last = pe(lambda e, k=k, ex=ex, half=half, ps=ps: e.matmul(
                            ps, w1[:, k, ex, :], xnT[:, k, half * BANK:(half + 1) * BANK],
                            start=(k == 0), stop=(k == KD - 1)),
                            free + [s for t in range(4 * half, 4 * half + 4) for s in xT_done[t]] + [w1_in])
                    hidden_done[ex] = act(lambda e, ex=ex, ps=ps: e.activation(hiddenT[:, ex, :], ps, ACT.Relu),
                                          [last, hidden_free.get(ex)])
                    bank_users[n] = [hidden_done[ex]]
                for i in range(4):
                    t = 4 * half + i
                    for ex in range(NE):
                        if ex % 2 == 0:
                            n, ps, free = next_bank()
                        cols = slice((ex % 2) * D, (ex % 2 + 1) * D)
                        last = pe(lambda e, ex=ex, i=i, ps=ps, cols=cols: e.matmul(
                            ps[:, cols], hiddenT[:, ex, i * P:(i + 1) * P], w2[:, ex, :], start=True, stop=True),
                            free + [hidden_done[ex], w2_in])
                        hidden_free[ex] = last
                        if ex % 2:
                            for o in (ex - 1, ex):
                                final[t] = dve(lambda e, t=t, o=o, ps=ps: e.scalar_tensor_tensor(
                                    out=x[:, t, :], in0=ps[:, (o % 2) * D:(o % 2 + 1) * D], scalar=mix[:, t, o:o + 1],
                                    in1=x[:, t, :], op0=ALU.mult, op1=ALU.add), [last, mix_done[t], final[t]])
                            bank_users[n] = [final[t]]
            x_ready[:] = final
            six.close()

        attention_and_experts()

        stored = dma(out.rearrange("b (t p) d -> p (b t) d", p=P), x[:, :, :], "store", x_ready)
        pr.emit()


def kernel(**inputs):
    import numpy as _np
    import concourse.bacc as _bacc
    from concourse import mybir as _mybir
    from concourse.bass_utils import run_bass_kernel_spmd as _run

    nc = _bacc.Bacc("TRN2", target_bir_lowering=False, num_devices=1)
    host = {name: _np.ascontiguousarray(a) for name, a in inputs.items()}
    host["const"], host["const2"] = constants()
    arrays, io = {}, {}
    for name, a in host.items():
        arrays[f"in_{name}_dram"] = a
        io[name] = nc.dram_tensor(f"in_{name}_dram", a.shape, _mybir.dt.from_np(a.dtype), kind="ExternalInput").ap()
    out = nc.dram_tensor("out_0_dram", (B, S, D), _mybir.dt.float32, kind="ExternalOutput").ap()
    build(nc, io, out)
    r = _run(nc, [arrays], core_ids=[0])
    return r.results[0]["out_0_dram"]
```

```python
from contextlib import ExitStack

import numpy as np

import concourse.bass as bass
from concourse import mybir

F32 = mybir.dt.float32
BF16 = mybir.dt.bfloat16
U32 = mybir.dt.uint32
ACT = mybir.ActivationFunctionType
ALU = mybir.AluOpType
AX = mybir.AxisListType

P = 128
B, S, D = 4, 256, 256
LC, C = 4096, 128
H, DH = 16, 16
NT = B * S // P
KD = D // P
QT = S // P
EPS_LN = 1e-5
BANK = 512
NE, HID = 8, 128

CONST_COLS = {}


def constants():
    p = np.arange(P)
    ident = np.eye(P, dtype=np.float32)
    head_block = (p[:, None] // DH == p[None, :] // DH).astype(np.float32)
    head_col = (p[:, None] // DH == np.arange(P // DH)[None, :]).astype(np.float32)
    gather = np.zeros((P, 2 * (DH + 1)), np.float32)
    for quad in range(4):
        for r in range(DH + 1):
            gather[32 * quad + r, (quad % 2) * (DH + 1) + r] = 1.0
    gather4 = np.zeros((P, 4 * (DH + 1)), np.float32)
    for quad in range(4):
        for r in range(DH + 1):
            gather4[32 * quad + r, quad * (DH + 1) + r] = 1.0
    pos = np.arange(S, dtype=np.float32)[:, None]
    inv = (np.float32(1.0) / np.float32(10000.0) ** (np.arange(0, D, 2, dtype=np.float32) / np.float32(D))).astype(np.float32)
    freqs = (pos * inv).astype(np.float32)
    cos = np.repeat(np.cos(freqs), 2, axis=-1)
    sin = np.repeat(np.sin(freqs), 2, axis=-1)
    sin[:, 0::2] *= -1.0
    by_tile = lambda a: a.reshape(QT, P, D).transpose(1, 0, 2).reshape(P, QT * D)
    causal = np.where(p[None, :] > p[:, None], np.float32(-3e38), np.float32(0.0)).astype(np.float32)
    iota = np.broadcast_to(np.arange(NE, dtype=np.float32), (P, NE))
    minus_half, half = np.full((P, NT), -0.5, np.float32), np.full((P, NT), 0.5, np.float32)
    groups = ([("ident", ident), ("gather", gather), ("minus_half", minus_half), ("half", half)],
              [("head_block", head_block), ("head_col", head_col), ("cos", by_tile(cos)), ("sin", by_tile(sin)),
               ("causal", causal), ("iota", iota), ("gather4", gather4)])
    for n, parts in enumerate(groups):
        at = 0
        for name, a in parts:
            CONST_COLS[name] = (n, at, at + a.shape[1])
            at += a.shape[1]
    return [np.ascontiguousarray(np.concatenate([a for _, a in parts], axis=1), dtype=np.float32) for parts in groups]


class Step:

    def __init__(self, queue, make, after, dma_sem, stage):
        self.queue, self.make, self.after, self.dma_sem, self.stage = queue, make, after, dma_sem, stage
        self.wanted = dma_sem is not None
        self.value = None


class Program:

    ENGINES = ("tensor", "vector", "scalar", "gpsimd", "sync")

    def __init__(self, nc, ctx):
        self.nc, self.ctx = nc, ctx
        self.queues = {e: [] for e in self.ENGINES}
        self.stage = "start"
        self.fences = {e: [] for e in self.ENGINES}

    def put(self, engine, make, after=(), dma_sem=None):
        steps = [s for s in list(after) + self.fences[engine] if s is not None]
        self.fences[engine] = []
        for s in steps:
            s.wanted = True
        step = Step(engine, make, steps, dma_sem, self.stage)
        self.queues[engine].append(step)
        return step

    def pe(self, make, after=()):
        return self.put("tensor", make, after)

    def dve(self, make, after=()):
        return self.put("vector", make, after)

    def act(self, make, after=()):
        return self.put("scalar", make, after)

    def pool(self, make, after=()):
        queue = self.queues["gpsimd"]
        if queue:
            after = list(after) + [queue[-1]]
        return self.put("gpsimd", make, after)

    def dma(self, out, in_, sem, after=(), engine="sync", **how):
        return self.put(engine, lambda e: e.dma_start(out, in_, **how), after, dma_sem=sem)

    def mark(self):
        return [q[-1] for q in self.queues.values() if q]

    def barrier(self, last=None):
        last = last or self.mark()
        for e in self.ENGINES[1:]:
            self.fences[e] = list(last)

    def emit(self):
        nc, sems, counts = self.nc, {}, {}
        for engine, queue in self.queues.items():
            for s in queue:
                if s.wanted:
                    name = s.dma_sem or f"{engine}_{s.stage}"
                    if name not in sems:
                        sems[name] = self.ctx.enter_context(nc.semaphore(name))
                        counts[name] = 0
                    counts[name] += 16 if s.dma_sem else 1
                    s.value = (name, counts[name])
        self.counts = counts
        block = self.ctx.enter_context(nc.Block())

        def run(queue):
            def body(engine):
                reached = {}
                for s in queue:
                    need = {}
                    for a in s.after:
                        name, value = a.value
                        need[name] = max(need.get(name, 0), value)
                    for name, value in need.items():
                        if reached.get(name, 0) < value:
                            engine.wait_ge(sems[name], value)
                            reached[name] = value
                    instruction = s.make(engine)
                    if s.wanted:
                        instruction.then_inc(sems[s.value[0]], 16 if s.dma_sem else 1)
                if queue is self.queues["sync"]:
                    engine.wait_ge(sems["store"], counts["store"])
            return body

        block.tensor(run(self.queues["tensor"]))
        block.vector(run(self.queues["vector"]))
        block.scalar(run(self.queues["scalar"]))
        block.gpsimd(run(self.queues["gpsimd"]))
        block.sync(run(self.queues["sync"]))


def build(nc, io, out):
    ctx = ExitStack()
    with ctx:
        pr = Program(nc, ctx)
        pe, dve, act, pool, dma = pr.pe, pr.dve, pr.act, pr.pool, pr.dma
        psum = ctx.enter_context(nc.psum_tensor("psum", [P, 8 * BANK], F32))
        bank_users = [[] for _ in range(8)]
        bank_turn = [0]
        held = set()

        def bank(k):
            return psum[:, k * BANK:(k + 1) * BANK]

        def next_bank():
            k = bank_turn[0] % 8
            bank_turn[0] += 1
            while k in held:
                k = bank_turn[0] % 8
                bank_turn[0] += 1
            return k, bank(k), bank_users[k]

        def sb(scope, name, shape, dt=F32):
            return scope.enter_context(nc.sbuf_tensor(name, shape, dt))

        const_tiles = [sb(ctx, "const", [P, io["const"].shape[1]]), None]
        const_in = dma(const_tiles[0][:, :], io["const"], "in_const")

        def constant(name):
            n, a, b = CONST_COLS[name]
            return const_tiles[n][:, a:b]

        ident = constant("ident")
        small = sb(ctx, "small", [P, 512])
        stat6 = small[:, 0:NT * 6].rearrange("p (t s) -> p t s", t=NT)
        meanvar = small[:, 48:48 + NT * 2].rearrange("p (t s) -> p t s", t=NT)
        rstd = small[:, 64:64 + NT]

        evacs = [0]

        def evacuate(dst, src, after):
            evacs[0] += 1
            if evacs[0] % 2:
                return act(lambda e: e.activation(dst, src, ACT.Copy), after)
            return dve(lambda e: e.tensor_copy(dst, src), after)

        def norm_by_tile(x, xn):
            stats, steps, waiting = [], [], []

            def tile(t, after):
                if t is None:
                    return waiting.pop()()
                s0 = dve(lambda e: e.bn_stats(stat6[:, t, :], x[:, t, :]), [after])
                stats.append(dve(lambda e: e.bn_aggr(meanvar[:, t, :], stat6[:, t, :]), [s0]))
                if waiting:
                    waiting.pop()()
                if t % 4 < 3:
                    return
                own = slice(t - 3, t + 1)
                guarded = dve(lambda e: e.tensor_scalar(rstd[:, own], meanvar[:, own, 1], EPS_LN, None, ALU.add),
                              stats[-4:])
                inverse = pool(lambda e: e.tensor_tensor(rstd[:, own], rstd[:, own], constant("minus_half")[:, own],
                                                         ALU.pow), [guarded, const_in])

                def scale():
                    steps.extend(dve(lambda e, u=u: e.tensor_scalar(xn[:, u, :], x[:, u, :], meanvar[:, u, 0:1],
                                                                    rstd[:, u:u + 1], ALU.subtract, ALU.mult), [inverse])
                                 for u in range(t - 3, t + 1))
                    pr.last_norm = steps[-1]
                waiting.append(scale)
                if t == NT - 1:
                    waiting.pop()()
            return tile, steps

        def layer_norm(x, xn, after):
            tile, steps = norm_by_tile(x, xn)
            for t in range(NT):
                tile(t, after[t])
            return steps

        class Turned:

            def __init__(self, xn, xnT, ready, affine=None):
                self.xn, self.xnT, self.ready, self.affine, self.halves = xn, xnT, ready, affine, {}

            def __getitem__(self, t):
                if t // 4 not in self.halves:
                    self.halves[t // 4] = self.turn(t // 4 * 4)
                return self.halves[t // 4]

            def turn(self, t0):
                done = []
                xn, ready = self.xn, self.ready
                for k in range(KD):
                    n, ps, free = next_bank()
                    for i in range(4):
                        last = pe(lambda e, t=t0 + i, i=i, k=k, ps=ps: e.transpose(
                            ps[:, i * P:(i + 1) * P], xn[:, t, k * P:(k + 1) * P], ident),
                            free + [ready[t0 + i], const_in])
                    dst = self.xnT[:, k, t0 * P:(t0 + 4) * P]
                    if self.affine:
                        (g, g_in), (bias, bias_in) = self.affine
                        copied = act(lambda e, dst=dst, ps=ps, k=k: e.activation(
                            dst, ps, ACT.Identity, scale=g[:, k:k + 1], bias=bias[:, k:k + 1]), [last, g_in, bias_in])
                    else:
                        copied = act(lambda e, dst=dst, ps=ps: e.activation(dst, ps, ACT.Copy), [last])
                    bank_users[n] = [copied]
                    done.append(copied)
                return done

        def transpose_tokens(xn, xnT, ready, affine=None):
            turned = Turned(xn, xnT, ready, affine)
            return [turned[t] for t in range(NT)]

        def project_tokens(actT, ready, w, w_ready, use, cols=slice(0, D), blocks=KD, tiles=range(NT)):
            width = cols.stop - cols.start
            taken = {}
            for t in tiles:
                n, ps, free = next_bank()
                for k in range(blocks):
                    last = pe(lambda e, t=t, k=k, ps=ps: e.matmul(
                        ps[:, 0:width], actT[:, k, t * P:(t + 1) * P], w[:, k, cols],
                        start=(k == 0), stop=(k == blocks - 1)), free + list(ready[t]) + [w_ready])
                bank_users[n] = use(t, ps[:, 0:width], last)
                taken[t] = n
            return taken

        def project_T(actT, ready, w, w_ready, use, col0=0):
            for half in range(2):
                for m in range(KD):
                    n, ps, free = next_bank()
                    for k in range(KD):
                        last = pe(lambda e, m=m, k=k, half=half, ps=ps: e.matmul(
                            ps, w[:, k, col0 + m * P:col0 + (m + 1) * P], actT[:, k, half * BANK:(half + 1) * BANK],
                            start=(k == 0), stop=(k == KD - 1)),
                            free + [s for t in range(4 * half, 4 * half + 4) for s in ready[t]] + [w_ready])
                    bank_users[n] = use(m, half, ps, last)

        def weight(scope, name, source, blocks, sem=None):
            n = source.shape[1]
            w = sb(scope, name, [P, blocks, n])
            return w, dma(w[:, :, :], source.rearrange("(k p) n -> p k n", p=P), sem or f"in_{name}")

        def bias_rows(scope, name, source):
            row = sb(scope, name, [P, D])
            return row, dma(row[:, :], source.partition_broadcast(P), f"in_{name}")

        def bias_columns(scope, name, source):
            col = sb(scope, name, [P, KD])
            return col, dma(col[:, :], source.rearrange("(m p) -> p m", p=P), f"in_{name}",
                            allow_slow_non_contiguous=True)

        pr.stage = "xattn0"
        x = sb(ctx, "x", [P, NT, D])
        heads_out = x
        wo_sb, bv_sb, bo_sb = sb(ctx, "wo", [P, KD, D]), sb(ctx, "bv", [P, D]), sb(ctx, "bo", [P, D])
        GH = 2
        outT, recip = sb(ctx, "outT", [P, S]), sb(ctx, "recip", [P, QT, GH])
        one = ExitStack()
        PARTS = 3
        PAIRS = 6
        ROWS = PAIRS * DH
        AUG = ROWS + 2
        NG = H // GH
        GROUPS = B * NG
        SLOTS = LC // P // 2
        UNIT_GROUPS = P // (GH * DH)
        RING = 3
        keysT = sb(one, "keysT", [P, RING, GH, LC], BF16)
        values = sb(one, "values", [P, LC // P, H, DH + 1])
        q_parts = sb(one, "q_parts", [P, NT, PARTS, D], BF16)
        q_rows = sb(one, "q_rows", [P, QT, H // 2, ROWS], BF16)
        queriesT = sb(one, "queriesT", [P, 4, GH, S], BF16)
        key_parts = sb(one, "key_parts", [P, 2, PARTS, LC], BF16)
        ctxT = sb(one, "ctxT", [P, LC])
        probs = sb(one, "probs", [P, 2, 4 * S])
        ctx_in = sb(one, "ctx_in", [P, 2, 4, C])
        key_f = sb(one, "key_f", [P, 2, BANK])
        key_r = sb(one, "key_r", [P, BANK])
        ident_b = sb(one, "ident_b", [P, P], BF16)
        peaks = sb(one, "peaks", [P, 2, GH * QT, 8])
        shift = sb(one, "shift", [P, 2, 3, GH * QT])
        shift_b = sb(one, "shift_b", [P, 2, GH * QT, 2], BF16)
        early = keysT[:, 2, :, :].rearrange("p h n -> p (h n)").bitcast(F32)
        x_norm = early[:, 0:NT * D].rearrange("p (t d) -> p t d", t=NT)
        x_normT = early[:, NT * D:2 * NT * D].rearrange("p (k n) -> p k n", k=KD)
        x0 = ctxT[:, LC - NT * D:LC].rearrange("p (t d) -> p t d", t=NT)
        wq = probs[:, 0, 0:KD * D].rearrange("p (k n) -> p k n", k=KD)
        bq = probs[:, 0, KD * D:KD * D + D]
        q_work = probs[:, 1, :].rearrange("p (w d) -> p w d", w=4)

        x_tiles = io["x"].rearrange("b (t p) d -> p (b t) d", p=P)
        ctx_first = key_parts[:, 1, :, :].rearrange("p i n -> p (i n)").bitcast(F32)[:, 0:LC].rearrange(
            "p (n t c) -> p n t c", t=4, c=C)
        CH = LC // BANK
        ctx_loaded = {}

        def load_first_ctx(c, chunks):
            step = dma(ctx_first[:, c:c + chunks, :, :],
                       io["ctx_512"][0, c * BANK:(c + chunks) * BANK, :].rearrange(
                           "(n t p) c -> p n t c", p=P, t=4), f"in_first{c}")
            for k in range(c, c + chunks):
                ctx_loaded[0, k] = step

        load_first_ctx(0, 1)
        x_in = [dma(x0[:, 0:NT // 2, :], x_tiles[:, 0:NT // 2, :], "in_x0")] * (NT // 2)
        wk, wk_in = weight(one, "wk", io["L0_xattn_Wk"], 1)
        bk, bk_in = bias_columns(one, "bk", io["L0_xattn_bk"])
        load_first_ctx(1, 1)
        x_in += [dma(x0[:, NT // 2:NT, :], x_tiles[:, NT // 2:NT, :], "in_x1")] * (NT // 2)
        wq_in = dma(wq, io["L0_xattn_Wq"].rearrange("(k p) n -> p k n", p=P), "in_wq")
        bq_in = dma(bq, io["L0_xattn_bq"].partition_broadcast(P), "in_bq")
        load_first_ctx(2, 2)
        load_first_ctx(4, 4)
        wv, wv_in = weight(one, "wv", io["L0_xattn_Wv"], 1)
        ident_b_made = dve(lambda e: e.tensor_copy(ident_b[:, :], ident), [const_in])
        clear_o = dve(lambda e: e.memset(bank(6), 0.0))
        bank_users[6] = [clear_o]
        normed = layer_norm(x0, x_norm, x_in)
        x_free = normed[-1]
        ones_v = pool(lambda e: e.memset(values[:, :, :, DH:DH + 1], 1.0))
        bq4 = dve(lambda e: e.tensor_scalar(bq, bq, DH ** -0.5, None, ALU.mult), [bq_in])
        split_done = [None] * NT
        work_free = [None, None]

        normedT, early_free = {}, []

        def turn_norm(t0):
            for k in range(KD):
                kb, ps, free = misc()
                for i in range(4):
                    last = pe(lambda e, i=i, k=k, ps=ps: e.transpose(
                        ps[:, i * P:(i + 1) * P], x_norm[:, t0 + i, k * P:(k + 1) * P], ident),
                        free + [normed[t0 + i], const_in])
                normedT[t0, k] = evacuate(x_normT[:, k, t0 * P:(t0 + 4) * P], ps, [last])
                bank_users[kb] = [normedT[t0, k]]

        def make_queries(t0):
            made, banks = [], []
            for t in (t0, t0 + 1):
                kb, ps, free = misc()
                banks.append((kb, ps))
                for k in range(KD):
                    last = pe(lambda e, t=t, k=k, ps=ps: e.matmul(
                        ps[:, 0:D], x_normT[:, k, t * P:(t + 1) * P], wq[:, k, :],
                        start=(k == 0), stop=(k == KD - 1)), free + [normedT[t // 4 * 4, k], wq_in])
                made.append(last)
            q, r = (lambda w: q_work[:, 2 * w, :]), (lambda w: q_work[:, 2 * w + 1, :])
            part = lambda w, n: q_parts[:, t0 + w, n, :]
            s0 = [dve(lambda e, w=w: e.scalar_tensor_tensor(out=q(w), in0=banks[w][1][:, 0:D], scalar=DH ** -0.5,
                                                            in1=bq, op0=ALU.mult, op1=ALU.add),
                      [made[w], bq4, work_free[w]]) for w in range(2)]
            s1 = [act(lambda e, w=w: e.activation(part(w, 0), q(w), ACT.Copy), [s0[w]]) for w in range(2)]
            s2 = [dve(lambda e, w=w: e.tensor_tensor(r(w), q(w), part(w, 0), ALU.subtract), [s1[w]])
                  for w in range(2)]
            s3 = [act(lambda e, w=w: e.activation(part(w, 1), r(w), ACT.Copy), [s2[w]]) for w in range(2)]
            for w in range(2):
                bank_users[banks[w][0]] = [s0[w]]
                s4 = dve(lambda e, w=w: e.tensor_tensor(part(w, 2), r(w), part(w, 1), ALU.subtract), [s3[w]])
                work_free[w] = split_done[t0 + w] = s4
            if t0 == NT - 2:
                early_free.extend([made[1], s4])

        def misc():
            choice = [7, 0, 1, 2, 3] if now[0] < -1 else [7]
            misc_turn[0] += 1
            k = choice[misc_turn[0] % len(choice)]
            return k, bank(k), bank_users[k]

        now, misc_turn = [-1000], [0]

        jobs = {}

        def at(slot, job):
            jobs.setdefault(slot, []).append(job)

        ctx_turned, ctx_read = {}, {}
        parts_ready, parts_free = {}, {}
        chunk_done = {}
        rows_ready, rows_free, qT_ready, qT_done = {}, {}, {}, {}
        keys_ready, keys_free = {}, {}
        shifts_ready = {}
        values_ready, values_free = {}, {}
        later = []
        key_work = [[(x[:, 2 * w:2 * w + 2, :].rearrange("p t d -> p (t d)"),
                      key_f[:, w, :] if w < 2 else ctx_in[:, w - 2, :, :].rearrange("p t c -> p (t c)"))
                     for w in range(4)],
                    [(key_f[:, w, :], key_r[:, :]) for w in range(2)]]
        key_work_free = [[] for _ in range(4)]
        recip_read = [[]]
        ctx_users = [[x_free]]

        def load_ctx(b, c):
            n = b * CH + c
            ctx_loaded[b, c] = dma(ctx_in[:, n % 2, :, :],
                                   io["ctx_512"][b, c * BANK:(c + 1) * BANK, :].rearrange("(t p) c -> p t c", p=P),
                                   f"in_ctx{n % 2}", ctx_read.get(n - 2, []))

        def turn_ctx(b, c):
            n = b * CH + c
            source = ctx_in[:, n % 2, :, :] if b else ctx_first[:, c, :, :]
            kb, ps, free = misc()
            for i in range(4):
                last = pe(lambda e, i=i: e.transpose(ps[:, i * P:(i + 1) * P], source[:, i, :], ident),
                          free + [ctx_loaded[b, c], const_in])
            if b:
                ctx_read[n] = [last]
            else:
                parts_free[-1] = [last]
            ctx_turned[b, c] = act(lambda e: e.activation(ctxT[:, c * BANK:(c + 1) * BANK], ps, ACT.Copy),
                                   [last] + (ctx_users[0] if b or c >= CH - NT * D // BANK else []))
            bank_users[kb] = [ctx_turned[b, c]]

        def fill_keys(u, c):
            b, m = divmod(u, KD)
            kb, ps, free_bank = misc()
            made = pe(lambda e: e.matmul(ps, wk[:, 0, m * P:(m + 1) * P], ctxT[:, c * BANK:(c + 1) * BANK],
                                         start=True, stop=True), free_bank + [ctx_turned[b, c], wk_in])
            n = c % len(key_work[u > 0])
            k, r = key_work[u > 0][n]
            part = lambda i: key_parts[:, u % 2, i, c * BANK:(c + 1) * BANK]
            free = parts_free.get(u - 2, []) + key_work_free[n]
            s0 = act(lambda e: e.activation(k, ps, ACT.Identity, bias=bk[:, m:m + 1]), [made, bk_in] + free)
            bank_users[kb] = [s0]
            if u == 0:
                s1 = act(lambda e: e.activation(part(0), ps, ACT.Identity, bias=bk[:, m:m + 1]), [made])
                bank_users[kb] = [s1]
                split = dve
            else:
                s1 = pool(lambda e: e.tensor_copy(part(0), k), [s0])
                split = pool

            def rest():
                s2 = split(lambda e: e.tensor_tensor(r, k, part(0), ALU.subtract), [s0, s1])
                s3 = split(lambda e: e.tensor_copy(part(1), r), [s2])
                s4 = split(lambda e: e.tensor_tensor(part(2), r, part(1), ALU.subtract), [s3])
                key_work_free[n] = [s4]
                chunk_done[u, c] = s4
                if u == 0 and c == CH - 1:
                    for w in range(2):
                        key_work_free[w] = ctx_read[CH - 2 + w] = [chunk_done[0, other] for other in range(CH)]
                    recip_read[0] = [chunk_done[0, other] for other in range(CH)]
            if u == 0:
                later.append(rest)
                if c:
                    later.pop(0)()
            else:
                rest()
            if m == KD - 1 and c == CH - 1:
                last_k_read[b] = made

        last_k_read = {}

        def lay_query_rows(u):
            b, m = divmod(u, KD)
            at_block = 0
            for part, times in ((0, 3), (1, 2), (2, 1)):
                for t in range(QT):
                    src = q_parts[:, QT * b + t, part, m * P:(m + 1) * P].rearrange("p (h d) -> p h d", d=DH)
                    for i in range(times):
                        dst = q_rows[:, t, :, (at_block + i) * DH:(at_block + i + 1) * DH]
                        last = pool(lambda e, dst=dst, src=src: e.tensor_copy(dst, src),
                                    [split_done[QT * b + t]] + rows_free.get(u - 1, []))
                at_block += times
            rows_ready[u] = last

        def turn_queries(i):
            u, g = divmod(i, UNIT_GROUPS)
            kb, ps, free = misc()
            out_b = ps.bitcast(BF16)
            for j in range(GH):
                for t in range(QT):
                    k = j * QT + t
                    last = pe(lambda e, k=k, j=j, t=t: e.transpose(
                        out_b[0:ROWS, k * P:(k + 1) * P], q_rows[:, t, g * GH + j, :], ident_b[:, :]),
                        free + [rows_ready[u], ident_b_made])
            rows_free[u] = [last]
            qT_ready[i] = dve(lambda e: e.tensor_copy(
                queriesT[0:ROWS, i % 4, :, :].rearrange("p h n -> p (h n)"), out_b[0:ROWS, 0:GH * S]),
                [last] + qT_done.get(i - 4, []))
            bank_users[kb] = [qT_ready[i]]

        def load_keys(i, chunks=range(CH)):
            keys = slice(chunks[0] * BANK, (chunks[-1] + 1) * BANK)
            u, g = divmod(i, UNIT_GROUPS)
            ring = i % RING
            for j in range(GH):
                src0 = (g * GH + j) * DH
                for block, part in enumerate((0, 1, 2, 0, 1, 0)):
                    last = dma(keysT[block * DH:(block + 1) * DH, ring, j, keys],
                               key_parts[src0:src0 + DH, u % 2, part, keys], f"keys{ring}_{j}",
                               [chunk_done[u, c] for c in chunks] + keys_free.get(i - RING, []) + (early_free if ring == 2 else []))
                keys_ready[i, j] = last
                parts_free[u] = parts_free.get(u, []) + [last]

        def make_values(b, p):
            kb, ps, free = misc()
            for e2 in range(2):
                kt = 2 * p + e2
                made = pe(lambda e, kt=kt, e2=e2: e.matmul(ps[:, e2 * D:(e2 + 1) * D],
                                                           ctxT[:, kt * P:(kt + 1) * P], wv[:, 0, :],
                                                           start=True, stop=True),
                          free + [ctx_turned[b, kt * P // BANK], wv_in])
            values_ready[b, p] = act(lambda e: e.activation(
                values[:, 2 * p:2 * p + 2, :, 0:DH],
                ps.rearrange("p (k h d) -> p k h d", k=2, h=H), ACT.Copy),
                [made] + values_free.get((b - 1, p), []))
            bank_users[kb] = [values_ready[b, p]]
            last_v_read[b] = made

        last_v_read = {}

        max_free = [None, None]
        peak_read = {}

        def max_step(n):
            i, r = divmod(n, GH * QT * CH)
            if i >= GROUPS:
                return
            pair, c = divmod(r, CH)
            j, t = divmod(pair, QT)
            k = 4 + n % 2
            made = pe(lambda e: e.matmul(bank(k), queriesT[0:ROWS, i % 4, j, t * P:(t + 1) * P],
                                         keysT[0:ROWS, i % RING, j, c * BANK:(c + 1) * BANK], start=True, stop=True),
                      [max_free[n % 2], qT_ready[i], keys_ready[i, j]] + (bank_users[k] if n < 2 else []))
            max_free[n % 2] = dve(lambda e: e.tensor_reduce(peaks[:, i % 2, pair, c:c + 1], bank(k), AX.X, ALU.max),
                                  [made] + peak_read.get(i - 2, []))
            if r == GH * QT * CH - 1:
                negative, high, rest = (shift[:, i % 2, w, :] for w in range(3))
                s0 = dve(lambda e: e.tensor_reduce(negative, peaks[:, i % 2, :, :], AX.X, ALU.max, negate=True),
                         [max_free[n % 2]])
                peak_read[i] = [s0]
                s1 = dve(lambda e: e.tensor_copy(shift_b[:, i % 2, :, 0], negative), [s0, shift_turned.get(i - 2)])
                s2 = dve(lambda e: e.tensor_tensor(shift_b[:, i % 2, :, 1], negative, shift_b[:, i % 2, :, 0],
                                                   ALU.subtract), [s1])
                shifts_ready[i] = s2

        shift_turned = {}

        def turn_shift(i):
            kb, ps, free = misc()
            out_b = ps.bitcast(BF16)
            for pair in range(GH * QT):
                last = pe(lambda e, pair=pair: e.transpose(out_b[ROWS:AUG, pair * P:(pair + 1) * P],
                                                           shift_b[:, i % 2, pair, :], ident_b[:, :]),
                          free + [shifts_ready[i]])
            shift_turned[i] = last
            qT_ready[i, "shift"] = dve(lambda e: e.tensor_copy(
                queriesT[ROWS:AUG, i % 4, :, :].rearrange("p h n -> p (h n)"), out_b[ROWS:AUG, 0:GH * S]), [last])
            bank_users[kb] = [qT_ready[i, "shift"]]

        score_free, probs_free, probs_ready = {}, {}, {}
        outT_ready, outT_read = {}, {}
        ones_steps = []

        def add_ones(ring):
            ones_steps.append(pool(lambda e: e.memset(keysT[ROWS:AUG, ring, :, :], 1.0),
                                   early_free if ring == 2 else []))


        def score_step(t):
            i, p = divmod(t, SLOTS)
            base = (t % 2) * 2 * BANK
            for e2 in range(2):
                for j in range(GH):
                    kt = 2 * p + e2
                    last = pe(lambda e, j=j, kt=kt, o=base + (e2 * GH + j) * S: e.matmul(
                        psum[:, o:o + S], keysT[0:AUG, i % RING, j, kt * P:(kt + 1) * P],
                        queriesT[0:AUG, i % 4, j, :], start=True, stop=True),
                        [score_free.get(t - 2), qT_ready[i, "shift"], keys_ready[i, j], ones_steps[i % RING]]
                        + (bank_users[2 * t] + bank_users[2 * t + 1] if t < 2 else []))
            probs_ready[t] = act(lambda e: e.activation(probs[:, t % 2, :], psum[:, base:base + 2 * BANK], ACT.Exp),
                                 [last, probs_free.get(t - 2)] + (work_free if t < 2 else []))
            score_free[t] = probs_ready[t]
            if p == SLOTS - 1:
                keys_free[i] = [last]
                qT_done[i] = [last]

        def value_step(t):
            i, p = divmod(t, SLOTS)
            b, g = divmod(i, NG)
            for e2 in range(2):
                for j in range(GH):
                    quad, kt = e2 * GH + j, 2 * p + e2
                    last = pe(lambda e, quad=quad, kt=kt, j=j: e.matmul(
                        bank(6)[32 * quad:32 * quad + DH + 1, 0:S], values[:, kt, g * GH + j, :],
                        probs[:, t % 2, quad * S:(quad + 1) * S], start=(p == 0), stop=(p == SLOTS - 1)),
                        [probs_ready[t], values_ready[b, p], ones_v, outT_ready.get(i - 1), clear_o])
            probs_free[t] = last
            if g == NG - 1:
                values_free[b, p] = [last]
            return last

        def finish_group(i, last):
            outT_ready[i] = act(lambda e: e.activation(outT[:, :], bank(6)[:, 0:S], ACT.Copy),
                                [last, outT_read.get(i - 1)])

        def normalize_group(i):
            b, g = divmod(i, NG)
            W = GH * (DH + 1)
            kb, ps, free = misc()
            for t in range(QT):
                last = pe(lambda e, t=t: e.matmul(ps[:, t * 64:t * 64 + W], outT[:, t * P:(t + 1) * P],
                                                  constant("gather"), start=True, stop=True),
                          free + [outT_ready[i], const_in])
            outT_read[i] = last
            both = ps[:, 0:QT * 64].rearrange("p (t w) -> p t w", t=QT)[:, :, 0:W].rearrange(
                "p t (h d) -> p t h d", h=GH)
            s0 = dve(lambda e: e.reciprocal(recip[:, :, :], both[:, :, :, DH]), [last] + recip_read[0])
            for t in range(QT):
                scaled = dve(lambda e, t=t: e.tensor_tensor(
                    heads_out[:, QT * b + t, g * GH * DH:(g + 1) * GH * DH].rearrange("p (h d) -> p h d", h=GH),
                    both[:, t, :, 0:DH], recip[:, t, :].unsqueeze(2).to_broadcast([P, GH, DH]), ALU.mult), [s0])
            recip_read[0] = bank_users[kb] = [scaled]
            group_out[i] = scaled
            if g == NG - 1:
                heads_biased[b] = dve(lambda e: e.tensor_tensor(
                    heads_out[:, QT * b:QT * b + QT, :], heads_out[:, QT * b:QT * b + QT, :],
                    bv_sb[:, :].unsqueeze(1).to_broadcast([P, QT, D]), ALU.add), [scaled, late[1]])

        group_out, heads_biased = {}, {}

        UNIT = UNIT_GROUPS * SLOTS
        first = -101
        for u in range(B * KD):
            b, m = divmod(u, KD)
            for c in range(CH):
                slot = UNIT * u + first + 8 * c
                if m == 0:
                    if b:
                        at(slot - 8, lambda b=b, c=c: load_ctx(b, c))

                    def turn(b=b, c=c):
                        if b and c == 0:
                            ctx_users[0] = [last_k_read[b - 1], last_v_read[b - 1]]
                        turn_ctx(b, c)
                    at(slot, turn)
                    at(slot + (2 if b else 9 if c < CH - 1 else 7), lambda u=u, c=c: fill_keys(u, c))
                else:
                    at(slot, lambda u=u, c=c: fill_keys(u, c))
            at(UNIT * u - SLOTS * 2 - 6 if u else first + 17, lambda u=u: lay_query_rows(u))
        for slot, job, t in ((first + 12, turn_norm, 0), (first + 13, make_queries, 0), (first + 20, turn_norm, 4),
                             (first + 28, make_queries, 2), (first + 36, make_queries, 4),
                             (first + 44, make_queries, 6)):
            at(slot, lambda job=job, t=t: job(t))
        for ring in range(RING):
            at((-37, -10, 2)[ring], lambda ring=ring: add_ones(ring))
        at(-60, lambda: load_keys(0, range(CH // 2)))
        at(-38, lambda: later.pop(0)())

        def load_output_weights():
            return (dma(wo_sb[:, :, :], io["L0_xattn_Wo"].rearrange("(k p) n -> p k n", p=P), "in_wo"),
                    dma(bv_sb[:, :], io["L0_xattn_bv"].partition_broadcast(P), "in_bv"),
                    dma(bo_sb[:, :], io["L0_xattn_bo"].partition_broadcast(P), "in_bo"))
        late = []
        at(4, lambda: late.extend(load_output_weights()))
        for i in range(GROUPS):
            at(SLOTS * i - (32 if i else 38), lambda i=i: load_keys(i, range(0 if i else CH // 2, CH)))
            at(SLOTS * i - 24, lambda i=i: turn_queries(i))
            at(SLOTS * i - 2, lambda i=i: turn_shift(i))
            if i < GROUPS - 1:
                at(SLOTS * i + SLOTS + 1, lambda i=i: normalize_group(i))
        for b in range(B):
            for p in range(SLOTS):
                slot = SLOTS * NG * b - SLOTS + p + 1
                at(-34 if slot < -SLOTS // 2 + 1 else slot, lambda b=b, p=p: make_values(b, p))
        LEAD = 18
        total = GROUPS * SLOTS
        for t in range(min(jobs), total + 2 + 1):
            if 0 <= t and t % (SLOTS * NG) == 0:
                pr.stage = f"xattn0_b{t // (SLOTS * NG)}"
            if 0 <= t < total:
                score_step(t)
            if t + LEAD >= 0:
                max_step(2 * (t + LEAD))
            if 1 <= t <= total:
                last = value_step(t - 1)
                if t % SLOTS == 0:
                    finish_group(t // SLOTS - 1, last)
            if t + LEAD >= 0:
                max_step(2 * (t + LEAD) + 1)
            now[0] = t
            for job in jobs.get(t, []):
                job()

        (wo, bv, bo), (wo_in, bv_in, bo_in) = (wo_sb, bv_sb, bo_sb), late
        pr.stage = "xattn0_out"
        bank_users[6] = [outT_ready[GROUPS - 1]]
        bank_users[4] = bank_users[5] = [max_free[0], max_free[1]]
        for k in range(4):
            bank_users[k] = [probs_ready[total - 1], probs_ready[total - 2]]
        pr.barrier()
        one.close()

        xn = sb(ctx, "xn", [P, NT, D])
        xnT = sb(ctx, "xnT", [P, KD, B * S])
        const_tiles[1] = sb(ctx, "const2", [P, io["const2"].shape[1]])
        x_old = sb(ctx, "x_old", [P, NT, D])
        x_old_in = []
        for tiles in (slice(0, NT // 2), slice(NT // 2, NT)):
            x_old_in += [dma(x_old[:, tiles, :], x_tiles[:, tiles, :], f"in_x_old{tiles.start}")] * (NT // 2)
        const2_in = dma(const_tiles[1][:, :], io["const2"], "in_const2")
        wl, wl_in = weight(ctx, "w_qkv", io["L0_attn_W_qkv"], KD)
        wlo, wlo_in = weight(ctx, "w_out", io["L0_attn_W_out"], KD)
        blo, blo_in = bias_rows(ctx, "b_out", io["L0_attn_b_out"])
        w3_q, w3_q_in = weight(ctx, "w3_q", io["L0_ffn_Wq"], KD)
        w3_k, w3_k_in = weight(ctx, "w3_k", io["L0_ffn_Wk"], KD)
        w3_v, w3_v_in = weight(ctx, "w3_v", io["L0_ffn_Wv"], KD)
        w3_ff, w3_ff_in = weight(ctx, "w3_ff", io["L0_ffn_Wff"], KD)
        QUADS, HG = 4, H // 4
        w3_o = sb(ctx, "w3_o", [P, HG, D])
        w3_o_zero = pool(lambda e: e.memset(w3_o[:, :, :], 0.0))
        for j in range(QUADS):
            w3_o_in = dma(w3_o[32 * j:32 * j + DH, :, :],
                          io["L0_ffn_Wo"].rearrange("(g j d) n -> j d g n", j=QUADS, d=DH)[j], "in_w3_o", [w3_o_zero])
        w4_q, w4_q_in = weight(ctx, "w4_q", io["L1_xattn_Wq"], KD)
        w4_k, w4_k_in = weight(ctx, "w4_k", io["L1_xattn_Wk"], 1)
        w4_v, w4_v_in = weight(ctx, "w4_v", io["L1_xattn_Wv"], 1)
        b4_q, b4_q_in = bias_columns(ctx, "b4_q", io["L1_xattn_bq"])
        b4_k, b4_k_in = bias_columns(ctx, "b4_k", io["L1_xattn_bk"])
        b4_v, b4_v_in = bias_rows(ctx, "b4_v", io["L1_xattn_bv"])
        KT = LC // P
        ctx_nat = [sb(ctx, "ctx_nat0", [P, KT, C]), None]
        ctx_T = sb(ctx, "ctx_T", [P, 2, LC])
        ctx_here, ctxT_here, nat_users, T_users = {}, {}, {}, {}

        def fetch_ctx(b, chunks=range(CH)):
            for c in chunks:
                ctx_here[b, c] = dma(ctx_nat[b % 2][:, 4 * c:4 * c + 4, :],
                                     io["ctx_512"][b, c * BANK:(c + 1) * BANK, :].rearrange("(t p) c -> p t c", p=P),
                                     f"in_nat{b % 2}_{c}", nat_users.get((b - 2, c), []))

        def turn_nat(b, c):
            n, ps, free = next_bank()
            nat = ctx_nat[b % 2]
            for i in range(4):
                last = pe(lambda e, i=i, ps=ps: e.transpose(ps[:, i * P:(i + 1) * P], nat[:, 4 * c + i, :], ident),
                          free + [ctx_here[b, c]])
            ctxT_here[b, c] = evacuate(ctx_T[:, b % 2, c * BANK:(c + 1) * BANK], ps, [last] + T_users.get(b - 2, []))
            bank_users[n] = [ctxT_here[b, c]]

        fetch_ctx(0)

        normalize_group(GROUPS - 1)
        biased = [heads_biased[t // QT] for t in range(NT)]
        outT_done = Turned(heads_out, xnT, biased)
        x_ready = [None] * NT

        x_bias = [pool(lambda e, t=t: e.tensor_tensor(x_old[:, t, :], x_old[:, t, :], bo[:, :], ALU.add),
                       [x_old_in[t], bo_in]) for t in range(NT)]

        def add_to_stream(t, ps, made):
            x_ready[t] = dve(lambda e: e.tensor_tensor(x[:, t, :], ps, x_old[:, t, :], ALU.add), [made, x_bias[t], biased[t]])
            return [x_ready[t]]

        norm_tile, normed = norm_by_tile(x, xn)

        def add_and_norm(t, ps, made):
            users = add_to_stream(t, ps, made)
            norm_tile(t, x_ready[t])
            return users

        project_tokens(xnT, outT_done, wo, wo_in, add_and_norm)
        def keep_T(dst, done):
            def use(m, half, ps, made):
                done[m, half] = evacuate(dst[:, m, half * BANK:(half + 1) * BANK], ps, [made])
                return [done[m, half]]
            return use

        def keep_tokens(dst, done):
            def use(t, ps, made):
                done[t] = evacuate(dst[:, t, :], ps, [made])
                return [done[t]]
            return use

        def isolate_heads(srcT, heads, b, m, ready, users, heads_ready, scale):
            n = (b * KD + m) % 2
            for h in range(P // DH):
                engine = dve if h % 2 else pool
                step = engine(lambda e, h=h: e.tensor_scalar(heads[:, n, h, :], srcT[:, m, b * S:(b + 1) * S],
                                                             constant("head_col")[:, h:h + 1], scale,
                                                             ALU.mult, ALU.mult),
                              [ready[m, b * S // BANK], const2_in] + users.get((n, h), []))
                heads_ready[n, h] = step

        def add_bias_to_stream(bias, bias_in):
            before = list(x_ready)
            return [pool(lambda e, t=t: e.tensor_tensor(x[:, t, :], x[:, t, :], bias[:, :], ALU.add),
                         [before[t], bias_in, pr.last_norm]) for t in range(NT)]

        def hand_over(scope, tile, last, turned):
            mark = pr.mark()
            tile(NT - 1, last)
            xT_next[:] = [turned]
            xT_next[0][0]
            pr.barrier(mark)
            scope.close()

        late = {}
        xT_next = [Turned(xn, xnT, normed)]

        def linear_attention():
            pr.stage = "attn0"
            two = ExitStack()
            k_feat = sb(two, "k_feat", [P, NT, D])
            v_aug = sb(two, "v_aug", [P, NT, KD, P + 1])
            q_featT = sb(two, "q_featT", [P, KD, B * S])
            NKV = P + P // DH
            kv = sb(two, "kv", [P, B, KD, NKV])
            lin_out = sb(two, "lin_out", [P, NT, D])
            lin_outT = sb(two, "lin_outT", [P, KD, B * S])
            low_part = sb(two, "low_part", [P, 4, BANK])
            den = sb(two, "den", [P, 2, KD, P // DH])
            xT_done = xT_next[0]
            ones_set = pool(lambda e: e.memset(v_aug[:, :, :, P:P + 1], 1.0))
            low_free = [None] * 4
            low_turn = [0]

            def elu_plus_one(dst, ps, made):
                n = low_turn[0] % 4
                low_turn[0] += 1
                low = low_part[:, n, 0:ps.shape[1]]
                s0 = dve(lambda e: e.tensor_scalar(low, ps, 0.0, None, ALU.min), [made, low_free[n]])
                s1 = act(lambda e: e.activation(low, low, ACT.Exp), [s0])
                low_free[n] = dve(lambda e: e.scalar_tensor_tensor(out=dst, in0=ps, scalar=0.0, in1=low,
                                                                   op0=ALU.max, op1=ALU.add), [s1])
                return low_free[n]

            k_done, v_done = {}, {}

            def keep_kv(t, ps, made):
                v_done[t] = act(lambda e: e.activation(v_aug[:, t, :, 0:P],
                                                       ps[:, D:2 * D].rearrange("p (m n) -> p m n", m=KD), ACT.Copy), [made])
                k_done[t] = elu_plus_one(k_feat[:, t, :], ps[:, 0:D], v_done[t])
                return [k_done[t], v_done[t]]

            project_tokens(xnT, xT_done, wl, wl_in, keep_kv, cols=slice(D, 3 * D))
            q_done = {}

            def keep_q(m, half, ps, made):
                q_done[m, half] = elu_plus_one(q_featT[:, m, half * BANK:(half + 1) * BANK], ps, made)
                return [q_done[m, half]]

            project_T(xnT, xT_done, wl, wl_in, keep_q)
            kv_done = {}
            for b in range(B):
                for m in range(KD):
                    n, ps, free = next_bank()
                    for i in range(QT):
                        t = QT * b + i
                        last = pe(lambda e, t=t, m=m, i=i, ps=ps: e.matmul(
                            ps[:, 0:P + 1], k_feat[:, t, m * P:(m + 1) * P], v_aug[:, t, m, :],
                            start=(i == 0), stop=(i == QT - 1)), free + [k_done[t], v_done[t], ones_set])
                    s0 = dve(lambda e, b=b, m=m, ps=ps: e.tensor_tensor(kv[:, b, m, 0:P], ps[:, 0:P],
                                                                        constant("head_block"), ALU.mult), [last, const2_in])
                    s1 = dve(lambda e, b=b, m=m, ps=ps: e.tensor_tensor(
                        kv[:, b, m, P:NKV], ps[:, P:P + 1].to_broadcast([P, P // DH]), constant("head_col"), ALU.mult), [last])
                    bank_users[n] = [s1]
                    kv_done[b, m] = s1
            lin_done = []
            for t in range(NT):
                n, ps, free = next_bank()
                b = t // QT
                for m in range(KD):
                    last = pe(lambda e, t=t, m=m, b=b, ps=ps: e.matmul(
                        ps[:, m * NKV:(m + 1) * NKV], q_featT[:, m, t * P:(t + 1) * P], kv[:, b, m, :],
                        start=True, stop=True), free + [q_done[m, t * P // BANK], kv_done[b, m]])
                both = ps[:, 0:KD * NKV].rearrange("p (m n) -> p m n", m=KD)
                dn = den[:, t % 2, :, :]
                s0 = dve(lambda e, both=both, dn=dn: e.tensor_scalar(dn, both[:, :, P:NKV], 1e-6, None, ALU.add),
                         [last] + lin_done[-2:-1])
                s1 = dve(lambda e, dn=dn: e.reciprocal(dn, dn), [s0])
                for m in range(KD):
                    s2 = dve(lambda e, t=t, m=m, both=both, dn=dn: e.tensor_tensor(
                        lin_out[:, t, m * P:(m + 1) * P].rearrange("p (h d) -> p h d", d=DH),
                        both[:, m, 0:P].rearrange("p (h d) -> p h d", d=DH),
                        dn[:, m, :].unsqueeze(2).to_broadcast([P, P // DH, DH]), ALU.mult), [s1])
                lin_done.append(s2)
                bank_users[n] = [s2]
            linT_done = Turned(lin_out, lin_outT, lin_done)

            biased = add_bias_to_stream(blo, blo_in)
            tile, normed = norm_by_tile(x, xn)

            def accumulate(t, ps, made):
                x_ready[t] = dve(lambda e: e.tensor_tensor(x[:, t, :], ps, x[:, t, :], ALU.add), [made, biased[t]])
                if t < NT - 1:
                    tile(t, x_ready[t])
                return [x_ready[t]]

            project_tokens(lin_outT, linT_done, wlo, wlo_in, accumulate)
            hand_over(two, tile, x_ready[NT - 1], Turned(xn, xnT, normed))

        linear_attention()

        def query_softmax_attention():
            pr.stage = "ffn0"
            three = ExitStack()
            qT = sb(three, "qT", [P, KD, B * S])
            kT = sb(three, "kT", [P, KD, B * S])
            kT_heads = sb(three, "kT_heads", [P, 2, P // DH, S])
            v_tok = sb(three, "v_tok", [P, NT, D])
            NR = 8
            weights3 = sb(three, "weights3", [P, NR, QT, S])
            v_scaled = sb(three, "v_scaled", [P, 2, QT, QUADS, 32])
            peaks3 = sb(three, "peaks3", [P, 2, QUADS, QT])
            sums3 = sb(three, "sums3", [P, 2, QT, QUADS])
            outT3 = sb(three, "outT3", [P, HG, B * S])
            norm3 = sb(three, "norm3", [P, 2, 3, NT])
            xT_done = xT_next[0]
            v_zero = pool(lambda e: e.memset(v_scaled[:, :, :, :, :], 0.0))

            qd, kd, vd = {}, {}, {}
            project_T(xnT, xT_done, w3_k, w3_k_in, keep_T(kT, kd))
            project_T(xnT, xT_done, w3_q, w3_q_in, keep_T(qT, qd))
            project_tokens(xnT, xT_done, w3_v, w3_v_in, keep_tokens(v_tok, vd))
            heads_ready, heads_users, ring_free = {}, {}, {}
            SC3 = 1.0 / D ** 0.5
            pending = []
            outT3_done = {}
            quad_bank = {}

            def scores3(b, m, h):
                hn = (b * KD + m) * (P // DH) + h
                r, w, j = hn % NR, hn // QUADS % 2, hn % QUADS
                n, ps, free = next_bank()
                hb = (b * KD + m) % 2
                for kt in range(QT):
                    last = pe(lambda e, kt=kt, ps=ps: e.matmul(
                        ps[:, kt * S:(kt + 1) * S], kT_heads[:, hb, h, kt * P:(kt + 1) * P],
                        qT[:, m, b * S:(b + 1) * S], start=True, stop=True),
                        free + [heads_ready[hb, h], qd[m, b * S // BANK]])
                heads_users[hb, h] = [last]
                peak = peaks3[:, w, j, :]
                s0 = dve(lambda e: e.tensor_reduce(peak, ps.rearrange("p (k q) -> p k q", k=QT), AX.X, ALU.max, negate=True),
                         [last] + ring_free.get(r, []))
                for kt in range(QT):
                    s2 = act(lambda e, kt=kt: e.activation(weights3[:, r, kt, :], ps[:, kt * S:(kt + 1) * S], ACT.Exp,
                                                           bias=peak[:, kt:kt + 1], accum_out=sums3[:, w, kt, j:j + 1]),
                             [s0] + sums_free.get(w, []))
                bank_users[n] = [s2]
                return s2

            scaled_done = {}

            def scale_values3(b, g, exps):
                w = (b * HG + g) % 2
                s0 = dve(lambda e: e.reciprocal(sums3[:, w, :, :], sums3[:, w, :, :]), [exps[-1]])
                c0 = g * QUADS * DH
                for kt in range(QT):
                    s1 = dve(lambda e, kt=kt: e.tensor_tensor(
                        v_scaled[:, w, kt, :, 0:DH], v_tok[:, QT * b + kt, c0:c0 + QUADS * DH].rearrange("p (j d) -> p j d", d=DH),
                        sums3[:, w, kt, :].unsqueeze(2).to_broadcast([P, QUADS, DH]), ALU.mult),
                        [s0, v_zero, vd[QT * b + kt]] + v_users.get(w, []))
                sums_free[w] = [s1]
                scaled_done[b, g] = s1

            def values3(b, g, exps):
                w, s1 = (b * HG + g) % 2, scaled_done[b, g]
                n, ps, free = next_bank()
                for kt in range(QT):
                    for j in range(QUADS):
                        r = (b * H + QUADS * g + j) % NR
                        last = pe(lambda e, kt=kt, j=j, r=r, ps=ps: e.matmul(
                            ps[32 * j:32 * j + 32, 0:S], v_scaled[:, w, kt, j, :], weights3[:, r, kt, :],
                            start=(kt == 0), stop=(kt == QT - 1)), free + [s1, exps[j]])
                v_users[w] = [last]
                for j in range(QUADS):
                    ring_free[(b * H + QUADS * g + j) % NR] = [last]
                outT3_done[b, g] = dve(lambda e: e.tensor_copy(outT3[:, g, b * S:(b + 1) * S], ps[:, 0:S]), [last])
                bank_users[n] = [outT3_done[b, g]]

            sums_free, v_users = {}, {}
            heads3 = {}
            z_done, z2_done = {}, {}
            zT = Turned(xn, xnT, z_done)
            in_banks = {}

            def l2_project(which, tiles):
                dst = (xn, v_tok)[which]
                if which == 0:
                    for t in tiles:
                        heads3[t] = [outT3_done[t // QT, g] for g in range(HG)]

                def keep(t, ps, made):
                    square = act(lambda e: e.activation(dst[:, t, :], ps, ACT.Square,
                                                        accum_out=norm3[:, which, 0, t:t + 1]), [made])
                    in_banks[t] = (ps, square)
                    return [square]

                if which == 0:
                    taken = project_tokens(outT3, heads3, w3_o, w3_o_in, keep, blocks=HG, tiles=tiles)
                else:
                    taken = project_tokens(xnT, zT, w3_ff, w3_ff_in, keep, tiles=tiles)
                for t in tiles:
                    in_banks[t] += (taken[t],)
                    held.add(taken[t])

            def l2_scale(which, tiles):
                dst, done = (xn, v_tok)[which], (z_done, z2_done)[which]
                own = slice(tiles[0], tiles[-1] + 1)
                v = norm3[:, which, :, own]
                s1 = pool(lambda e: e.tensor_tensor(v[:, 1, :], v[:, 0, :], constant("half")[:, own], ALU.pow),
                          [in_banks[t][1] for t in tiles])
                s2 = dve(lambda e: e.tensor_scalar(v[:, 1, :], v[:, 1, :], 1e-12, None, ALU.max), [s1])
                s3 = dve(lambda e: e.reciprocal(v[:, 2, :], v[:, 1, :]), [s2])
                for t in tiles:
                    ps, _, n = in_banks[t]
                    done[t] = dve(lambda e, t=t, ps=ps: e.tensor_scalar(
                        dst[:, t, :], ps, norm3[:, which, 2, t:t + 1], None, ALU.mult), [s3])
                    bank_users[n] = [done[t]]
                    held.discard(n)

            tile, normed = norm_by_tile(x, xn)

            def add_gelu(t):
                s0 = act(lambda e: e.activation(v_tok[:, t, :], v_tok[:, t, :], ACT.Gelu), [z2_done[t], x_ready[t]])
                x_ready[t] = dve(lambda e: e.tensor_tensor(x[:, t, :], x[:, t, :], v_tok[:, t, :], ALU.add), [s0])
                if t < NT - 1:
                    tile(t, x_ready[t])

            ahead = {9: lambda: l2_project(0, (0, 1)),
                     10: lambda: (l2_scale(0, (0, 1)), l2_project(0, (2, 3))),
                     11: lambda: l2_scale(0, (2, 3)),
                     12: lambda: zT[0],
                     13: lambda: l2_project(1, (0, 1)),
                     14: lambda: (l2_scale(1, (0, 1)), l2_project(1, (2, 3))),
                     15: lambda: l2_scale(1, (2, 3))}
            isolate_heads(kT, kT_heads, 0, 0, kd, heads_users, heads_ready, SC3)
            for b in range(B):
                for m in range(KD):
                    following = b * KD + m + 1
                    if following < B * KD:
                        isolate_heads(kT, kT_heads, *divmod(following, KD), kd, heads_users, heads_ready, SC3)
                    for g in range(2):
                        exps = []
                        for j in range(QUADS):
                            exps.append(scores3(b, m, QUADS * g + j))
                            if j == 1 and pending:
                                scale_values3(*pending[0])
                        if pending:
                            values3(*pending.pop(0))
                        pending.append((b, 2 * m + g, exps))
                        ahead.get(b * HG + 2 * m + g, lambda: None)()
                        if len(ctxT_here) < CH // 2:
                            turn_nat(0, len(ctxT_here))
            scale_values3(*pending[0])
            values3(*pending.pop(0))
            second = range(NT // 2, NT)
            for t in range(NT // 2):
                add_gelu(t)
            tile(None, None)
            for which in range(2):
                l2_project(which, second)
                if which:
                    turned = Turned(xn, xnT, normed)
                    turned[0]
                l2_scale(which, second)
                for _ in range(CH // 4):
                    turn_nat(0, len(ctxT_here))
            for t in second:
                add_gelu(t)
            hand_over(three, tile, x_ready[NT - 1], turned)
            ctx_nat[1] = sb(ctx, "ctx_nat1", [P, KT, C])
            w5_rows = sb(ctx, "w5_rows", [P, 3, KD, D])
            w5 = [sb(ctx, f"w5_{n}", [P, KD, D]) for n in "qkv"]
            fetch_ctx(1)
            w5_in = [dma(w5_rows[:, n, :, :], io[f"L1_attn_w{name}"].rearrange("(k p) n -> p k n", p=P), f"in_w5_{name}")
                     for n, name in enumerate("qkv")]
            late.update(w5_rows=w5_rows, w5_in=w5_in, w5=w5, w5_done=[])

        query_softmax_attention()

        def context_attention():
            pr.stage = "xattn1"
            four = ExitStack()
            w_kT = sb(four, "w4_kT", [P, KD, C])
            q4T = sb(four, "q4T", [P, KD, B * S])
            qcT = sb(four, "qcT", [P, B * S])
            offset = sb(four, "offset", [P, NT])
            row_w = sb(four, "row_w", [P, 2, LC])
            col_w = sb(four, "col_w", [P, 4, BANK])
            peaks4 = sb(four, "peaks4", [P, 2, 8])
            stat4 = sb(four, "stat4", [P, NT, 6])
            sums4 = sb(four, "sums4", [P, 2, 2])
            ucT = sb(four, "ucT", [P, B * S])
            xT_done = xT_next[0]
            n, ps, free = next_bank()
            for k in range(KD):
                last = pe(lambda e, k=k, ps=ps: e.transpose(ps[:, k * C:(k + 1) * C], w4_k[:, 0, k * P:(k + 1) * P], ident),
                          free + [w4_k_in])
            w_kT_done = evacuate(w_kT[:, :, :].rearrange("p k c -> p (k c)"), ps[:, 0:KD * C], [last])
            bank_users[n] = [w_kT_done]
            q4_done = {}

            def keep_q4(m, half, ps, made):
                q4_done[m, half] = act(lambda e: e.activation(q4T[:, m, half * BANK:(half + 1) * BANK], ps, ACT.Identity,
                                                              bias=b4_q[:, m:m + 1]), [made, b4_q_in])
                return [q4_done[m, half]]

            project_T(xnT, xT_done, w4_q, w4_q_in, keep_q4)
            qc_done = {}
            for half in range(2):
                n, ps, free = next_bank()
                for k in range(KD):
                    last = pe(lambda e, k=k, half=half, ps=ps: e.matmul(ps, w_kT[:, k, :],
                                                                        q4T[:, k, half * BANK:(half + 1) * BANK],
                                                                        start=(k == 0), stop=(k == KD - 1)),
                              free + [w_kT_done, q4_done[k, half]])
                qc_done[half] = evacuate(qcT[:, half * BANK:(half + 1) * BANK], ps, [last])
                bank_users[n] = [qc_done[half]]
            n, ps, free = next_bank()
            for t in range(NT):
                for k in range(KD):
                    last = pe(lambda e, t=t, k=k, ps=ps: e.matmul(ps[:, t:t + 1], q4T[:, k, t * P:(t + 1) * P], b4_k[:, k:k + 1],
                                                                  start=(k == 0), stop=(k == KD - 1)),
                              free + [b4_k_in, q4_done[k, t * P // BANK]])
            offset_done = dve(lambda e, ps=ps: e.tensor_copy(offset[:, :], ps[:, 0:NT]), [last])
            bank_users[n] = [offset_done]

            w_rows, w_in, w5, w5_done = late["w5_rows"], late["w5_in"], late["w5"], late["w5_done"]
            for w in range(3):
                n, ps, free = next_bank()
                for k in range(KD):
                    for m in range(KD):
                        last = pe(lambda e, k=k, m=m, w=w, ps=ps: e.transpose(
                            ps[:, (k * KD + m) * P:(k * KD + m + 1) * P], w_rows[:, w, m, k * P:(k + 1) * P], ident),
                            free + [w_in[w]])
                w5_done.append(evacuate(w5[w][:, :, :].rearrange("p k n -> p (k n)"), ps, [last]))
                bank_users[n] = [w5_done[w]]
            row_free, col_free, uc_done = {}, {}, {}
            exp4 = {}

            def score_chunk(t, c):
                b, r = t // QT, t % 2
                n, ps, free = next_bank()
                here = slice(c * BANK, (c + 1) * BANK)
                made = pe(lambda e: e.matmul(ps, qcT[:, t * P:(t + 1) * P], ctx_T[:, b % 2, here], start=True, stop=True),
                          free + [qc_done[t * P // BANK], ctxT_here[b, c]])
                T_users[b] = [made]
                copied = act(lambda e: e.activation(row_w[:, r, here], ps, ACT.Copy), [made, row_free.get((r, c))])
                bank_users[n] = [copied]
                found = dve(lambda e: e.tensor_reduce(peaks4[:, r, c:c + 1], row_w[:, r, here], AX.X, ALU.max),
                            [copied, exp4.get(t - 2)])
                if c < CH - 1:
                    return
                w = stat4[:, t, :]
                s0 = dve(lambda e: e.tensor_reduce(w[:, 0:1], peaks4[:, r, :], AX.X, ALU.max), [found])
                s1 = dve(lambda e: e.tensor_tensor(w[:, 1:2], w[:, 0:1], offset[:, t:t + 1], ALU.add), [s0, offset_done])
                s2 = dve(lambda e: e.tensor_tensor(w[:, 2:3], offset[:, t:t + 1], w[:, 1:2], ALU.subtract), [s1])
                for half in range(2):
                    own = slice(half * LC // 2, (half + 1) * LC // 2)
                    exp4[t, half] = act(lambda e, half=half, own=own: e.activation(
                        row_w[:, r, own], row_w[:, r, own], ACT.Exp, bias=w[:, 2:3], accum_out=w[:, 3 + half:4 + half]), [s2])
                exp4[t] = exp4[t, 1]

            def turn_chunk(t, c):
                r, w = t % 2, (t * CH + c) % 4
                n, ps, free = next_bank()
                for i in range(4):
                    kt = 4 * c + i
                    last = pe(lambda e, i=i, kt=kt: e.transpose(ps[:, i * P:(i + 1) * P],
                                                                row_w[:, r, kt * P:(kt + 1) * P], ident),
                              free + [exp4[t, 2 * c // CH]])
                row_free[r, c] = last
                columns[t, c] = dve(lambda e: e.tensor_copy(col_w[:, w, :], ps), [last, col_free.get(w)])
                bank_users[n] = [columns[t, c]]

            def weigh_chunk(t, c):
                b, w = t // QT, (t * CH + c) % 4
                if c == 0:
                    acc_bank[t] = next_bank()
                    held.add(acc_bank[t][0])
                no, acc, free = acc_bank[t]
                for i in range(4):
                    kt = 4 * c + i
                    last = pe(lambda e, i=i, kt=kt: e.matmul(acc[:, 0:P], ctx_nat[b % 2][:, kt, :],
                                                             col_w[:, w, i * P:(i + 1) * P],
                                                             start=(kt == 0), stop=(kt == KT - 1)),
                              free + [columns[t, c], ctx_here[b, c]])
                col_free[w] = last
                nat_users[b, c] = [last]
                if c == CH - 1:
                    uc_done[t] = dve(lambda e: e.tensor_copy(ucT[:, t * P:(t + 1) * P], acc[:, 0:P]), [last])
                    bank_users[no] = [uc_done[t]]
                    held.discard(no)
                    w4 = stat4[:, t, :]
                    s3 = dve(lambda e: e.tensor_tensor(w4[:, 5:6], w4[:, 3:4], w4[:, 4:5], ALU.add), [exp4[t, 1]])
                    exp4[t, "inverse"] = dve(lambda e: e.reciprocal(w4[:, 5:6], w4[:, 5:6]), [s3])

            biased = [pool(lambda e, t=t: e.tensor_tensor(x[:, t, :], x[:, t, :], b4_v[:, :], ALU.add),
                           [x_ready[t], b4_v_in, pr.last_norm]) for t in range(NT)]
            columns, acc_bank = {}, {}
            AHEAD = CH + 3
            BATCH = QT * CH
            for s in range(-AHEAD, NT * CH + 2):
                if 0 <= s + AHEAD < NT * CH:
                    score_chunk(*divmod(s + AHEAD, CH))
                if 0 <= s < NT * CH:
                    turn_chunk(*divmod(s, CH))
                if 0 <= s - 2:
                    weigh_chunk(*divmod(s - 2, CH))
                for b in range(1, B):
                    if b >= 2 and 0 <= s - (BATCH * (b - 1) - 5) < CH:
                        fetch_ctx(b, [s - (BATCH * (b - 1) - 5)])
                    if 0 <= s - (BATCH * (b - 1) + 1 - 4 * (b == 1)) < CH:
                        turn_nat(b, s - (BATCH * (b - 1) + 1 - 4 * (b == 1)))
            tile, normed = norm_by_tile(x, xn)
            for t in range(NT):
                n, ps, free = next_bank()
                last = pe(lambda e, t=t, ps=ps: e.matmul(ps[:, 0:D], ucT[:, t * P:(t + 1) * P], w4_v[:, 0, :],
                                                         start=True, stop=True), free + [uc_done[t], w4_v_in])
                x_ready[t] = dve(lambda e, t=t, ps=ps: e.scalar_tensor_tensor(
                    out=x[:, t, :], in0=ps[:, 0:D], scalar=stat4[:, t, 5:6], in1=x[:, t, :], op0=ALU.mult, op1=ALU.add),
                    [last, biased[t], exp4[t, "inverse"]])
                bank_users[n] = [x_ready[t]]
                if t < NT - 1:
                    tile(t, x_ready[t])
            hand_over(four, tile, x_ready[NT - 1], Turned(xn, xnT, normed))
            late["w6"] = {n: weight(ctx, f"w6_{n}", io[f"L1_ffn_W{n}"], KD) for n in "qkvog"}
            late["rows6"] = {n: bias_columns(ctx, f"r6_{n}", io[f"L1_ffn_{n}"]) for n in ("g1", "b1", "g2", "b2")}
            w1 = sb(ctx, "w6_1", [P, KD, NE, HID])
            for k in range(KD):
                w1_in = dma(w1[:, k, :, :], io["L1_ffn_W1"][:, k * P:(k + 1) * P, :].rearrange("e p h -> p e h"), "in_w6_1")
            w2 = sb(ctx, "w6_2", [P, NE, D])
            w2_in = dma(w2[:, :, :], io["L1_ffn_W2"].rearrange("e h n -> h e n"), "in_w6_2")
            late.update(w1=w1, w1_in=w1_in, w2=w2, w2_in=w2_in)

        context_attention()

        def causal_attention():
            pr.stage = "attn1"
            five = ExitStack()
            w5, w5_done = late["w5"], late["w5_done"]
            swapped = sb(five, "swapped", [P, 2, 2, D])
            qk = ctx_nat[0][:, :, :].rearrange("p (t w two) c -> p t w (two c)", w=2, two=2)
            rotated = ctx_T[:, 0, :].rearrange("p (t w d) -> p t w d", w=2, d=D)
            turned5 = ctx_T[:, 1, :].rearrange("p (w k n) -> p w k n", w=2, k=KD)
            v5 = sb(five, "v5", [P, NT, D])
            rows5 = sb(five, "rows5", [P, NT, S])
            cols5 = sb(five, "cols5", [P, NT, QT, P])
            stat5 = sb(five, "stat5", [P, NT, 4])
            xT_done = xT_next[0]
            qk_done, turned_done = [None] * NT, [None] * NT
            cos = constant("cos").rearrange("p (t d) -> p t d", t=QT)
            sin = constant("sin").rearrange("p (t d) -> p t d", t=QT)
            pair = lambda a, o: a.rearrange("p w (n two) -> p w n two", two=2)[:, :, :, o]
            wide = lambda a: a.unsqueeze(1).to_broadcast([P, 2, a.shape[1]])
            for t in range(NT):
                i = t % QT
                n, ps, free = next_bank()
                for w in range(2):
                    for k in range(KD):
                        last = pe(lambda e, t=t, w=w, k=k, ps=ps: e.matmul(
                            ps[:, w * D:(w + 1) * D], xnT[:, k, t * P:(t + 1) * P], w5[w][:, k, :],
                            start=(k == 0), stop=(k == KD - 1)), free + list(xT_done[t]) + [w5_done[w]])
                src, dst, other = qk[:, t, :, :], rotated[:, t, :, :], swapped[:, t % 2, :, :]
                qk_done[t] = act(lambda e, src=src, ps=ps: e.activation(
                    src, ps.rearrange("p (w d) -> p w d", w=2), ACT.Copy), [last])
                bank_users[n] = [qk_done[t]]
                s0 = dve(lambda e, src=src, dst=dst, i=i: e.tensor_tensor(dst, src, wide(cos[:, i, :]), ALU.mult),
                         [qk_done[t], const2_in])
                s1 = pool(lambda e, src=src, other=other, i=i: e.tensor_tensor(
                    pair(other, 0), pair(src, 1), wide(sin[:, i, 0::2]), ALU.mult),
                    [qk_done[t], const2_in] + ([turned_done[t - 2]] if t >= 2 else []))
                s2 = dve(lambda e, src=src, other=other, i=i: e.tensor_tensor(
                    pair(other, 1), pair(src, 0), wide(sin[:, i, 1::2]), ALU.mult), [qk_done[t], const2_in]
                    + ([turned_done[t - 2]] if t >= 2 else []))
                turned_done[t] = dve(lambda e, dst=dst, other=other: e.tensor_tensor(dst, dst, other, ALU.add), [s0, s1, s2])
            v5_done = {}
            project_tokens(xnT, xT_done, w5[2], w5_done[2], keep_tokens(v5, v5_done))
            tT = []
            for w in range(2):
                tT.append(transpose_tokens(rotated[:, :, w, :], turned5[:, w, :, :], turned_done))
            SC5 = 1.0 / D ** 0.5
            out5, half_sums = {}, {}

            def turn5(t):
                b, i = divmod(t, QT)
                s1 = out5[t]
                n, ps, free = next_bank()
                for kt in range(i + 1):
                    last = pe(lambda e, t=t, kt=kt, ps=ps: e.transpose(ps[:, kt * P:(kt + 1) * P],
                                                                       rows5[:, t, kt * P:(kt + 1) * P], ident), free + [s1])
                s3 = act(lambda e: e.activation(cols5[:, t, 0:i + 1, :].rearrange("p k q -> p (k q)"),
                                                ps[:, 0:(i + 1) * P], ACT.Copy), [last])
                bank_users[n] = [s3]
                out5[t] = s3

            for t in range(NT):
                b, i = divmod(t, QT)
                width = (i + 1) * P
                n, ps, free = next_bank()
                for k in range(KD):
                    last = pe(lambda e, t=t, b=b, k=k, width=width, ps=ps: e.matmul(
                        ps[:, 0:width], turned5[:, 0, k, t * P:(t + 1) * P], turned5[:, 1, k, b * S:b * S + width],
                        start=(k == 0), stop=(k == KD - 1)),
                        free + tT[0][t] + [s for u in range(QT * b, QT * b + i + 1) for s in tT[1][u]])
                w = stat5[:, t, :]
                row = rows5[:, t, 0:width]
                steps = []
                if i:
                    steps.append(act(lambda e, row=row, ps=ps, i=i: e.activation(row[:, 0:i * P], ps[:, 0:i * P], ACT.Copy,
                                                                                 scale=SC5), [last]))
                steps.append(dve(lambda e, row=row, ps=ps, i=i: e.scalar_tensor_tensor(
                    out=row[:, i * P:(i + 1) * P], in0=ps[:, i * P:(i + 1) * P], scalar=SC5, in1=constant("causal"),
                    op0=ALU.mult, op1=ALU.add), [last] + steps))
                bank_users[n] = steps
                s0 = dve(lambda e, w=w, row=row: e.tensor_reduce(w[:, 0:1], row, AX.X, ALU.max, negate=True), steps)
                s1 = act(lambda e, w=w, row=row: e.activation(row, row, ACT.Exp, bias=w[:, 0:1], accum_out=w[:, 1:2]), [s0])
                out5[t] = s1
                if t % 4 == 3:
                    half_sums[t // 4] = [out5[u] for u in range(t - 3, t + 1)]
                if t >= 4:
                    turn5(t - 4)

            second_done = []
            first_tile, y_made = norm_by_tile(x, x_old)
            second_tile, normed = norm_by_tile(x_old, xn)

            def tile(t, after):
                first_tile(t, after)
                while len(second_done) < len(y_made):
                    u = len(second_done)
                    second_tile(u, y_made[u])
                    second_done.append(u)
                if t == 5:
                    second_tile(None, None)

            for t in range(NT):
                if t == 4:
                    for u in range(4, NT):
                        turn5(u)
                if t % 4 == 0:
                    own = slice(t, t + 4)
                    inverse5 = dve(lambda e, own=own: e.reciprocal(stat5[:, own, 2], stat5[:, own, 1]),
                                   half_sums[t // 4])
                b, i = divmod(t, QT)
                s3, s2 = out5[t], inverse5
                n, ps, free = next_bank()
                for kt in range(i + 1):
                    last = pe(lambda e, t=t, b=b, i=i, kt=kt, ps=ps: e.matmul(
                        ps[:, 0:D], cols5[:, t, kt, :], v5[:, QT * b + kt, :], start=(kt == 0), stop=(kt == i)),
                        free + [s3, v5_done[QT * b + kt]])
                x_ready[t] = dve(lambda e, t=t, ps=ps: e.scalar_tensor_tensor(
                    out=x[:, t, :], in0=ps[:, 0:D], scalar=stat5[:, t, 2:3], in1=x[:, t, :], op0=ALU.mult, op1=ALU.add),
                    [last, s2, pr.last_norm])
                bank_users[n] = [x_ready[t]]
                if t < NT - 1:
                    tile(t, x_ready[t])
            rows6 = late["rows6"]
            hand_over(five, tile, x_ready[NT - 1], Turned(xn, xnT, normed, (rows6["g1"], rows6["b1"])))

        causal_attention()

        def attention_and_experts():
            pr.stage = "ffn1"
            six = ExitStack()
            w6, w1, w1_in, w2, w2_in = (late[n] for n in ("w6", "w1", "w1_in", "w2", "w2_in"))
            y = x_old
            qT = ctx_T[:, 0, 0:KD * B * S].rearrange("p (k n) -> p k n", k=KD)
            kT = ctx_T[:, 0, KD * B * S:2 * KD * B * S].rearrange("p (k n) -> p k n", k=KD)
            hiddenT = ctx_T[:, 1, :].rearrange("p (x n) -> p x n", x=NE)
            q_heads = ctx_nat[0][:, :, :].rearrange("p (w h two) c -> p w h (two c)", w=2, two=2)
            NR6, NC6 = 4, 8
            rows_w = sb(six, "rows_w", [P, NR6, QT, S])
            cols_w = sb(six, "cols_w", [P, NC6, QT, S])
            peaks6 = sb(six, "peaks6", [P, B * H, QT])
            v_ones = ctx_nat[1][:, :, :].rearrange("p k c -> p (k c)").rearrange("p (t h f) -> p t h f", t=NT, h=H)
            outT6 = sb(six, "outT6", [P, 2, S])
            recip6 = sb(six, "recip6", [P, 2, QUADS])
            gates = sb(six, "gates", [P, NT, NE])
            top = sb(six, "top", [P, NT, NE])
            top_at = sb(six, "top_at", [P, NT, NE], U32)
            top_f = sb(six, "top_f", [P, NT, 2])
            pick = sb(six, "pick", [P, NT, 2, NE])
            prob = sb(six, "prob", [P, NT, 4])
            mix = sb(six, "mix", [P, NT, NE])
            xT_done = xT_next[0]

            qd, kd, vd = {}, {}, {}
            project_T(xnT, xT_done, *w6["q"], keep_T(qT, qd))
            project_T(xnT, xT_done, *w6["k"], keep_T(kT, kd))
            zeros6 = pool(lambda e: e.memset(v_ones[:, :, :, DH + 1:], 0.0))
            ones6 = pool(lambda e: e.memset(v_ones[:, :, :, DH:DH + 1], 1.0))

            def keep_v6(t, ps, made):
                vd[t] = evacuate(v_ones[:, t, :, 0:DH], ps.rearrange("p (h d) -> p h d", d=DH), [made])
                return [vd[t]]

            project_tokens(xnT, xT_done, *w6["v"], keep_v6)
            heads_ready, heads_users = {}, {}
            SC6 = DH ** -0.5
            rows_free, cols_free = {}, {}

            def scores6(b, m, h):
                hn = (b * KD + m) * (P // DH) + h
                r, hb = hn % NR6, (b * KD + m) % 2
                n, ps, free = next_bank()
                for i in range(QT):
                    last = pe(lambda e, i=i, ps=ps: e.matmul(ps[:, i * S:(i + 1) * S], q_heads[:, hb, h, i * P:(i + 1) * P],
                                                             kT[:, m, b * S:(b + 1) * S], start=True, stop=True),
                              free + [heads_ready[hb, h], kd[m, b * S // BANK]])
                heads_users[hb, h] = [last]
                peak = peaks6[:, hn, :]
                s0 = dve(lambda e: e.tensor_reduce(peak, ps.rearrange("p (k q) -> p k q", k=QT), AX.X, ALU.max, negate=True),
                         [last])
                for i in range(QT):
                    s2 = act(lambda e, i=i: e.activation(rows_w[:, r, i, :], ps[:, i * S:(i + 1) * S], ACT.Exp,
                                                         bias=peak[:, i:i + 1]), [s0] + rows_free.get(r, []))
                bank_users[n] = [s2]
                return s2

            def turn6(b, m, h, made):
                hn = (b * KD + m) * (P // DH) + h
                r = hn % NR6
                n, ps, free = next_bank()
                for kt in range(QT):
                    for i in range(QT):
                        last = pe(lambda e, kt=kt, i=i, ps=ps: e.transpose(
                            ps[:, kt * S + i * P:kt * S + (i + 1) * P], rows_w[:, r, i, kt * P:(kt + 1) * P], ident),
                            free + [made])
                rows_free[r] = [last]
                rc = hn % NC6
                s = evacuate(cols_w[:, rc, :, :].rearrange("p k q -> p (k q)"), ps, [last] + cols_free.get(rc, []))
                bank_users[n] = [s]
                return s

            def weigh6(b, g, ready):
                w = (b * HG + g) % 2
                n, ps, free = next_bank()
                for kt in range(QT):
                    for j in range(QUADS):
                        rc = (b * H + g * QUADS + j) % NC6
                        last = pe(lambda e, kt=kt, j=j, rc=rc: e.matmul(
                            ps[32 * j:32 * j + 32, 0:S], v_ones[:, QT * b + kt, g * QUADS + j, :],
                            cols_w[:, rc, kt, :], start=(kt == 0), stop=(kt == QT - 1)),
                            free + [ready[j], vd[QT * b + kt], ones6])
                for j in range(QUADS):
                    cols_free[(b * H + g * QUADS + j) % NC6] = [last]
                out6[b, g] = dve(lambda e: e.tensor_copy(outT6[:, w, :], ps[:, 0:S]), [last] + outT6_free.get(w, []))
                bank_users[n] = [out6[b, g]]

            def finish6(b, g):
                w, W = (b * HG + g) % 2, QUADS * (DH + 1)
                n, ps, free = next_bank()
                for i in range(QT):
                    last = pe(lambda e, i=i: e.matmul(ps[:, i * W:(i + 1) * W], outT6[:, w, i * P:(i + 1) * P],
                                                      constant("gather4"), start=True, stop=True),
                              free + [out6[b, g], const2_in])
                outT6_free[w] = [last]
                both = ps[:, 0:QT * W].rearrange("p (t h d) -> p t h d", t=QT, h=QUADS)
                s0 = dve(lambda e: e.reciprocal(recip6[:, :, :], both[:, :, :, DH]), [last] + o_done[-1:])
                for i in range(QT):
                    c0 = g * QUADS * DH
                    s1 = dve(lambda e, i=i: e.tensor_tensor(
                        xn[:, QT * b + i, c0:c0 + QUADS * DH].rearrange("p (h d) -> p h d", d=DH), both[:, i, :, 0:DH],
                        recip6[:, i, :].unsqueeze(2).to_broadcast([P, QUADS, DH]), ALU.mult), [s0])
                o_done.append(s1)
                bank_users[n] = [s1]

            out6, outT6_free, o_done = {}, {}, []
            heads_at = {}
            oT = Turned(xn, xnT, heads_at)
            y_ready, base, gate_done, mix_done = [None] * NT, [None] * NT, {}, {}
            tile, normed = norm_by_tile(y, xn)
            moe_T = Turned(xn, xnT, normed, affine=(late["rows6"]["g2"], late["rows6"]["b2"]))

            def add_to_y(t, ps, made):
                y_ready[t] = dve(lambda e: e.tensor_tensor(y[:, t, :], ps, y[:, t, :], ALU.add), [made])
                tile(t, y_ready[t])
                if t == NT // 2 - 1:
                    tile(None, None)
                return [y_ready[t]]

            def out_tiles6(tiles):
                project_tokens(xnT, oT, *w6["o"], add_to_y, tiles=tiles)
                for t in tiles:
                    base[t] = pool(lambda e, t=t: e.tensor_tensor(x[:, t, :], x[:, t, :], y[:, t, :], ALU.add),
                                   [y_ready[t]])

            def turn_heads(half):
                for t in range(4 * half, 4 * half + 4):
                    heads_at[t] = o_done[HG * (t // QT) + HG - 1]
                oT[4 * half]

            def gate_half(half):
                tiles = range(4 * half, 4 * half + 4)
                project_tokens(xnT, moe_T, *w6["g"], keep_tokens(gates, gate_done), cols=slice(0, NE), tiles=tiles)
                found, weighed = {}, {}
                for t in tiles:
                    g, p4 = gates[:, t, :], prob[:, t, :]
                    s0 = dve(lambda e, t=t, g=g: e.max(top[:, t, :], g), [gate_done[t]])
                    s1 = dve(lambda e, t=t, g=g: e.max_index(top_at[:, t, :], top[:, t, :], g), [s0])
                    found[t] = dve(lambda e, t=t: e.tensor_copy(top_f[:, t, :], top_at[:, t, 0:2]), [s1])
                    s3 = dve(lambda e, t=t, p4=p4: e.tensor_scalar(p4[:, 0:2], top[:, t, 0:2], top[:, t, 0:1], None,
                                                                   ALU.subtract), [s0])
                    weighed[t] = act(lambda e, p4=p4: e.activation(p4[:, 0:2], p4[:, 0:2], ACT.Exp,
                                                                   accum_out=p4[:, 2:3]), [s3])
                for t in tiles:
                    p4 = prob[:, t, :]
                    s5 = dve(lambda e, p4=p4: e.reciprocal(p4[:, 3:4], p4[:, 2:3]), [weighed[t]])
                    s6 = dve(lambda e, p4=p4: e.tensor_scalar(p4[:, 0:2], p4[:, 0:2], p4[:, 3:4], None, ALU.mult), [s5])
                    for j in range(2):
                        s7 = dve(lambda e, t=t, j=j, p4=p4: e.tensor_scalar(
                            pick[:, t, j, :], constant("iota"), top_f[:, t, j:j + 1], p4[:, j:j + 1],
                            ALU.is_equal, ALU.mult), [found[t], s6])
                    mix_done[t] = dve(lambda e, t=t: e.tensor_tensor(mix[:, t, :], pick[:, t, 0, :], pick[:, t, 1, :],
                                                                     ALU.add), [s7])

            hidden_free, hidden_done = {}, {}
            final = base

            def hidden(half):
                for ex in range(NE):
                    n, ps, free = next_bank()
                    for k in range(KD):
                        last = pe(lambda e, k=k, ex=ex, half=half, ps=ps: e.matmul(
                            ps, w1[:, k, ex, :], xnT[:, k, half * BANK:(half + 1) * BANK],
                            start=(k == 0), stop=(k == KD - 1)), free + list(moe_T[4 * half]) + [w1_in])
                    hidden_done[ex] = act(lambda e, ex=ex, ps=ps: e.activation(hiddenT[:, ex, :], ps, ACT.Relu),
                                          [last, hidden_free.get(ex)])
                    bank_users[n] = [hidden_done[ex]]

            def mix_experts(half):
                for i in range(4):
                    t = 4 * half + i
                    for ex in range(NE):
                        if ex % 2 == 0:
                            n, ps, free = next_bank()
                        cols = slice((ex % 2) * D, (ex % 2 + 1) * D)
                        last = pe(lambda e, ex=ex, i=i, ps=ps, cols=cols: e.matmul(
                            ps[:, cols], hiddenT[:, ex, i * P:(i + 1) * P], w2[:, ex, :], start=True, stop=True),
                            free + [hidden_done[ex], w2_in])
                        hidden_free[ex] = last
                        if ex % 2:
                            for o in (ex - 1, ex):
                                final[t] = dve(lambda e, t=t, o=o, ps=ps: e.scalar_tensor_tensor(
                                    out=x[:, t, :], in0=ps[:, (o % 2) * D:(o % 2 + 1) * D], scalar=mix[:, t, o:o + 1],
                                    in1=x[:, t, :], op0=ALU.mult, op1=ALU.add), [last, mix_done[t], final[t]])
                            bank_users[n] = [final[t]]

            made6, turned6 = [], []
            isolate_heads(qT, q_heads, 0, 0, qd, heads_users, heads_ready, SC6)
            LAG6 = 2
            for n6 in range(B * H + LAG6):
                if n6 < B * H:
                    unit, h = divmod(n6, P // DH)
                    if h == 1 and unit + 1 < B * KD:
                        isolate_heads(qT, q_heads, *divmod(unit + 1, KD), qd, heads_users, heads_ready, SC6)
                    made6.append(scores6(*divmod(unit, KD), h))
                if n6 >= LAG6:
                    hn = n6 - LAG6
                    unit, h = divmod(hn, P // DH)
                    turned6.append(turn6(*divmod(unit, KD), h, made6[hn]))
                    if hn % QUADS == 1 and hn > QUADS:
                        group = hn // QUADS - 1
                        weigh6(*divmod(group, HG), turned6[group * QUADS:(group + 1) * QUADS])
                    if hn % QUADS == 3 and hn > QUADS:
                        finish6(*divmod(hn // QUADS - 1, HG))
                    after_half = hn - (B * H // 2 + QUADS)
                    if after_half == 1:
                        turn_heads(0)
                    if 2 <= after_half < 6:
                        out_tiles6([after_half - 2])
                    if after_half == 10:
                        moe_T[0]
            weigh6(B - 1, HG - 1, turned6[-QUADS:])
            finish6(B - 1, HG - 1)
            turn_heads(1)
            out_tiles6(range(4, 8))
            gate_half(0)
            hidden(0)
            moe_T[4]
            mix_experts(0)
            gate_half(1)
            hidden(1)
            mix_experts(1)
            x_ready[:] = final
            six.close()

        attention_and_experts()
        out_tiles = out.rearrange("b (t p) d -> p (b t) d", p=P)
        for tiles in (slice(0, 4), slice(4, 6), slice(6, 7), slice(7, 8)):
            dma(out_tiles[:, tiles, :], x[:, tiles, :], "store", x_ready[tiles])
        pr.emit()


def kernel(**inputs):
    import numpy as _np
    import concourse.bacc as _bacc
    from concourse import mybir as _mybir
    from concourse.bass_utils import run_bass_kernel_spmd as _run

    nc = _bacc.Bacc("TRN2", target_bir_lowering=False, num_devices=1)
    host = {name: _np.ascontiguousarray(a) for name, a in inputs.items()}
    host["const"], host["const2"] = constants()
    arrays, io = {}, {}
    for name, a in host.items():
        arrays[f"in_{name}_dram"] = a
        io[name] = nc.dram_tensor(f"in_{name}_dram", a.shape, _mybir.dt.from_np(a.dtype), kind="ExternalInput").ap()
    out = nc.dram_tensor("out_0_dram", (B, S, D), _mybir.dt.float32, kind="ExternalOutput").ap()
    build(nc, io, out)
    r = _run(nc, [arrays], core_ids=[0])
    return r.results[0]["out_0_dram"]
```
